# Optimizing a Trainium2 kernel written in Bass

```python
import numpy as np
import jax
import jax.numpy as jnp

def _softmax(x, axis=-1):
    return jax.nn.softmax(x, axis=axis)

def _gelu(x):
    return jax.nn.gelu(x, approximate=True)

def _silu(x):
    return jax.nn.silu(x)

def _sigmoid(x):
    return jax.nn.sigmoid(x)

def _layernorm(x, axis=-1, eps=1e-05):
    m = jnp.mean(x, axis=axis, keepdims=True)
    v = jnp.var(x, axis=axis, keepdims=True)
    return (x - m) / jnp.sqrt(v + eps)

def _scatter_add(tgt, idx, src, axis=0):
    return tgt.at[idx].add(src)

def _segment_sum(src, seg, n):
    return jax.ops.segment_sum(src, seg, n)
kernel_name = 'mk_prb_d1_jaxref_r8_b2efb3'

def setup_inputs(seed: int=0):
    np.random.seed(seed)
    _w = jnp.asarray

    def _L0_attn_setup():
        import jax, jax.numpy as jnp
        import numpy as np
        D_MODEL = 128
        D_STATE = 128
        D_CONV = 4
        EXPAND = 2
        HEADDIM = 64
        D_INNER = EXPAND * D_MODEL
        NHEADS = D_INNER // HEADDIM
        CONV_DIM = D_INNER + 2 * D_STATE
        D_IN_PROJ = 2 * D_INNER + 2 * D_STATE + NHEADS
        CHUNK = 64
        BATCH, SEQ = (8, 256)
        EPS = 1e-05

        def _segsum(a):
            T = a.shape[-1]
            cs = jnp.cumsum(a, axis=-1)
            d = cs[..., :, None] - cs[..., None, :]
            return jnp.where(jnp.tril(jnp.ones((T, T), bool)), d, -jnp.inf)

        def _mamba2_layer(x, ln_w, ln_b, W_in, conv_w, conv_b, dt_bias, A_log, D, rms_w, W_out):
            b, l, _ = x.shape
            mu = jnp.mean(x, -1, keepdims=True)
            xc = x - mu
            var = jnp.mean(xc * xc, -1, keepdims=True)
            xn = xc * jax.lax.rsqrt(var + EPS) * ln_w + ln_b
            zxbcdt = xn @ W_in.T
            z = zxbcdt[..., :D_INNER]
            xBC = zxbcdt[..., D_INNER:D_INNER + CONV_DIM]
            dt = zxbcdt[..., D_INNER + CONV_DIM:]
            dt = jax.nn.softplus(dt + dt_bias)
            xp = jnp.pad(xBC, ((0, 0), (D_CONV - 1, 0), (0, 0)))
            conv = conv_b + sum((xp[:, k:k + l, :] * conv_w[:, k] for k in range(D_CONV)))
            xBC = conv * jax.nn.sigmoid(conv)
            xs = xBC[..., :D_INNER].reshape(b, l, NHEADS, HEADDIM)
            Bm = xBC[..., D_INNER:D_INNER + D_STATE]
            Cm = xBC[..., D_INNER + D_STATE:]
            A = -jnp.exp(A_log)
            A_dt = dt * A
            Xdt = xs * dt[..., None]
            nc = l // CHUNK
            Xc = Xdt.reshape(b, nc, CHUNK, NHEADS, HEADDIM)
            Ac = A_dt.reshape(b, nc, CHUNK, NHEADS).transpose(0, 3, 1, 2)
            Bc = Bm.reshape(b, nc, CHUNK, D_STATE)
            Cc = Cm.reshape(b, nc, CHUNK, D_STATE)
            A_cs = jnp.cumsum(Ac, -1)
            Lmat = jnp.exp(_segsum(Ac))
            Y_diag = jnp.einsum('bcln,bcsn,bhcls,bcshp->bclhp', Cc, Bc, Lmat, Xc)
            decay_states = jnp.exp(A_cs[..., -1:] - A_cs)
            states = jnp.einsum('bcln,bhcl,bclhp->bchpn', Bc, decay_states, Xc)
            states = jnp.concatenate([jnp.zeros_like(states[:, :1]), states], axis=1)
            chunk_sum = jnp.pad(A_cs[..., -1], ((0, 0), (0, 0), (1, 0)))
            decay_chunk = jnp.exp(_segsum(chunk_sum))
            new_states = jnp.einsum('bhzc,bchpn->bzhpn', decay_chunk, states)
            states_prev = new_states[:, :-1]
            state_decay_out = jnp.exp(A_cs)
            Y_off = jnp.einsum('bcln,bchpn,bhcl->bclhp', Cc, states_prev, state_decay_out)
            Y = (Y_diag + Y_off).reshape(b, l, NHEADS, HEADDIM)
            Y = Y + xs * D[None, None, :, None]
            y = Y.reshape(b, l, D_INNER)
            y = y * (z * jax.nn.sigmoid(z))
            y = y * jax.lax.rsqrt(jnp.mean(y * y, -1, keepdims=True) + EPS) * rms_w
            out = y @ W_out.T
            return x + out
        key = jax.random.key(seed)
        ks = jax.random.split(key, 8)
        x = jax.random.normal(ks[0], (BATCH, SEQ, D_MODEL), dtype=jnp.float32)
        ln_w = jnp.ones((D_MODEL,), jnp.float32)
        ln_b = jnp.zeros((D_MODEL,), jnp.float32)
        W_in = jax.random.normal(ks[1], (D_IN_PROJ, D_MODEL), jnp.float32) * 0.02
        conv_w = jax.random.normal(ks[2], (CONV_DIM, D_CONV), jnp.float32) * 0.2
        conv_b = jnp.zeros((CONV_DIM,), jnp.float32)
        dt = jnp.exp(jax.random.uniform(ks[3], (NHEADS,), jnp.float32, minval=float(np.log(0.001)), maxval=float(np.log(0.1))))
        dt_bias = dt + jnp.log(-jnp.expm1(-dt))
        A_log = jnp.log(jax.random.uniform(ks[4], (NHEADS,), jnp.float32, minval=1.0, maxval=16.0))
        D = jnp.ones((NHEADS,), jnp.float32)
        rms_w = jnp.ones((D_INNER,), jnp.float32)
        W_out = jax.random.normal(ks[5], (D_MODEL, D_INNER), jnp.float32) * 0.02
        return {'x': x, 'ln_w': ln_w, 'ln_b': ln_b, 'W_in': W_in, 'conv_w': conv_w, 'conv_b': conv_b, 'dt_bias': dt_bias, 'A_log': A_log, 'D': D, 'rms_w': rms_w, 'W_out': W_out}
    _L0_attn_in = _L0_attn_setup()

    def _L0_ffn_setup():
        import jax, jax.numpy as jnp
        import numpy as np
        TOP_K = 2
        key = jax.random.key(seed)
        ks = jax.random.split(key, 5)
        B, T, D, E, F = (2, 256, 128, 8, 256)
        scale_d = 1.0 / np.sqrt(D)
        scale_f = 1.0 / np.sqrt(F)
        return {'x': jax.random.normal(ks[0], (B, T, D), jnp.float32), 'kernel_router_DE': jax.random.normal(ks[1], (D, E), jnp.float32) * scale_d, 'kernel_gating_EDF': jax.random.normal(ks[2], (E, D, F), jnp.float32) * scale_d, 'kernel_up_EDF': jax.random.normal(ks[3], (E, D, F), jnp.float32) * scale_d, 'kernel_down_EFD': jax.random.normal(ks[4], (E, F, D), jnp.float32) * scale_f}
    _L0_ffn_in = _L0_ffn_setup()
    _d = {'L0_attn_x': _L0_attn_in['x'], 'L0_attn_ln_w': _L0_attn_in['ln_w'], 'L0_attn_ln_b': _L0_attn_in['ln_b'], 'L0_attn_W_in': _L0_attn_in['W_in'], 'L0_attn_conv_w': _L0_attn_in['conv_w'], 'L0_attn_conv_b': _L0_attn_in['conv_b'], 'L0_attn_dt_bias': _L0_attn_in['dt_bias'], 'L0_attn_A_log': _L0_attn_in['A_log'], 'L0_attn_D': _L0_attn_in['D'], 'L0_attn_rms_w': _L0_attn_in['rms_w'], 'L0_attn_W_out': _L0_attn_in['W_out'], 'L0_ffn_kernel_router_DE': _L0_ffn_in['kernel_router_DE'], 'L0_ffn_kernel_gating_EDF': _L0_ffn_in['kernel_gating_EDF'], 'L0_ffn_kernel_up_EDF': _L0_ffn_in['kernel_up_EDF'], 'L0_ffn_kernel_down_EFD': _L0_ffn_in['kernel_down_EFD']}
    _x0 = _d['L0_attn_x']
    _d['L0_attn_x'] = jax.random.normal(jax.random.fold_in(jax.random.key(seed), 1), (8, 1024, 128), dtype=_x0.dtype)
    del _x0
    return _d

def reference(L0_attn_x, L0_attn_ln_w, L0_attn_ln_b, L0_attn_W_in, L0_attn_conv_w, L0_attn_conv_b, L0_attn_dt_bias, L0_attn_A_log, L0_attn_D, L0_attn_rms_w, L0_attn_W_out, L0_ffn_kernel_router_DE, L0_ffn_kernel_gating_EDF, L0_ffn_kernel_up_EDF, L0_ffn_kernel_down_EFD):

    def _L0_attn_ref(x, ln_w, ln_b, W_in, conv_w, conv_b, dt_bias, A_log, D, rms_w, W_out):
        import jax, jax.numpy as jnp
        import numpy as np
        D_MODEL = 128
        D_STATE = 128
        D_CONV = 4
        EXPAND = 2
        HEADDIM = 64
        D_INNER = EXPAND * D_MODEL
        NHEADS = D_INNER // HEADDIM
        CONV_DIM = D_INNER + 2 * D_STATE
        D_IN_PROJ = 2 * D_INNER + 2 * D_STATE + NHEADS
        CHUNK = 64
        BATCH, SEQ = (8, 256)
        EPS = 1e-05

        def _segsum(a):
            T = a.shape[-1]
            cs = jnp.cumsum(a, axis=-1)
            d = cs[..., :, None] - cs[..., None, :]
            return jnp.where(jnp.tril(jnp.ones((T, T), bool)), d, -jnp.inf)

        def _mamba2_layer(x, ln_w, ln_b, W_in, conv_w, conv_b, dt_bias, A_log, D, rms_w, W_out):
            b, l, _ = x.shape
            mu = jnp.mean(x, -1, keepdims=True)
            xc = x - mu
            var = jnp.mean(xc * xc, -1, keepdims=True)
            xn = xc * jax.lax.rsqrt(var + EPS) * ln_w + ln_b
            zxbcdt = xn @ W_in.T
            z = zxbcdt[..., :D_INNER]
            xBC = zxbcdt[..., D_INNER:D_INNER + CONV_DIM]
            dt = zxbcdt[..., D_INNER + CONV_DIM:]
            dt = jax.nn.softplus(dt + dt_bias)
            xp = jnp.pad(xBC, ((0, 0), (D_CONV - 1, 0), (0, 0)))
            conv = conv_b + sum((xp[:, k:k + l, :] * conv_w[:, k] for k in range(D_CONV)))
            xBC = conv * jax.nn.sigmoid(conv)
            xs = xBC[..., :D_INNER].reshape(b, l, NHEADS, HEADDIM)
            Bm = xBC[..., D_INNER:D_INNER + D_STATE]
            Cm = xBC[..., D_INNER + D_STATE:]
            A = -jnp.exp(A_log)
            A_dt = dt * A
            Xdt = xs * dt[..., None]
            nc = l // CHUNK
            Xc = Xdt.reshape(b, nc, CHUNK, NHEADS, HEADDIM)
            Ac = A_dt.reshape(b, nc, CHUNK, NHEADS).transpose(0, 3, 1, 2)
            Bc = Bm.reshape(b, nc, CHUNK, D_STATE)
            Cc = Cm.reshape(b, nc, CHUNK, D_STATE)
            A_cs = jnp.cumsum(Ac, -1)
            Lmat = jnp.exp(_segsum(Ac))
            Y_diag = jnp.einsum('bcln,bcsn,bhcls,bcshp->bclhp', Cc, Bc, Lmat, Xc)
            decay_states = jnp.exp(A_cs[..., -1:] - A_cs)
            states = jnp.einsum('bcln,bhcl,bclhp->bchpn', Bc, decay_states, Xc)
            states = jnp.concatenate([jnp.zeros_like(states[:, :1]), states], axis=1)
            chunk_sum = jnp.pad(A_cs[..., -1], ((0, 0), (0, 0), (1, 0)))
            decay_chunk = jnp.exp(_segsum(chunk_sum))
            new_states = jnp.einsum('bhzc,bchpn->bzhpn', decay_chunk, states)
            states_prev = new_states[:, :-1]
            state_decay_out = jnp.exp(A_cs)
            Y_off = jnp.einsum('bcln,bchpn,bhcl->bclhp', Cc, states_prev, state_decay_out)
            Y = (Y_diag + Y_off).reshape(b, l, NHEADS, HEADDIM)
            Y = Y + xs * D[None, None, :, None]
            y = Y.reshape(b, l, D_INNER)
            y = y * (z * jax.nn.sigmoid(z))
            y = y * jax.lax.rsqrt(jnp.mean(y * y, -1, keepdims=True) + EPS) * rms_w
            out = y @ W_out.T
            return x + out
        return _mamba2_layer(x, ln_w, ln_b, W_in, conv_w, conv_b, dt_bias, A_log, D, rms_w, W_out)

    def _L0_ffn_ref(x, kernel_router_DE, kernel_gating_EDF, kernel_up_EDF, kernel_down_EFD):
        import jax, jax.numpy as jnp
        import numpy as np
        TOP_K = 2
        E = kernel_router_DE.shape[-1]
        x = x.astype(jnp.float32)
        router_logits_BTE = jnp.einsum('BTD,DE->BTE', x, kernel_router_DE)
        probs_BTE = jax.nn.softmax(router_logits_BTE.astype(jnp.float32), axis=-1)
        weights_BTX, indices_BTX = jax.lax.top_k(probs_BTE, TOP_K)
        norm_weights_BTX = jax.nn.softmax(weights_BTX, axis=-1)
        one_hot_BTXE = jax.nn.one_hot(indices_BTX, num_classes=E, dtype=jnp.float32)
        full_weights_BTE = jnp.sum(one_hot_BTXE * norm_weights_BTX[..., None], axis=2)
        gating_BTEF = jnp.einsum('BTD,EDF->BTEF', x, kernel_gating_EDF)
        fuse_BTEF = jax.nn.silu(gating_BTEF) * jnp.einsum('BTD,EDF->BTEF', x, kernel_up_EDF)
        down_BTED = jnp.einsum('BTEF,EFD->BTED', fuse_BTEF, kernel_down_EFD)
        out_BTD = jnp.einsum('BTED,BTE->BTD', down_BTED, full_weights_BTE)
        return out_BTD.astype(jnp.float32)
    x = L0_attn_x
    xn = _layernorm(x, axis=-1)
    x = x + _L0_attn_ref(xn, L0_attn_ln_w, L0_attn_ln_b, L0_attn_W_in, L0_attn_conv_w, L0_attn_conv_b, L0_attn_dt_bias, L0_attn_A_log, L0_attn_D, L0_attn_rms_w, L0_attn_W_out) + _L0_ffn_ref(xn, L0_ffn_kernel_router_DE, L0_ffn_kernel_gating_EDF, L0_ffn_kernel_up_EDF, L0_ffn_kernel_down_EFD)
    return x

_drawn_inputs = setup_inputs


def setup_inputs(seed=0):
    import zlib

    import numpy as np

    out = dict(_drawn_inputs(seed))
    spreads = {'L0_attn_ln_w': (1.0, 0.2),
     'L0_attn_ln_b': (0.0, 0.419),
     'L0_attn_conv_b': (0.0, 0.1),
     'L0_attn_D': (1.0, 0.6),
     'L0_attn_rms_w': (1.0, 0.2)}
    factors = {'L0_attn_dt_bias': 8.0, 'L0_attn_A_log': 8.0}
    for name, (base, spread) in spreads.items():
        noise = np.random.default_rng([zlib.crc32(name.encode()), seed]).standard_normal(out[name].shape)
        drawn = base * np.exp(spread * noise) if base else spread * noise
        out[name] = jnp.asarray(drawn.astype(out[name].dtype))
    for name, factor in factors.items():
        out[name] = (out[name] * factor).astype(out[name].dtype)
    return out
```

```python
from contextlib import ExitStack

import concourse.bass as bass
from concourse import mybir

F32 = mybir.dt.float32
F32R = mybir.dt.float32r
BF16 = mybir.dt.bfloat16
I32 = mybir.dt.int32
ALU = mybir.AluOpType
ACT = mybir.ActivationFunctionType
AX = mybir.AxisListType.X

P = 128
NB, SEQ, D = 8, 1024, 128
NT = NB * SEQ // P
NH, HD = 4, 64
DI = NH * HD
NS = 128
CONV = DI + 2 * NS
TAPS = 4
PADW = 4
SW = SEQ + PADW
GT = 512
GC = GT // P
NG = NB * SEQ // GT
SC = SEQ // P
NCT = CONV // P
NAT = NCT + DI // P
XT0, BT, CT, ZT0 = 0, 2, 3, 4
E, F = 8, 256
K = 2
ROUTE = E + NH
MT = K * NT + E
ROW = D + 4
R = 4
EPS = 1e-5
EXP_FLOOR = -104.0
MASKED = -1.0e30


def program(nc, x, ln_w, ln_b, w_in_t, w_dt, conv_w, conv_b, dt_bias, a_log, d_skip, rms_w, w_out_t,
            router, gate_w, up_w, down_w, out):
    ctx = ExitStack()
    with ctx:
        def sb(name, shape, dt=F32):
            return ctx.enter_context(nc.sbuf_tensor(name, shape, dt))

        def sem(name):
            return ctx.enter_context(nc.semaphore(name))

        bank = [ctx.enter_context(nc.psum_tensor(f"bank{i}", [P, 512], F32)) for i in range(8)]

        slots_d = nc.dram_tensor("slots_d", (MT * P, ROW), F32, kind="Internal").ap()
        moe_d = nc.dram_tensor("moe_d", (K * NT * P, D), F32, kind="Internal").ap()
        cs_d = nc.dram_tensor("cs_d", (2, NT * NH * P), F32, kind="Internal").ap()
        ncs_d = nc.dram_tensor("ncs_d", (2 * NH, NT, P), F32, kind="Internal").ap()

        x_sb = sb("x_sb", [P, NT, D])
        xw_hi = sb("xw_hi", [P, NB * SW], F32R)
        xw_lo = sb("xw_lo", [P, NB * SW], F32R)
        act = sb("act", [P, 2 * NAT * GT])
        raw = sb("raw", [P, NAT * GT])
        wk_hi = sb("wk_hi", [P, TAPS * CONV], F32R)
        wk_lo = sb("wk_lo", [P, TAPS * CONV], F32R)
        wz_hi = sb("wz_hi", [P, DI], F32R)
        wz_lo = sb("wz_lo", [P, DI], F32R)
        wo_sb = sb("wo_sb", [P, 2, D])
        rdt_w = sb("rdt_w", [P, ROUTE])
        ident = sb("ident", [P, P])
        upper = sb("upper", [P, P])
        ones = sb("ones", [P, P])
        ident_b = sb("ident_b", [P, P], BF16)
        mask_b = sb("mask_b", [P, P], BF16)
        strict_b = sb("strict_b", [P, P], BF16)
        ones_b = sb("ones_b", [P, P], BF16)
        dd_l = sb("dd_l", [10, 2, 2, P], F32R)
        dd_r = sb("dd_r", [10, 2, 2 * NH * P], F32R)
        csp = sb("csp", [P, 4, 2, P], F32R)
        cols = sb("cols", [P, 10])
        lnw_c, lnb_c, cb_c, ds_c, rms_c = (cols[:, 0:1], cols[:, 1:2], cols[:, 2:6], cols[:, 6:8], cols[:, 8:10])
        heads = sb("heads", [P, 5, NH])
        dtb_in, alog_in, dtb, a_pos, a_neg = (heads[:, i, :] for i in range(5))
        lnb_b = sb("lnb_b", [P, P])
        wdt_sb = sb("wdt_sb", [P, NH])
        stats = sb("stats", [P, NT, 6])
        tok = sb("tok", [P, 11, NT])
        mean, var, r1, q_in, sq2, r12, nm, t_a, t_b, ssq, nmr1 = (tok[:, i, :] for i in range(11))
        dts = sb("dts", [P, NT, NH])
        cs_sb = sb("cs_sb", [P, NT, NH])
        e_cs = sb("e_cs", [P, NT, NH])
        e_end = sb("e_end", [P, NT, NH])
        e_tot = sb("e_tot", [P, NT, NH])
        meta = sb("meta", [P, NT, K, 2])
        slot_i = sb("slot_i", [P, NT, K], I32)
        eid = sb("eid", [1, MT], I32)
        l_sb = sb("l_sb", [P, 2, NH * P])
        m_sb = sb("m_sb", [P, 2, NH * P])
        xdt = sb("xdt", [P, 2, DI])
        xde = sb("xde", [P, 2, DI])
        b_sb = sb("b_sb", [P, 2, NS])
        yo_sb = sb("yo_sb", [P, DI])
        y_sb = sb("y_sb", [P, DI])
        yd_sb = sb("yd_sb", [P, DI])
        yg = sb("yg", [P, 2, DI])
        sq = sb("sq", [P, 2, DI])
        state = sb("state", [P, DI])
        state_k = sb("state_k", [P, DI])
        rows = sb("rows", [P, R, K, ROW])
        slot_st = sb("slot_st", [P, R, K], I32)

        wkf, w_raw, wo_raw = act[:, 0:2048], act[:, 2048:2816], act[:, 2816:3072].rearrange("p (j d) -> p j d", j=2)
        convw = act[:, 3072:5120]
        route_sb = raw[:, 2048:2048 + NT * ROUTE].rearrange("p (t c) -> p t c", c=ROUTE)
        xn2 = [m_sb[:, u, :] for u in range(2)]
        xt_g = [l_sb[:, u, :] for u in range(2)]
        xwf = [t[:, :, :].rearrange("p a n -> p (a n)") for t in (xdt, xde)]
        te = [act[:, i * 512:(i + 1) * 512].rearrange("p (t e) -> p t e", e=E) for i in range(9)]
        th = [act[:, 4608 + i * 256:4608 + (i + 1) * 256].rearrange("p (t h) -> p t h", h=NH) for i in range(6)]
        tv = [raw[:, i * NT:(i + 1) * NT] for i in range(10)]
        oh_b = raw[:, 640:896].bitcast(BF16).rearrange("p (t e) -> p t e", e=E)
        rev = raw[:, 896:904]
        cnt_i = raw[:, 904:912].bitcast(I32)
        ntl = raw[:, 912:920]
        base = raw[:, 920:928]
        base_s = raw[:, 928:936]
        iota_r = raw[:, 936:936 + MT].bitcast(I32)
        iota_f = raw[:, 1080:1080 + MT]
        eid_f = raw[:, 1220:1220 + MT]
        tokid = raw[:, 1360:1360 + NT].bitcast(I32)
        rev_i = raw[:, 1424:1432].bitcast(I32)
        ddr0 = raw[:, 1440:1440 + 2 * NH * P // 2]
        gu_sb = act[:, 0:E * 2 * F]
        dn_sb = act[:, E * 2 * F:E * 2 * F + 2 * E * D]

        ld_w, ld_moe_w, st_zero, st_cs, st_out = (sem(n) for n in ("ld_w", "ld_moe_w", "st_zero", "st_cs", "st_out"))
        scatters = sem("scatters")
        ld_x = [sem(f"ld_x{i}") for i in range(8)]
        ld_dd = [sem(f"ld_dd{i}") for i in range(2)]
        scat = [sem(f"scat{i}") for i in range(R)]
        ld_slot = [sem(f"ld_slot{i}") for i in range(R)]
        st_moe = [sem(f"st_moe{i}") for i in range(R)]
        ld_sum = [sem(f"ld_sum{i}") for i in range(2)]
        st_sum = [sem(f"st_sum{i}") for i in range(2)]
        pool_c, pool_chain, consts, wkf_done, wk_hi_done, wdt_done, lnb_done, dtb_ps, wdve_done = (sem(n) for n in (
            "pool_c", "pool_chain", "consts", "wkf_done", "wk_hi_done", "wdt_done", "lnb_done", "dtb_ps", "wdve_done"))
        dve_chain, act_chain = sem("dve_chain"), sem("act_chain")
        var_done, sq_r1, q_done, sq_q, norm_done = (sem(n) for n in ("var_done", "sq_r1", "q_done", "sq_q", "norm_done"))
        a_xn, a_tp, a_xt, a_xw, a_hi, a_lo, a_rt, a_rs = (sem(n) for n in (
            "a_xn", "a_tp", "a_xt", "a_xw", "a_hi", "a_lo", "a_rt", "a_rs"))
        a_exp, dabs, dexp, adt_done, cs_ps, cs_copied, e_done, dsub_done, csT_ps, csp_done = (sem(n) for n in (
            "a_exp", "dabs", "dexp", "adt_done", "cs_ps", "cs_copied", "e_done", "dsub_done", "csT_ps", "csp_done"))
        gap_done, gap_exp, oh_done, rank_ps, top2_done, top2_exp, dp_done, dp_exp, slots_done, eid_done = (
            sem(n) for n in ("gap_done", "gap_exp", "oh_done", "rank_ps", "top2_done", "top2_exp", "dp_done",
                             "dp_exp", "slots_done", "eid_done"))
        conv_done, raw_done, silu_done = sem("conv_done"), sem("raw_done"), sem("silu_done")
        (dd_done, l_done, front_done, b_done, m_done, xdt_done, xde_done, mid_done, yo_done, y_done, keep_done,
         state_done, yt_done, skip_done, gate_done, sq_done, o_done, o_kept, row_done, xn_done) = (sem(n) for n in (
            "dd_done", "l_done", "front_done", "b_done", "m_done", "xdt_done", "xde_done", "mid_done", "yo_done",
            "y_done", "keep_done", "state_done", "yt_done", "skip_done", "gate_done", "sq_done", "o_done", "o_kept",
            "row_done", "xn_done"))
        (xt_done, xts_done, gu_done, silu_m, h_done, ht_done, hts_done, id_done, out_done, ym_done) = (
            sem(n) for n in ("xt_done", "xts_done", "gu_done", "silu_m", "h_done", "ht_done", "hts_done", "id_done",
                             "out_done", "ym_done"))
        ms_done, rms_sq, rms_done, resid_done, moe_sum, part_done, total_done = (sem(n) for n in (
            "ms_done", "rms_sq", "rms_done", "resid_done", "moe_sum", "part_done", "total_done"))

        def heads_b(t, n):
            return t[:, n, :].unsqueeze(2).broadcast_to([P, NH, HD])

        def by_head(t):
            return t.rearrange("p (h c) -> p h c", h=NH)

        def tile_ix(nn):
            return bass.ds(nn, 1)

        def heads_b2(t, nn):
            return t[:, tile_ix(nn), :].rearrange("p a h -> p (a h)").unsqueeze(2).broadcast_to([P, NH, HD])

        def store_sum(sp, k):
            sp.wait_ge(total_done, k + 1)
            o = (k % 2) * 3072
            sp.dma_start(out[:, 8 * k:8 * k + 8, :].rearrange("p t d -> p (t d)"), act[:, o:o + 1024])\
                .then_inc(st_sum[k % 2], 16)

        block = ctx.enter_context(nc.Block())

        def over_sequences(eng, body):
            body(0)
            with eng.Fori(1, NB - 1) as b:
                body(b)
            body(NB - 1)

        def over_tiles(eng, stages):
            lags = [lag for _, lag in stages]
            lo = 1 + -(-max(lags) // R)
            hi = (MT + min(lags)) // R

            def turn(m, checked):
                for r in range(R):
                    for fn, lag in stages:
                        if not checked or 0 <= m * R + r - lag < MT:
                            fn(m + (r - lag) // R, (r - lag) % R)

            for m in range(lo):
                turn(m, True)
            with eng.Fori(lo, hi) as m:
                turn(m, False)
            for m in range(hi, -(-(MT + max(lags)) // R)):
                turn(m, True)

        def is_first(m):
            return isinstance(m, int) and m <= 0

        @block.sync
        def _(sp):
            for i in range(8):
                sp.dma_start(x_sb[:, 8 * i:8 * i + 8, :], x[:, 8 * i:8 * i + 8, :]).then_inc(ld_x[i], 16)
            for dst, src in ((cols[:, 0:1], ln_w), (cols[:, 1:2], ln_b), (cols[:, 2:6], conv_b), (cols[:, 6:8], d_skip),
                             (cols[:, 8:10], rms_w), (w_raw, w_in_t), (wdt_sb[:, :], w_dt), (rdt_w[:, 0:E], router),
                             (wo_raw, w_out_t), (dtb_in, dt_bias.broadcast_to([P, NH])),
                             (alog_in, a_log.broadcast_to([P, NH])), (convw, conv_w.broadcast_to([P, TAPS * CONV]))):
                sp.dma_start(dst, src).then_inc(ld_w, 16)
            sp.wait_ge(consts, 1)
            for i in range(8):
                n = MT // 8
                sp.dma_start(slots_d[i * n * P:(i + 1) * n * P, :].rearrange("(t p) c -> p t c", p=P),
                             rows[:, 0, 0, :].unsqueeze(1).broadcast_to([P, n, ROW])).then_inc(st_zero, 16)
            sp.wait_ge(csp_done, 4)
            for hl in range(2):
                sp.dma_start(cs_d[hl].rearrange("(k p l) -> p k l", p=P, l=P),
                             csp[:, hl, :, :].bitcast(F32)).then_inc(st_cs, 16)
                for k in range(2):
                    nt = NT // 2
                    for h in range(NH):
                        sp.dma_start(ncs_d[hl * NH + h, k * nt:(k + 1) * nt, :],
                                     csp[h:P:NH, 2 + hl, k, :].bitcast(F32)).then_inc(st_cs, 16)
            sp.wait_ge(st_cs, 16 * 2 * (1 + 2 * NH))
            sp.wait_ge(wdve_done, 1)

            def dd_loads(b):
                for i in range(SC // 2):
                    if not (is_first(b) and i < 2):
                        sp.wait_ge(dd_done, b * SC + 2 * i - 2)
                    n = b * SC + 2 * i
                    sp.dma_start(dd_l[0:8, i % 2, :, :].bitcast(F32), ncs_d[:, bass.ds(n, 2), :])\
                        .then_inc(ld_dd[i % 2], 16)
                    sp.dma_start(dd_r[8:10, i % 2, :].bitcast(F32), cs_d[:, bass.ds(n * NH * P, 2 * NH * P)])\
                        .then_inc(ld_dd[i % 2], 16)

            over_sequences(sp, dd_loads)

            sp.wait_ge(gate_done, NT)
            sp.wait_ge(mid_done, NT)
            sp.dma_start(gu_sb.rearrange("p (e g f) -> p e g f", e=E, g=2)[:, :, 0, :],
                         gate_w.rearrange("e d f -> d e f")).then_inc(ld_moe_w, 16)
            sp.dma_start(gu_sb.rearrange("p (e g f) -> p e g f", e=E, g=2)[:, :, 1, :],
                         up_w.rearrange("e d f -> d e f")).then_inc(ld_moe_w, 16)
            sp.dma_start(dn_sb.rearrange("p (j d) -> p j d", d=D),
                         down_w.rearrange("e (j p) d -> p (e j) d", p=P)).then_inc(ld_moe_w, 16)
            for r in range(R):
                sp.wait_ge(scat[r], 16 * K * NT // R)

            def slot_load(m, r):
                if not is_first(m):
                    sp.wait_ge(xt_done, (m - 1) * R + r + 1)
                    sp.wait_ge(h_done, (m - 1) * R + r + 1)
                    sp.wait_ge(id_done, (m - 1) * R + r + 1)
                sp.dma_start(rows[:, r, 0, :], slots_d[bass.ds((m * R + r) * P, P), :]).then_inc(ld_slot[r], 16)

            over_tiles(sp, [(slot_load, 0)])

            for r in range(R):
                sp.wait_ge(st_moe[r], 16 * MT // R)
            for k in range(8):
                if k >= 2:
                    sp.wait_ge(st_sum[k % 2], 16 * (k // 2))
                    sp.wait_ge(total_done, k - 1)
                o = (k % 2) * 3072
                sp.dma_start(act[:, o:o + 1024], x[:, 8 * k:8 * k + 8, :].rearrange("p t d -> p (t d)"))\
                    .then_inc(ld_sum[k % 2], 16)
                for c in range(K):
                    sp.dma_start(act[:, o + 1024 * (c + 1):o + 1024 * (c + 2)].rearrange("p (t d) -> p t d", d=D),
                                 moe_d[(c * NT + 8 * k) * P:(c * NT + 8 * k + 8) * P, :]
                                 .rearrange("(t p) d -> p t d", p=P)).then_inc(ld_sum[k % 2], 16)
                if k >= 1:
                    store_sum(sp, k - 1)
            store_sum(sp, 7)
            for u in range(2):
                sp.wait_ge(st_sum[u], 16 * 4)

        @block.gpsimd
        def _(pool):
            n = [0]

            def chain(ins):
                n[0] += 1
                ins.then_inc(pool_chain, 1)
                pool.wait_ge(pool_chain, n[0])

            chain(pool.memset(rows[:, :, :, :], 0.0))
            chain(pool.iota(tokid[:, 0:1], pattern=[[0, 1]], base=K * NT * P, channel_multiplier=1))
            pool.tensor_copy(rows[:, 0, 0, D:D + 1], tokid[:, 0:1]).then_inc(consts, 1)
            for t, v in ((ident, 0.0), (upper, 1.0), (strict_b, 1.0), (mask_b, 0.0)):
                chain(pool.memset(t[:, :], v))
            pool.memset(ones[:, :], 1.0)
            chain(pool.memset(ones_b[:, :], 1.0))
            chain(pool.affine_select(out=ident[:, :], in_=ident[:, :], compare_op=ALU.not_equal, fill=1.0, base=0,
                                     pattern=[[-1, P]], channel_multiplier=1))
            chain(pool.affine_select(out=upper[:, :], in_=upper[:, :], compare_op=ALU.is_ge, fill=0.0, base=0,
                                     pattern=[[1, P]], channel_multiplier=-1))
            chain(pool.affine_select(out=strict_b[:, :], in_=strict_b[:, :], compare_op=ALU.is_ge, fill=0.0, base=-1,
                                     pattern=[[1, P]], channel_multiplier=-1))
            chain(pool.affine_select(out=mask_b[:, :], in_=mask_b[:, :], compare_op=ALU.is_ge, fill=MASKED, base=0,
                                     pattern=[[1, P]], channel_multiplier=-1))
            ind = ddr0[0:8, :].rearrange("p (h l) -> p h l", h=NH)
            chain(pool.memset(ddr0[0:8, :], 0.0))
            for part in range(2):
                chain(pool.affine_select(out=ind, in_=ind, compare_op=ALU.not_equal, fill=1.0, base=NH * part,
                                         pattern=[[1, NH], [0, P]], channel_multiplier=-1))
            chain(pool.iota(rev_i, pattern=[[-1, E]], base=E, channel_multiplier=0))
            chain(pool.iota(iota_r, pattern=[[1, MT]], base=0, channel_multiplier=0))
            pool.wait_ge(consts, 1)
            chain(pool.iota(tokid, pattern=[[P, NT]], base=0, channel_multiplier=1))
            pool.tensor_copy(ident_b[:, :], ident[:, :]).then_inc(consts, 1)

            pool.wait_ge(norm_done, 2)
            pool.wait_ge(st_zero, 16 * 8)
            pool.wait_ge(slots_done, 1)

            def chunk(b, j):
                nn, r = b * SC + j, j % R
                if j:
                    pool.wait_ge(state_done, nn)
                    nc.gpsimd.tensor_tensor(by_head(state_k[:, :]), by_head(state[:, :]),
                                            heads_b2(e_tot, nn), ALU.mult).then_inc(keep_done, 1)
                pool.wait_ge(xdt_done, nn + 1)
                if not (is_first(b) and j < 2):
                    pool.wait_ge(mid_done, nn - 1)
                nc.gpsimd.tensor_tensor(by_head(xde[:, j % 2, :]), by_head(xdt[:, j % 2, :]),
                                        heads_b2(e_end, nn), ALU.mult).then_inc(xde_done, 1)
                if not (is_first(b) and j < R):
                    pool.wait_ge(slots_done, 1)
                    pool.wait_ge(scat[r], 16 * K * (b * 2 + j // R))
                nc.gpsimd.tensor_copy(rows[:, r, :, D:D + 2],
                                      meta[:, tile_ix(nn), :, :].rearrange("p a k v -> p (a k) v")).then_inc(row_done, 1)
                nc.gpsimd.tensor_copy(slot_st[:, r, :],
                                      slot_i[:, tile_ix(nn), :].rearrange("p a k -> p (a k)")).then_inc(row_done, 1)
                pool.wait_ge(slots_done, 1)
                pool.wait_ge(xn_done, nn + 1)
                nc.gpsimd.tensor_copy(rows[:, r, 1, 0:D], rows[:, r, 0, 0:D]).then_inc(row_done, 1)
                pool.wait_ge(row_done, 3 * (nn + 1))
                pool.sem_inc(scatters, 1)
                for c in range(K):
                    nc.gpsimd.indirect_dma_start(
                        out=slots_d, out_offset=bass.IndirectOffsetOnAxis(ap=slot_st[:, r, c:c + 1], axis=0),
                        in_=rows[:, r, c, :], in_offset=None).then_inc(scat[r], 16)

            def sequence(b):
                for j in range(SC):
                    chunk(b, j)

            over_sequences(pool, sequence)

            def moe_scatter(m, r):
                pool.wait_ge(id_done, m * R + r + 1)
                pool.wait_ge(ym_done, m * R + r + 1)
                pool.sem_inc(scatters, 1)
                nc.gpsimd.indirect_dma_start(
                    out=moe_d, out_offset=bass.IndirectOffsetOnAxis(ap=slot_st[:, r, 0:1], axis=0),
                    in_=raw[:, r * D:(r + 1) * D], in_offset=None,
                    bounds_check=K * NT * P - 1, oob_is_err=False).then_inc(st_moe[r], 16)

            over_tiles(pool, [(moe_scatter, 0)])

            for k in range(8):
                o = (k % 2) * 3072
                pool.wait_ge(ld_sum[k % 2], 48 * (k // 2 + 1))
                nc.gpsimd.tensor_tensor(act[:, o + 1024:o + 2048], act[:, o + 1024:o + 2048],
                                        act[:, o + 2048:o + 3072], ALU.add).then_inc(moe_sum, 1)

        @block.scalar
        def _(act_e):
            A = nc.scalar.activation
            n = [0]

            def chain(ins):
                n[0] += 1
                ins.then_inc(act_chain, 1)
                act_e.wait_ge(act_chain, n[0])

            act_e.wait_ge(var_done, 1)
            A(t_b, t_a, ACT.Sqrt).then_inc(sq_r1, 1)
            act_e.wait_ge(q_done, 1)
            A(sq2, q_in, ACT.Sqrt).then_inc(sq_q, 1)
            act_e.wait_ge(ld_w, 16 * 12)
            A(a_pos, alog_in, ACT.Exp).then_inc(a_exp, 1)
            act_e.wait_ge(wkf_done, 1)
            A(wk_hi[:, :], wkf, ACT.Copy).then_inc(wk_hi_done, 1)
            A(wz_hi[:, :], w_raw[:, 0:DI], ACT.Copy).then_inc(wk_hi_done, 1)
            for i in range(2):
                A(wo_sb[:, i, :], wo_raw[:, i, :], ACT.Copy, scale=rms_c[:, i:i + 1]).then_inc(wk_hi_done, 1)

            def group(it):
                for u in range(2):
                    g = it * 2 + u
                    act_e.wait_ge(a_tp, g + 1)
                    if not is_first(it):
                        act_e.wait_ge(a_rt, g - 1)
                        act_e.wait_ge(a_lo, g - 1)
                    A(xt_g[u], bank[u][:, :], ACT.Copy).then_inc(a_xt, 1)
                    A(xwf[u], bank[u][:, :], ACT.Identity, bias=lnb_c, scale=lnw_c).then_inc(a_xw, 1)
                    act_e.wait_ge(sq_q, 1)
                    act_e.wait_ge(a_xw, g + 1)
                    A(xw_hi[:, bass.ds(it * SW + PADW + u * GT, GT)], xwf[u], ACT.Copy).then_inc(a_hi, 1)

            group(0)
            with act_e.Fori(1, NB) as it:
                group(it)

            act_e.wait_ge(dabs, 1)
            A(th[2], th[1], ACT.Exp, scale=-1.0).then_inc(dexp, 1)
            act_e.wait_ge(cs_copied, 2)
            A(e_cs[:, :, :], cs_sb[:, :, :], ACT.Exp).then_inc(e_done, 1)
            A(e_tot[:, :, :], th[5], ACT.Exp).then_inc(e_done, 1)
            act_e.wait_ge(dsub_done, 1)
            A(e_end[:, :, :], th[3], ACT.Exp).then_inc(e_done, 1)
            act_e.wait_ge(gap_done, 1)
            A(te[3], te[1], ACT.Exp).then_inc(gap_exp, 1)
            act_e.wait_ge(top2_done, 1)
            A(tv[4], tv[3], ACT.Exp).then_inc(top2_exp, 1)
            act_e.wait_ge(dp_done, 1)
            A(tv[7], tv[6], ACT.Exp).then_inc(dp_exp, 1)
            act_e.wait_ge(norm_done, 2)
            act_e.wait_ge(st_zero, 16 * 8)
            act_e.wait_ge(slots_done, 1)
            act_e.wait_ge(eid_done, 1)

            def evac(g6, i):
                act_e.wait_ge(conv_done, g6 + i + 1)
                dst = raw[:, i * GT:(i + 1) * GT]
                if i < NCT:
                    A(dst, bank[i % 2][:, :], ACT.Identity, bias=cb_c[:, i:i + 1]).then_inc(raw_done, 1)
                else:
                    A(dst, bank[i % 2][:, :], ACT.Copy).then_inc(raw_done, 1)

            def silu(g, par, early):
                act_e.wait_ge(raw_done, g * NAT + NAT)
                if not early:
                    for s in (front_done, mid_done, skip_done, gate_done):
                        act_e.wait_ge(s, g * GC - GC)
                A(act[:, par * NAT * GT:(par + 1) * NAT * GT], raw[:, :], ACT.Silu).then_inc(silu_done, 1)

            for i in range(NAT):
                evac(0, i)
            silu(0, 0, True)

            def row(nn, r, uses):
                act_e.wait_ge(norm_done, 2)
                if uses is not None:
                    act_e.wait_ge(scat[r], 16 * K * uses)
                t = tile_ix(nn)
                A(rows[:, r, 0, 0:D], x_sb[:, t, :].rearrange("p a d -> p (a d)"), ACT.Identity,
                  bias=nmr1[:, t], scale=r1[:, t]).then_inc(xn_done, 1)

            def keep_out(nn):
                act_e.wait_ge(norm_done, 2)
                act_e.wait_ge(o_done, nn + 1)
                act_e.wait_ge(xn_done, nn + 1)
                A(x_sb[:, tile_ix(nn), :].rearrange("p a d -> p (a d)"), bank[7][:, 0:D], ACT.Copy)
                A(ssq[:, tile_ix(nn)], bank[7][:, D:D + 1], ACT.Copy).then_inc(o_kept, 1)

            def square(nn, par, early):
                act_e.wait_ge(gate_done, nn + 1)
                if not early:
                    act_e.wait_ge(o_done, nn - 1)
                A(sq[:, par, :], yg[:, par, :], ACT.Square).then_inc(sq_done, 1)

            def sequence(b):
                first, last = is_first(b), isinstance(b, int) and b == NB - 1
                for j in range(SC):
                    nn, q, g = b * SC + j, j % GC, j // GC
                    act_e.wait_ge(dd_done, nn + 1)
                    if not (first and j < 2):
                        act_e.wait_ge(m_done, nn - 1)
                    A(l_sb[:, j % 2, :], bank[2][:, :], ACT.Exp).then_inc(l_done, 1)
                    row(nn, j % R, None if first and j < R else b * 2 + j // R)
                    more = not (last and g == 1)
                    if more and q < 3:
                        evac((b * 2 + g + 1) * NAT, 2 * q)
                    if not (first and j < 1):
                        square(nn - 1, (j - 1) % 2, first and j < 3)
                    if not (first and j < 2):
                        keep_out(nn - 2)
                    if more and q < 3:
                        evac((b * 2 + g + 1) * NAT, 2 * q + 1)
                    if more and q == 2:
                        silu(b * 2 + g + 1, 1 - g, first and g == 0)

            over_sequences(act_e, sequence)
            square(NT - 1, (NT - 1) % 2, False)
            keep_out(NT - 2)
            keep_out(NT - 1)
            act_e.wait_ge(ms_done, 1)
            A(t_b, t_a, ACT.Sqrt).then_inc(rms_sq, 1)

            def silu_tile(m, r):
                act_e.wait_ge(gu_done, m * R + r + 1)
                if not (is_first(m) and r < 2):
                    act_e.wait_ge(h_done, m * R + r - 1)
                A(l_sb[:, r % 2, 0:F], bank[2 + r % 2][:, 0:F], ACT.Silu).then_inc(silu_m, 1)

            def hidden_keep(m, r):
                act_e.wait_ge(ht_done, m * R + r + 1)
                if not (is_first(m) and r < 2):
                    act_e.wait_ge(out_done, m * R + r - 1)
                A(xde[:, r % 2, :], bank[4 + r % 2][:, 0:2 * P], ACT.Copy).then_inc(hts_done, 1)

            over_tiles(act_e, [(silu_tile, 0), (hidden_keep, 1)])

            act_e.wait_ge(rms_done, 1)
            for k in range(8):
                act_e.wait_ge(ld_sum[k % 2], 48 * (k // 2 + 1))
                for i in range(8):
                    t, o = 8 * k + i, (k % 2) * 3072 + i * D
                    A(act[:, o:o + D], act[:, o:o + D], ACT.Identity, bias=nmr1[:, t:t + 1],
                      scale=r12[:, t:t + 1]).then_inc(resid_done, 1)

        @block.tensor
        def _(pe):
            mm = nc.tensor.matmul
            pe.wait_ge(lnb_done, 1)
            mm(bank[7][:, 0:NH], lnb_b[:, :], wdt_sb[:, :], start=True, stop=True).then_inc(dtb_ps, 1)
            pe.wait_ge(wdt_done, 1)
            pe.wait_ge(consts, 2)

            def group(it):
                for u in range(2):
                    g = it * 2 + u
                    for i in range(4):
                        pe.wait_ge(a_xn, g * 4 + i + 1)
                        if i == 0 and not is_first(it):
                            pe.wait_ge(a_xt, g - 1)
                            pe.wait_ge(a_xw, g - 1)
                        tp = nc.tensor.transpose(bank[u][:, i * P:(i + 1) * P], xn2[u][:, i * P:(i + 1) * P], ident[:, :])
                    tp.then_inc(a_tp, 1)
                    pe.wait_ge(a_xt, g + 1)
                    if not is_first(it):
                        pe.wait_ge(a_rs, g - 1)
                    for i in range(4):
                        rt = mm(bank[4 + u][:, i * ROUTE:(i + 1) * ROUTE], xt_g[u][:, i * P:(i + 1) * P], rdt_w[:, :],
                                start=True, stop=True)
                    rt.then_inc(a_rt, 1)

            group(0)
            with pe.Fori(1, NB) as it:
                group(it)

            pe.wait_ge(adt_done, 1)
            adt = th[4].rearrange("p t h -> p (t h)")
            mm(bank[7][:, 0:256], upper[:, :], adt, start=True, stop=True)
            mm(bank[7][:, 256:512], ones[:, :], adt, start=True, stop=True).then_inc(cs_ps, 1)
            pe.wait_ge(cs_copied, 2)
            csf = cs_sb[:, :, :].rearrange("p t h -> p (t h)")
            nc.tensor.transpose(bank[6][:, 0:P], csf[:, 0:P], ident[:, :])
            nc.tensor.transpose(bank[6][:, P:2 * P], csf[:, P:2 * P], ident[:, :]).then_inc(csT_ps, 1)
            pe.wait_ge(oh_done, 1)
            ohf = oh_b.rearrange("p t e -> p (t e)")
            mm(bank[4][:, :], strict_b[:, :], ohf, start=True, stop=True)
            mm(bank[5][:, :], ones_b[:, :], ohf, start=True, stop=True).then_inc(rank_ps, 1)

            pe.wait_ge(wdve_done, 1)
            pe.wait_ge(wk_hi_done, 4)
            for done in (a_hi, a_xt, a_xw, a_rs):
                pe.wait_ge(done, NG)
            pe.wait_ge(a_lo, NG)

            def conv(b, half, g6, i, early):
                if not early:
                    pe.wait_ge(raw_done, g6 + i - 1)
                ps = bank[i % 2][:, :]
                if i < NCT:
                    terms = [(w[:, k * CONV + i * P:k * CONV + (i + 1) * P], s, k - TAPS + 1)
                             for k in range(TAPS) for w, s in ((wk_hi, xw_hi), (wk_hi, xw_lo), (wk_lo, xw_hi))]
                else:
                    c = slice((i - NCT) * P, (i - NCT + 1) * P)
                    terms = [(w[:, c], s, 0) for w, s in ((wz_hi, xw_hi), (wz_hi, xw_lo), (wz_lo, xw_hi))]
                for a, (w, s, shift) in enumerate(terms):
                    m = mm(ps, w, s[:, bass.ds(b * SW + PADW + half * GT + shift, GT)],
                           start=(a == 0), stop=(a == len(terms) - 1))
                m.then_inc(conv_done, 1)

            pe.wait_ge(e_done, 2)
            pe.wait_ge(csp_done, 4)
            for i in range(NAT):
                conv(0, 0, 0, i, i < 2)

            def project_out(nn, par, early):
                pe.wait_ge(gate_done, nn + 1)
                pe.wait_ge(sq_done, nn + 1)
                if not early:
                    pe.wait_ge(o_kept, nn)
                for c in range(2):
                    mm(bank[7][:, 0:D], yg[:, par, c * P:(c + 1) * P], wo_sb[:, c, :], start=(c == 0), stop=(c == 1))
                for c in range(2):
                    m = mm(bank[7][:, D:D + 1], sq[:, par, c * P:(c + 1) * P], ones[:, 0:1], start=(c == 0),
                           stop=(c == 1))
                m.then_inc(o_done, 1)

            def sequence(b):
                first, last = is_first(b), isinstance(b, int) and b == NB - 1
                for j in range(SC):
                    nn, q, g, u = b * SC + j, j % GC, j // GC, j % 2
                    ab = act[:, g * NAT * GT:(g + 1) * NAT * GT].rearrange("p (t n) -> p t n", n=GT)
                    cs = slice(q * P, (q + 1) * P)
                    more = not (last and g == 1)
                    nxt = (b if g == 0 else b + 1), 1 - g, (b * 2 + g + 1) * NAT
                    pe.wait_ge(ld_dd[(j // 2) % 2], 32 * (b * 2 + j // 4 + 1))
                    if not (first and j < 1):
                        pe.wait_ge(l_done, nn)
                    mm(bank[2][:, :], dd_l[:, (j // 2) % 2, j % 2, :],
                       dd_r[:, (j // 2) % 2, (j % 2) * NH * P:(j % 2 + 1) * NH * P], start=True, stop=False)
                    mm(bank[2][:, :], ident_b[:, :], mask_b[:, :].unsqueeze(1).broadcast_to([P, NH, P]),
                       start=False, stop=True).then_inc(dd_done, 1)
                    pe.wait_ge(silu_done, b * 2 + g + 1)
                    if not (first and j < 2):
                        for s in (m_done, xdt_done, b_done):
                            pe.wait_ge(s, nn - 1)
                    fb = bank[3 + u]
                    mm(fb[:, 0:P], ab[:, BT, cs], ab[:, CT, cs], start=True, stop=True)
                    for i, t in enumerate((XT0, XT0 + 1, BT)):
                        tp = nc.tensor.transpose(fb[:, (i + 1) * P:(i + 2) * P], ab[:, t, cs], ident[:, :])
                    tp.then_inc(front_done, 1)
                    if more and q < 3:
                        conv(*nxt, 2 * q, False)
                    for s in (m_done, xdt_done, b_done, xde_done):
                        pe.wait_ge(s, nn + 1)
                    if not (first and j < 1):
                        pe.wait_ge(y_done, nn)
                        pe.wait_ge(state_done, nn)
                    for h in range(NH):
                        mm(bank[5][:, h * HD:(h + 1) * HD], m_sb[:, u, h * P:(h + 1) * P],
                           xdt[:, u, h * HD:(h + 1) * HD], start=True, stop=True)
                    if j:
                        mm(bank[5][:, DI:2 * DI], ab[:, CT, cs], state[:, :], start=True, stop=True)
                    if not (first and j < 1):
                        pe.wait_ge(skip_done, nn)
                    mm(bank[6][:, 0:DI], b_sb[:, u, :], xde[:, u, :], start=True, stop=True).then_inc(mid_done, 1)
                    if more and q < 3:
                        conv(*nxt, 2 * q + 1, False)
                    pe.wait_ge(y_done, nn + 1)
                    for c in range(2):
                        tp = nc.tensor.transpose(bank[6][:, DI + c * P:DI + (c + 1) * P], y_sb[:, c * P:(c + 1) * P],
                                                 ident[:, :])
                    tp.then_inc(yt_done, 1)
                    if not (first and j < 1):
                        project_out(nn - 1, (j - 1) % 2, first and j < 2)

            over_sequences(pe, sequence)
            project_out(NT - 1, (NT - 1) % 2, False)
            pe.wait_ge(o_kept, NT)
            pe.wait_ge(ld_moe_w, 48)

            def turn_x(m, r):
                pe.wait_ge(ld_slot[r], 16 * (m + 1))
                if not (is_first(m) and r < 2):
                    pe.wait_ge(xts_done, m * R + r - 1)
                nc.tensor.transpose(bank[r % 2][:, 0:P], rows[:, r, 0, 0:D], ident[:, :]).then_inc(xt_done, 1)

            def gate_up(m, r):
                ex = pe.value_load(eid[0:1, bass.ds(m * R + r, 1)], min_val=0, max_val=E - 1)
                pe.wait_ge(xts_done, m * R + r + 1)
                if not (is_first(m) and r < 2):
                    pe.wait_ge(silu_m, m * R + r - 1)
                    pe.wait_ge(h_done, m * R + r - 1)
                mm(bank[2 + r % 2][:, :], xdt[:, r % 2, 0:P], gu_sb[:, bass.ds(ex * (2 * F), 2 * F)],
                   start=True, stop=True).then_inc(gu_done, 1)

            def turn_h(m, r):
                pe.wait_ge(h_done, m * R + r + 1)
                if not (is_first(m) and r < 2):
                    pe.wait_ge(hts_done, m * R + r - 1)
                for c in range(2):
                    tp = nc.tensor.transpose(bank[4 + r % 2][:, c * P:(c + 1) * P], m_sb[:, r % 2, c * P:(c + 1) * P],
                                             ident[:, :])
                tp.then_inc(ht_done, 1)

            def down(m, r):
                ex = pe.value_load(eid[0:1, bass.ds(m * R + r, 1)], min_val=0, max_val=E - 1)
                pe.wait_ge(hts_done, m * R + r + 1)
                if not (is_first(m) and r < 2):
                    pe.wait_ge(ym_done, m * R + r - 1)
                for c in range(2):
                    o = mm(bank[6 + r % 2][:, 0:D], xde[:, r % 2, c * P:(c + 1) * P],
                           dn_sb[:, bass.ds(ex * (2 * D) + c * D, D)], start=(c == 0), stop=(c == 1))
                o.then_inc(out_done, 1)

            over_tiles(pe, [(turn_x, 0), (gate_up, 1), (turn_h, 2), (down, 3)])

        @block.vector
        def _(dve):
            V = nc.vector
            n = [0]

            def chain(ins):
                n[0] += 1
                ins.then_inc(dve_chain, 1)
                dve.wait_ge(dve_chain, n[0])

            for t in (xw_hi, xw_lo):
                V.memset(t[:, :].rearrange("p (b s) -> p b s", b=NB)[:, :, 0:PADW].bitcast(F32), 0.0)
            V.memset(dd_l[:, :, :, :].bitcast(F32), 1.0)
            for t in range(NT):
                if t % 8 == 0:
                    dve.wait_ge(ld_x[t // 8], 16)
                st = V.bn_stats(stats[:, t, :], x_sb[:, t, :])
            chain(st)
            me, mo, ve, vo = (stats[:, :, i] for i in (1, 4, 2, 5))
            chain(V.tensor_tensor(mean, me, mo, ALU.add))
            chain(V.tensor_scalar(nm, mean, -0.5, None, ALU.mult))
            chain(V.tensor_tensor(t_a, me, mo, ALU.subtract))
            chain(V.tensor_tensor(t_a, t_a, t_a, ALU.mult))
            chain(V.tensor_tensor(var, ve, vo, ALU.add))
            chain(V.scalar_tensor_tensor(out=var, in0=t_a, scalar=float(D // 4), in1=var, op0=ALU.mult, op1=ALU.add))
            chain(V.tensor_scalar(var, var, 1.0 / D, None, ALU.mult))
            V.tensor_scalar(t_a, var, EPS, None, ALU.add).then_inc(var_done, 1)
            dve.wait_ge(sq_r1, 1)
            chain(V.reciprocal(r1, t_b))
            chain(V.tensor_tensor(t_b, r1, r1, ALU.mult))
            chain(V.tensor_tensor(t_b, t_b, var, ALU.mult))
            V.tensor_scalar(q_in, t_b, EPS, None, ALU.add).then_inc(q_done, 1)
            dve.wait_ge(sq_q, 1)
            chain(V.reciprocal(r12, sq2))
            V.tensor_tensor(nmr1, nm, r1, ALU.mult).then_inc(norm_done, 1)
            V.tensor_tensor(r12, r12, r1, ALU.mult).then_inc(norm_done, 1)
            dve.wait_ge(norm_done, 2)

            dve.wait_ge(ld_w, 16 * 12)
            chain(V.memset(lnb_b[:, :], 1.0))
            V.tensor_scalar(lnb_b[:, :], lnb_b[:, :], lnb_c, None, ALU.mult).then_inc(lnb_done, 1)
            V.tensor_scalar(rdt_w[:, E:ROUTE], wdt_sb[:, :], lnw_c, None, ALU.mult).then_inc(wdt_done, 1)
            V.tensor_tensor(wkf.rearrange("p (k c) -> p k c", k=TAPS), convw.rearrange("p (k c) -> p k c", k=TAPS),
                            w_raw[:, DI:DI + CONV].unsqueeze(1).broadcast_to([P, TAPS, CONV]), ALU.mult)\
                .then_inc(wkf_done, 1)
            dve.wait_ge(a_exp, 1)
            chain(V.tensor_scalar(a_neg, a_pos, -1.0, None, ALU.mult))
            dve.wait_ge(dtb_ps, 1)
            chain(V.tensor_tensor(dtb, dtb_in, bank[7][:, 0:NH], ALU.add))
            dve.wait_ge(wk_hi_done, 4)
            V.tensor_tensor(wk_lo[:, :], wkf, wk_hi[:, :].bitcast(F32), ALU.subtract)
            chain(V.tensor_tensor(wz_lo[:, :], w_raw[:, 0:DI], wz_hi[:, :].bitcast(F32), ALU.subtract))
            dve.wait_ge(consts, 2)
            for i in range(2):
                for a in range(2):
                    last = V.tensor_copy(dd_r[0:8, i, a * NH * P:(a + 1) * NH * P], ddr0[0:8, :])
            last.then_inc(wdve_done, 1)
            V.tensor_copy(rev, rev_i)
            V.tensor_copy(iota_f, iota_r)
            V.tensor_copy(meta[:, :, 0, 0], tokid)
            chain(V.tensor_copy(meta[:, :, 1, 0], tokid))
            chain(V.tensor_scalar(meta[:, :, 1, 0], meta[:, :, 1, 0], float(NT * P), None, ALU.add))

            def norm_group(it, u):
                g = it * 2 + u
                if not is_first(it):
                    dve.wait_ge(a_tp, g - 1)
                for i in range(4):
                    t = bass.ds(it * 8 + u * 4 + i, 1)
                    V.tensor_scalar(xn2[u][:, i * P:(i + 1) * P], x_sb[:, t, :].rearrange("p a d -> p (a d)"),
                                    nm[:, t], r12[:, t], ALU.add, ALU.mult).then_inc(a_xn, 1)

            def low_part(it, u):
                g = it * 2 + u
                dve.wait_ge(a_hi, g + 1)
                c = bass.ds(it * SW + PADW + u * GT, GT)
                V.tensor_tensor(xw_lo[:, c], xwf[u], xw_hi[:, c].bitcast(F32), ALU.subtract).then_inc(a_lo, 1)
                dve.wait_ge(a_rt, g + 1)
                V.tensor_copy(route_sb[:, bass.ds(g * 4, 4), :],
                              bank[4 + u][:, 0:4 * ROUTE].rearrange("p (t c) -> p t c", c=ROUTE)).then_inc(a_rs, 1)

            norm_group(0, 0)
            norm_group(0, 1)
            with dve.Fori(1, NB) as it:
                for u in range(2):
                    low_part(it - 1, u)
                    norm_group(it, u)
            low_part(NB - 1, 0)
            low_part(NB - 1, 1)
            dve.wait_ge(a_rs, NG)

            def over_tok(c):
                return c.unsqueeze(1).broadcast_to([P, NT, NH])

            chain(V.tensor_tensor(th[0], route_sb[:, :, E:ROUTE], over_tok(dtb), ALU.add))
            V.scalar_tensor_tensor(out=th[1], in0=th[0], scalar=-1.0, in1=th[0], op0=ALU.mult, op1=ALU.max)\
                .then_inc(dabs, 1)
            dve.wait_ge(dexp, 1)
            chain(V.tensor_scalar(th[3], th[2], 2.0, None, ALU.add))
            chain(V.reciprocal(th[3], th[3]))
            chain(V.tensor_tensor(th[2], th[2], th[3], ALU.mult))
            chain(V.tensor_tensor(th[3], th[2], th[2], ALU.mult))
            chain(V.tensor_scalar(th[5], th[3], 1.0 / 17, None, ALU.mult))
            for c in (15, 13, 11, 9, 7, 5, 3):
                chain(V.scalar_tensor_tensor(out=th[5], in0=th[5], scalar=1.0 / c, in1=th[3], op0=ALU.add,
                                             op1=ALU.mult))
            chain(V.scalar_tensor_tensor(out=th[5], in0=th[5], scalar=1.0, in1=th[2], op0=ALU.add, op1=ALU.mult))
            chain(V.tensor_scalar(th[0], th[0], 0.0, None, ALU.max))
            chain(V.scalar_tensor_tensor(out=dts[:, :, :], in0=th[5], scalar=2.0, in1=th[0], op0=ALU.mult,
                                         op1=ALU.add))
            V.tensor_tensor(th[4], dts[:, :, :], over_tok(a_neg), ALU.mult).then_inc(adt_done, 1)
            dve.wait_ge(cs_ps, 1)
            V.tensor_copy(cs_sb[:, :, :], bank[7][:, 0:256].rearrange("p (t h) -> p t h", h=NH))\
                .then_inc(cs_copied, 1)
            V.tensor_copy(th[5], bank[7][:, 256:512].rearrange("p (t h) -> p t h", h=NH)).then_inc(cs_copied, 1)
            dve.wait_ge(cs_copied, 2)
            chain(V.tensor_tensor(th[3], th[5], cs_sb[:, :, :], ALU.subtract))
            V.tensor_scalar(th[3], th[3], 0.0, None, ALU.min).then_inc(dsub_done, 1)
            dve.wait_ge(csT_ps, 1)
            tp = bank[6][:, 0:2 * P].rearrange("p (k l) -> p k l", k=2)
            hi, lo, nhi, nlo = (csp[:, i, :, :] for i in range(4))
            V.tensor_copy(hi, tp).then_inc(csp_done, 1)
            dve.wait_ge(csp_done, 1)
            V.tensor_tensor(lo, tp, hi.bitcast(F32), ALU.subtract).then_inc(csp_done, 1)
            dve.wait_ge(csp_done, 2)
            V.tensor_scalar(nhi, hi.bitcast(F32), -1.0, None, ALU.mult).then_inc(csp_done, 1)
            V.tensor_scalar(nlo, lo.bitcast(F32), -1.0, None, ALU.mult).then_inc(csp_done, 1)

            def over_e(c):
                return c.unsqueeze(2).broadcast_to([P, NT, E])

            def over_t(c):
                return c.unsqueeze(1).broadcast_to([P, NT, E])

            lg, gap, pick, ex, oh0, gap2, oh1, pos, cnt = te
            chain(V.tensor_tensor(lg, route_sb[:, :, 0:E], over_e(sq2), ALU.mult))
            chain(V.tensor_reduce(tv[0], lg, AX, ALU.max))
            chain(V.tensor_tensor(gap, lg, over_e(tv[0]), ALU.subtract))
            V.tensor_scalar(gap, gap, EXP_FLOOR, None, ALU.max).then_inc(gap_done, 1)
            dve.wait_ge(gap_done, 1)
            chain(V.scalar_tensor_tensor(out=pick, in0=gap, scalar=0.0, in1=over_t(rev), op0=ALU.is_ge,
                                         op1=ALU.mult))
            chain(V.tensor_reduce(tv[1], pick, AX, ALU.max))
            chain(V.tensor_tensor(oh0, pick, over_e(tv[1]), ALU.is_equal))
            chain(V.scalar_tensor_tensor(out=gap2, in0=oh0, scalar=-1.0e4, in1=gap, op0=ALU.mult, op1=ALU.add))
            V.tensor_reduce(tv[3], gap2, AX, ALU.max).then_inc(top2_done, 1)
            dve.wait_ge(top2_done, 1)
            chain(V.tensor_tensor(pick, gap2, over_e(tv[3]), ALU.is_equal))
            chain(V.tensor_tensor(pick, pick, over_t(rev), ALU.mult))
            chain(V.tensor_reduce(tv[1], pick, AX, ALU.max))
            chain(V.tensor_tensor(oh1, pick, over_e(tv[1]), ALU.is_equal))
            V.tensor_tensor(oh_b, oh0, oh1, ALU.add).then_inc(oh_done, 1)
            dve.wait_ge(gap_exp, 1)
            chain(V.tensor_reduce(tv[0], ex, AX, ALU.add))
            chain(V.reciprocal(tv[5], tv[0]))
            dve.wait_ge(top2_exp, 1)
            chain(V.tensor_tensor(tv[6], tv[4], tv[5], ALU.mult))
            V.tensor_tensor(tv[6], tv[6], tv[5], ALU.subtract).then_inc(dp_done, 1)
            dve.wait_ge(rank_ps, 1)
            chain(V.tensor_copy(cnt, bank[5][:, :].rearrange("p (t e) -> p t e", e=E)))
            src, spare = cnt, [lg, gap2]
            step, turn = 1, 0
            while step < NT:
                dst = spare[turn % 2]
                V.tensor_copy(dst[:, 0:step, :], src[:, 0:step, :])
                chain(V.tensor_tensor(dst[:, step:, :], src[:, step:, :], src[:, 0:NT - step, :], ALU.add))
                src, step, turn = dst, 2 * step, turn + 1
            incl = src
            chain(V.tensor_tensor(pos, incl, bank[4][:, :].rearrange("p (t e) -> p t e", e=E), ALU.add))
            chain(V.tensor_tensor(pos, pos, cnt, ALU.subtract))
            chain(V.tensor_scalar(cnt_i, incl[:, NT - 1, :], float(P - 1), None, ALU.add))
            chain(V.tensor_scalar(cnt_i, cnt_i, 7, None, ALU.arith_shift_right))
            chain(V.tensor_copy(ntl, cnt_i))
            chain(V.memset(base, 0.0))
            for e in range(1, E):
                chain(V.tensor_tensor(base[:, e:e + 1], base[:, e - 1:e], ntl[:, e - 1:e], ALU.add))
            chain(V.tensor_scalar(base_s, base, float(P), None, ALU.mult))
            chain(V.tensor_tensor(pos, pos, over_t(base_s), ALU.add))
            for c, oh in enumerate((oh0, oh1)):
                chain(V.tensor_tensor(pick, oh, pos, ALU.mult))
                chain(V.tensor_reduce(tv[8], pick, AX, ALU.add))
                chain(V.tensor_copy(slot_i[:, :, c], tv[8]))
            dve.wait_ge(dp_exp, 1)
            chain(V.tensor_scalar(tv[8], tv[7], 1.0, None, ALU.add))
            chain(V.reciprocal(tv[9], tv[8]))
            chain(V.tensor_tensor(meta[:, :, 1, 1], tv[7], tv[9], ALU.mult))
            V.tensor_copy(meta[:, :, 0, 1], tv[9]).then_inc(slots_done, 1)
            chain(V.memset(eid_f[0:1, :], 0.0))
            for e in range(1, E):
                chain(V.scalar_tensor_tensor(out=eid_f[0:1, :], in0=iota_f[0:1, :], scalar=base[0:1, e:e + 1],
                                             in1=eid_f[0:1, :], op0=ALU.is_ge, op1=ALU.add))
            V.tensor_copy(eid[:, :], eid_f[0:1, :]).then_inc(eid_done, 1)

            dve.wait_ge(e_done, 3)

            def sequence(b):
                first = is_first(b)
                for j in range(SC):
                    nn, q, g, u = b * SC + j, j % GC, j // GC, j % 2
                    ab = act[:, g * NAT * GT:(g + 1) * NAT * GT].rearrange("p (t n) -> p t n", n=GT)
                    cs = slice(q * P, (q + 1) * P)
                    fb = bank[3 + u]
                    dve.wait_ge(front_done, nn + 1)
                    if not (first and j < 2):
                        dve.wait_ge(mid_done, nn - 1)
                        dve.wait_ge(xde_done, nn - 1)
                    V.tensor_tensor(by_head(xdt[:, u, :]), by_head(fb[:, P:P + DI]), heads_b2(dts, nn),
                                    ALU.mult).then_inc(xdt_done, 1)
                    dve.wait_ge(l_done, nn + 1)
                    V.tensor_tensor(m_sb[:, u, :].rearrange("p (h l) -> p h l", h=NH),
                                    l_sb[:, u, :].rearrange("p (h l) -> p h l", h=NH),
                                    fb[:, 0:P].unsqueeze(1).broadcast_to([P, NH, P]), ALU.mult).then_inc(m_done, 1)
                    V.tensor_copy(b_sb[:, u, :], fb[:, 384:512]).then_inc(b_done, 1)
                    dve.wait_ge(mid_done, nn + 1)
                    if j:
                        if not (first and j == 1):
                            dve.wait_ge(y_done, nn)
                        V.tensor_tensor(by_head(yo_sb[:, :]), by_head(bank[5][:, DI:2 * DI]), heads_b2(e_cs, nn),
                                        ALU.mult).then_inc(yo_done, 1)
                        dve.wait_ge(keep_done, b * (SC - 1) + j)
                        V.tensor_tensor(state[:, :], state_k[:, :], bank[6][:, 0:DI], ALU.add).then_inc(state_done, 1)
                        dve.wait_ge(yo_done, b * (SC - 1) + j)
                        dve.wait_ge(yt_done, nn)
                        V.tensor_tensor(y_sb[:, :], yo_sb[:, :], bank[5][:, 0:DI], ALU.add).then_inc(y_done, 1)
                    else:
                        V.tensor_copy(state[:, :], bank[6][:, 0:DI]).then_inc(state_done, 1)
                        if not first:
                            dve.wait_ge(yt_done, nn)
                        V.tensor_copy(y_sb[:, :], bank[5][:, 0:DI]).then_inc(y_done, 1)
                    dve.wait_ge(yt_done, nn + 1)
                    for c in range(2):
                        sk = V.scalar_tensor_tensor(out=yd_sb[:, c * P:(c + 1) * P], in0=ab[:, XT0 + c, cs],
                                                    scalar=ds_c[:, c:c + 1], in1=bank[6][:, DI + c * P:DI + (c + 1) * P],
                                                    op0=ALU.mult, op1=ALU.add)
                    sk.then_inc(skip_done, 1)
                    dve.wait_ge(skip_done, nn + 1)
                    if not (first and j < 2):
                        dve.wait_ge(o_done, nn - 1)
                        dve.wait_ge(sq_done, nn - 1)
                    V.tensor_tensor(yg[:, u, :].rearrange("p (c l) -> p c l", c=2),
                                    yd_sb[:, :].rearrange("p (c l) -> p c l", c=2), ab[:, ZT0:ZT0 + 2, cs],
                                    ALU.mult).then_inc(gate_done, 1)

            over_sequences(dve, sequence)
            dve.wait_ge(o_kept, NT)
            V.tensor_scalar(t_a, ssq, 1.0 / DI, EPS, ALU.mult, ALU.add).then_inc(ms_done, 1)
            dve.wait_ge(rms_sq, 1)
            chain(V.reciprocal(var, t_b))
            V.tensor_scalar(r12, r1, 1.0, None, ALU.add).then_inc(rms_done, 1)
            for r in range(R):
                dve.wait_ge(scat[r], 16 * K * NT // R)

            def x_keep(m, r):
                dve.wait_ge(xt_done, m * R + r + 1)
                if not (is_first(m) and r < 2):
                    dve.wait_ge(gu_done, m * R + r - 1)
                V.tensor_copy(xdt[:, r % 2, 0:P], bank[r % 2][:, 0:P]).then_inc(xts_done, 1)

            def destination(m, r):
                dve.wait_ge(ld_slot[r], 16 * (m + 1))
                if not is_first(m):
                    dve.wait_ge(st_moe[r], 16 * m)
                V.tensor_copy(slot_st[:, r, 0:1], rows[:, r, 0, D:D + 1]).then_inc(id_done, 1)

            def hidden(m, r):
                dve.wait_ge(silu_m, m * R + r + 1)
                if not (is_first(m) and r < 2):
                    dve.wait_ge(ht_done, m * R + r - 1)
                V.scalar_tensor_tensor(out=m_sb[:, r % 2, 0:F], in0=l_sb[:, r % 2, 0:F],
                                       scalar=rows[:, r, 0, D + 1:D + 2], in1=bank[2 + r % 2][:, F:2 * F],
                                       op0=ALU.mult, op1=ALU.mult).then_inc(h_done, 1)

            def y_keep(m, r):
                dve.wait_ge(out_done, m * R + r + 1)
                if not is_first(m):
                    dve.wait_ge(st_moe[r], 16 * m)
                V.tensor_copy(raw[:, r * D:(r + 1) * D], bank[6 + r % 2][:, 0:D]).then_inc(ym_done, 1)

            over_tiles(dve, [(x_keep, 0), (y_keep, 4), (hidden, 2), (destination, 2)])

            for k in range(8):
                o = (k % 2) * 3072
                for i in range(8):
                    t = 8 * k + i
                    dve.wait_ge(resid_done, t + 1)
                    V.scalar_tensor_tensor(out=act[:, o + i * D:o + (i + 1) * D], in0=x_sb[:, t, :],
                                           scalar=var[:, t:t + 1], in1=act[:, o + i * D:o + (i + 1) * D],
                                           op0=ALU.mult, op1=ALU.add).then_inc(part_done, 1)
                dve.wait_ge(part_done, 8 * (k + 1))
                dve.wait_ge(moe_sum, k + 1)
                V.tensor_tensor(act[:, o:o + 1024], act[:, o:o + 1024], act[:, o + 1024:o + 2048], ALU.add)\
                    .then_inc(total_done, 1)


def kernel(**inputs):
    import numpy as np
    import concourse.bacc as bacc
    from concourse.bass_utils import run_bass_kernel_spmd

    a = {k.removeprefix("L0_"): np.asarray(v) for k, v in inputs.items()}
    xi = a["attn_x"]
    w_in = a["attn_W_in"]
    arrays = {
        "x": xi.reshape(NT, P, D).transpose(1, 0, 2),
        "ln_w": a["attn_ln_w"].reshape(D, 1),
        "ln_b": a["attn_ln_b"].reshape(D, 1),
        "w_in_t": w_in[:DI + CONV].T,
        "w_dt": w_in[DI + CONV:].T,
        "conv_w": a["attn_conv_w"].T.reshape(1, TAPS * CONV),
        "conv_b": a["attn_conv_b"].reshape(NCT, P).T,
        "dt_bias": a["attn_dt_bias"].reshape(1, NH),
        "a_log": a["attn_A_log"].reshape(1, NH),
        "d_skip": np.repeat(a["attn_D"], HD).reshape(2, P).T,
        "rms_w": a["attn_rms_w"].reshape(2, P).T,
        "w_out_t": a["attn_W_out"].T.reshape(2, P, D).transpose(1, 0, 2),
        "router": a["ffn_kernel_router_DE"],
        "gate_w": a["ffn_kernel_gating_EDF"],
        "up_w": a["ffn_kernel_up_EDF"],
        "down_w": a["ffn_kernel_down_EFD"],
    }
    nc = bacc.Bacc("TRN2", target_bir_lowering=False, num_devices=1)
    feeds, args = {}, []
    for name, v in arrays.items():
        v = np.ascontiguousarray(v)
        feeds[f"in_{name}"] = v
        args.append(nc.dram_tensor(f"in_{name}", v.shape, mybir.dt.from_np(v.dtype), kind="ExternalInput").ap())
    args.append(nc.dram_tensor("out_0", (P, NT, D), F32, kind="ExternalOutput").ap())
    program(nc, *args)
    r = run_bass_kernel_spmd(nc, [feeds], core_ids=[0])
    got = r.results[0]["out_0"]
    return np.ascontiguousarray(got.transpose(1, 0, 2)).reshape(NB, SEQ, D)
```

```python
from contextlib import ExitStack

import concourse.bass as bass
from concourse import mybir

F32 = mybir.dt.float32
F32R = mybir.dt.float32r
BF16 = mybir.dt.bfloat16
I32 = mybir.dt.int32
ALU = mybir.AluOpType
ACT = mybir.ActivationFunctionType
AX = mybir.AxisListType.X

P = 128
NB, SEQ, D = 8, 1024, 128
NT = NB * SEQ // P
NH, HD = 4, 64
DI = NH * HD
NS = 128
CONV = DI + 2 * NS
TAPS = 4
PADW = 4
SW = SEQ + PADW
GT = 512
GC = GT // P
NG = NB * SEQ // GT
SC = SEQ // P
NCT = CONV // P
NAT = NCT + DI // P
XT0, BT, CT, ZT0 = 0, 2, 3, 4
ORDER = (BT, CT, XT0, XT0 + 1, ZT0, ZT0 + 1)
HALO = TAPS - 1
E, F = 8, 256
K = 2
ROUTE = E + NH
PS = 2 * P
MP = K * NT * P // PS + E
ROW = D + 4
R = 4
EPS = 1e-5
EXP_FLOOR = -104.0
MASKED = -1.0e30


def program(nc, x, ln_w, ln_b, w_in_t, w_dt, conv_w, conv_b, dt_bias, a_log, d_skip, rms_w, w_out_t,
            router, gate_w, up_w, down_w, out):
    ctx = ExitStack()
    with ctx:
        def sb(name, shape, dt=F32):
            return ctx.enter_context(nc.sbuf_tensor(name, shape, dt))

        def sem(name):
            return ctx.enter_context(nc.semaphore(name))

        bank = [ctx.enter_context(nc.psum_tensor(f"bank{i}", [P, 512], F32)) for i in range(8)]

        slots_d = nc.dram_tensor("slots_d", (MP * PS, ROW), F32, kind="Internal").ap()
        moe_d = nc.dram_tensor("moe_d", (K * NT * P, D), F32, kind="Internal").ap()
        cs_d = nc.dram_tensor("cs_d", (2, NT * NH * P), F32, kind="Internal").ap()
        ncs_d = nc.dram_tensor("ncs_d", (2 * NH, NT, P), F32, kind="Internal").ap()

        x_sb = sb("x_sb", [P, NT, D])
        xw_hi = sb("xw_hi", [P, NB * SW], F32R)
        xw_lo = sb("xw_lo", [P, NB * SW], F32R)
        act = sb("act", [P, 2 * NAT * GT])
        raw = sb("raw", [P, NAT * GT])
        w_hi = sb("w_hi", [P, DI + CONV], F32R)
        w_lo = sb("w_lo", [P, DI + CONV], F32R)
        taps = sb("taps", [P, NCT, TAPS])
        wo_sb = sb("wo_sb", [P, 2, D])
        rdt_w = sb("rdt_w", [P, ROUTE])
        ident = sb("ident", [P, P])
        upper = sb("upper", [P, P])
        ones = sb("ones", [P, P])
        ident_b = sb("ident_b", [P, P], BF16)
        mask_b = sb("mask_b", [P, P], BF16)
        strict_b = sb("strict_b", [P, P], BF16)
        ones_b = sb("ones_b", [P, P], BF16)
        dd_l = sb("dd_l", [10, 2, 2, P], F32R)
        dd_r = sb("dd_r", [10, 2, 2 * NH * P], F32R)
        csp = sb("csp", [P, 4, 2, P], F32R)
        cols = sb("cols", [P, 10])
        lnw_c, lnb_c, cb_c, ds_c, rms_c = (cols[:, 0:1], cols[:, 1:2], cols[:, 2:6], cols[:, 6:8], cols[:, 8:10])
        heads = sb("heads", [P, 5, NH])
        dtb_in, alog_in, dtb, a_pos, a_neg = (heads[:, i, :] for i in range(5))
        lnb_b = sb("lnb_b", [P, P])
        wdt_sb = sb("wdt_sb", [P, NH])
        stats = sb("stats", [P, NT, 6])
        tok = sb("tok", [P, 11, NT])
        mean, var, r1, q_in, sq2, r12, nm, t_a, t_b, ssq, nmr1 = (tok[:, i, :] for i in range(11))
        dts = sb("dts", [P, NT, NH])
        cs_sb = sb("cs_sb", [P, NT, NH])
        e_cs = sb("e_cs", [P, NT, NH])
        e_end = sb("e_end", [P, NT, NH])
        e_tot = sb("e_tot", [P, NT, NH])
        meta = sb("meta", [P, NT, K, 2])
        slot_i = sb("slot_i", [P, NT, K], I32)
        eid = sb("eid", [1, MP], I32)
        l_sb = sb("l_sb", [P, 2, NH * P])
        m_sb = sb("m_sb", [P, 2, NH * P])
        xdt = sb("xdt", [P, 2, DI])
        xde = sb("xde", [P, 2, DI])
        b_sb = sb("b_sb", [P, 2, NS])
        yo_sb = sb("yo_sb", [P, DI])
        y_sb = sb("y_sb", [P, 2, DI])
        yd_sb = sb("yd_sb", [P, DI])
        yg = sb("yg", [P, 2, DI])
        sq = sb("sq", [P, 2, DI])
        state = sb("state", [P, DI])
        state_k = sb("state_k", [P, DI])
        rows = sb("rows", [P, R, K, ROW])
        slot_st = sb("slot_st", [P, R, K], I32)

        w_raw, wo_raw = act[:, 2048:2816], act[:, 2816:3072].rearrange("p (j d) -> p j d", j=2)
        proj = raw[:, 0:NCT * (HALO + GT)].rearrange("p (i n) -> p i n", i=NCT)
        route_sb = raw[:, 2048:2048 + NT * ROUTE].rearrange("p (t c) -> p t c", c=ROUTE)
        xn2 = [m_sb[:, u, :] for u in range(2)]
        xt_g = [l_sb[:, u, :] for u in range(2)]
        xwf = [t[:, :, :].rearrange("p a n -> p (a n)") for t in (xdt, xde)]
        te = [act[:, i * 512:(i + 1) * 512].rearrange("p (t e) -> p t e", e=E) for i in range(9)]
        th = [act[:, 4608 + i * 256:4608 + (i + 1) * 256].rearrange("p (t h) -> p t h", h=NH) for i in range(6)]
        tv = [raw[:, i * NT:(i + 1) * NT] for i in range(10)]
        oh_b = raw[:, 640:896].bitcast(BF16).rearrange("p (t e) -> p t e", e=E)
        rev = raw[:, 896:904]
        cnt_i = raw[:, 904:912].bitcast(I32)
        ntl = raw[:, 912:920]
        base = raw[:, 920:928]
        base_s = raw[:, 928:936]
        iota_r = raw[:, 936:936 + MP].bitcast(I32)
        iota_f = raw[:, 1080:1080 + MP]
        eid_f = raw[:, 1220:1220 + MP]
        tokid = raw[:, 1360:1360 + NT].bitcast(I32)
        rev_i = raw[:, 1424:1432].bitcast(I32)
        ddr0 = raw[:, 1440:1440 + 2 * NH * P // 2]
        ym = [raw[:, r * 2 * D:(r + 1) * 2 * D] for r in range(R)]
        ht = [raw[:, (2 * R + u * 4) * P:(2 * R + u * 4 + 4) * P] for u in range(2)]
        gu_sb = act[:, 0:E * 2 * F]
        dn_sb = act[:, E * 2 * F:E * 2 * F + 2 * E * D]

        ld_w, ld_moe_w, st_zero, st_cs, st_out = (sem(n) for n in ("ld_w", "ld_moe_w", "st_zero", "st_cs", "st_out"))
        scatters = sem("scatters")
        ld_x = [sem(f"ld_x{i}") for i in range(8)]
        ld_dd = [sem(f"ld_dd{i}") for i in range(2)]
        scat = [sem(f"scat{i}") for i in range(R)]
        ld_slot = [sem(f"ld_slot{i}") for i in range(R)]
        st_moe = [sem(f"st_moe{i}") for i in range(R)]
        ld_sum = [sem(f"ld_sum{i}") for i in range(2)]
        st_sum = [sem(f"st_sum{i}") for i in range(2)]
        pool_chain, consts, w_hi_done, wdt_done, lnb_done, dtb_ps, wdve_done = (sem(n) for n in (
            "pool_chain", "consts", "w_hi_done", "wdt_done", "lnb_done", "dtb_ps", "wdve_done"))
        dve_chain, act_chain = sem("dve_chain"), sem("act_chain")
        var_done, sq_r1, q_done, sq_q, norm_done = (sem(n) for n in ("var_done", "sq_r1", "q_done", "sq_q", "norm_done"))
        a_xn, a_tp, a_xt, a_xw, a_hi, a_lo, a_rt, a_rs = (sem(n) for n in (
            "a_xn", "a_tp", "a_xt", "a_xw", "a_hi", "a_lo", "a_rt", "a_rs"))
        a_exp, dabs, dexp, adt_done, cs_ps, cs_copied, e_done, dsub_done, csT_ps, csp_done = (sem(n) for n in (
            "a_exp", "dabs", "dexp", "adt_done", "cs_ps", "cs_copied", "e_done", "dsub_done", "csT_ps", "csp_done"))
        gap_done, gap_exp, oh_done, rank_ps, top2_done, top2_exp, dp_done, dp_exp, slots_done, eid_done = (
            sem(n) for n in ("gap_done", "gap_exp", "oh_done", "rank_ps", "top2_done", "top2_exp", "dp_done",
                             "dp_exp", "slots_done", "eid_done"))
        proj_ps, proj_done, halo_done, tap0_done, taps_done, silu_done, gate_silu = (sem(n) for n in (
            "proj_ps", "proj_done", "halo_done", "tap0_done", "taps_done", "silu_done", "gate_silu"))
        (dd_done, l_done, front_done, b_done, m_done, xdt_done, xde_done, mid_done, yo_done, y_done, keep_done,
         state_done, yt_done, skip_done, gate_done, sq_done, o_done, o_kept, row_done, xn_done) = (sem(n) for n in (
            "dd_done", "l_done", "front_done", "b_done", "m_done", "xdt_done", "xde_done", "mid_done", "yo_done",
            "y_done", "keep_done", "state_done", "yt_done", "skip_done", "gate_done", "sq_done", "o_done", "o_kept",
            "row_done", "xn_done"))
        (xt_done, xts_done, gu_done, silu_m, h_done, ht_done, hts_done, id_done, out_done, ym_done) = (
            sem(n) for n in ("xt_done", "xts_done", "gu_done", "silu_m", "h_done", "ht_done", "hts_done", "id_done",
                             "out_done", "ym_done"))
        ms_done, rms_sq, rms_done, resid_done, moe_sum, part_done, total_done = (sem(n) for n in (
            "ms_done", "rms_sq", "rms_done", "resid_done", "moe_sum", "part_done", "total_done"))

        def heads_b(t, n):
            return t[:, n, :].unsqueeze(2).broadcast_to([P, NH, HD])

        def by_head(t):
            return t.rearrange("p (h c) -> p h c", h=NH)

        def tile_ix(nn):
            return bass.ds(nn, 1)

        def heads_b2(t, nn):
            return t[:, tile_ix(nn), :].rearrange("p a h -> p (a h)").unsqueeze(2).broadcast_to([P, NH, HD])

        def store_sum(sp, k):
            sp.wait_ge(total_done, k + 1)
            o = (k % 2) * 3072
            sp.dma_start(out[:, 8 * k:8 * k + 8, :].rearrange("p t d -> p (t d)"), act[:, o:o + 1024])\
                .then_inc(st_sum[k % 2], 16)

        block = ctx.enter_context(nc.Block())

        def over_sequences(eng, body):
            body(0)
            with eng.Fori(1, NB - 1) as b:
                body(b)
            body(NB - 1)

        def over_pairs(eng, stages):
            lags = [lag for _, lag in stages]
            lo = 1 + -(-max(lags) // R)
            hi = (MP + min(lags)) // R

            def turn(m, checked):
                for r in range(R):
                    for fn, lag in stages:
                        if not checked or 0 <= m * R + r - lag < MP:
                            fn(m + (r - lag) // R, (r - lag) % R)

            for m in range(lo):
                turn(m, True)
            with eng.Fori(lo, hi) as m:
                turn(m, False)
            for m in range(hi, -(-(MP + max(lags)) // R)):
                turn(m, True)

        def is_first(m):
            return isinstance(m, int) and m <= 0

        def is_last(b):
            return isinstance(b, int) and b == NB - 1

        def group_act(g):
            return act[:, (g % 2) * NAT * GT:(g % 2 + 1) * NAT * GT].rearrange("p (t n) -> p t n", n=GT)

        def in_group(j):
            return slice((j % GC) * P, (j % GC + 1) * P)

        @block.sync
        def _(sp):
            for i in range(8):
                sp.dma_start(x_sb[:, 8 * i:8 * i + 8, :], x[:, 8 * i:8 * i + 8, :]).then_inc(ld_x[i], 16)
            for dst, src in ((cols[:, 0:1], ln_w), (cols[:, 1:2], ln_b), (cols[:, 2:6], conv_b), (cols[:, 6:8], d_skip),
                             (cols[:, 8:10], rms_w), (w_raw, w_in_t), (wdt_sb[:, :], w_dt), (rdt_w[:, 0:E], router),
                             (wo_raw, w_out_t), (dtb_in, dt_bias.broadcast_to([P, NH])),
                             (alog_in, a_log.broadcast_to([P, NH])), (taps[:, :, :], conv_w)):
                sp.dma_start(dst, src).then_inc(ld_w, 16)
            sp.wait_ge(consts, 1)
            for i in range(8):
                n = MP * PS // P // 8
                sp.dma_start(slots_d[i * n * P:(i + 1) * n * P, :].rearrange("(t p) c -> p t c", p=P),
                             rows[:, 0, 0, :].unsqueeze(1).broadcast_to([P, n, ROW])).then_inc(st_zero, 16)
            sp.wait_ge(csp_done, 4)
            for hl in range(2):
                sp.dma_start(cs_d[hl].rearrange("(k p l) -> p k l", p=P, l=P),
                             csp[:, hl, :, :].bitcast(F32)).then_inc(st_cs, 16)
                for k in range(2):
                    nt = NT // 2
                    for h in range(NH):
                        sp.dma_start(ncs_d[hl * NH + h, k * nt:(k + 1) * nt, :],
                                     csp[h:P:NH, 2 + hl, k, :].bitcast(F32)).then_inc(st_cs, 16)
            sp.wait_ge(st_cs, 16 * 2 * (1 + 2 * NH))
            sp.wait_ge(wdve_done, 1)

            def dd_loads(b):
                for i in range(SC // 2):
                    if not (is_first(b) and i < 2):
                        sp.wait_ge(dd_done, b * SC + 2 * i - 2)
                    n = b * SC + 2 * i
                    sp.dma_start(dd_l[0:8, i % 2, :, :].bitcast(F32), ncs_d[:, bass.ds(n, 2), :])\
                        .then_inc(ld_dd[i % 2], 16)
                    sp.dma_start(dd_r[8:10, i % 2, :].bitcast(F32), cs_d[:, bass.ds(n * NH * P, 2 * NH * P)])\
                        .then_inc(ld_dd[i % 2], 16)

            over_sequences(sp, dd_loads)

            sp.wait_ge(gate_done, NT)
            sp.wait_ge(mid_done, NT)
            sp.dma_start(gu_sb.rearrange("p (e g f) -> p e g f", e=E, g=2)[:, :, 0, :],
                         gate_w.rearrange("e d f -> d e f")).then_inc(ld_moe_w, 16)
            sp.dma_start(gu_sb.rearrange("p (e g f) -> p e g f", e=E, g=2)[:, :, 1, :],
                         up_w.rearrange("e d f -> d e f")).then_inc(ld_moe_w, 16)
            sp.dma_start(dn_sb.rearrange("p (j d) -> p j d", d=D),
                         down_w.rearrange("e (j p) d -> p (e j) d", p=P)).then_inc(ld_moe_w, 16)
            for r in range(R):
                sp.wait_ge(scat[r], 16 * K * NT // R)

            def slot_load(m, r):
                if not is_first(m):
                    sp.wait_ge(id_done, (m - 1) * R + r + 1)
                sp.dma_start(rows[:, r, :, :], slots_d[bass.ds((m * R + r) * PS, PS), :]
                             .rearrange("(p c) v -> p c v", c=2)).then_inc(ld_slot[r], 16)

            over_pairs(sp, [(slot_load, 0)])

            for r in range(R):
                sp.wait_ge(st_moe[r], 16 * 2 * MP // R)
            for k in range(8):
                if k >= 2:
                    sp.wait_ge(st_sum[k % 2], 16 * (k // 2))
                    sp.wait_ge(total_done, k - 1)
                o = (k % 2) * 3072
                sp.dma_start(act[:, o:o + 1024], x[:, 8 * k:8 * k + 8, :].rearrange("p t d -> p (t d)"))\
                    .then_inc(ld_sum[k % 2], 16)
                for c in range(K):
                    sp.dma_start(act[:, o + 1024 * (c + 1):o + 1024 * (c + 2)].rearrange("p (t d) -> p t d", d=D),
                                 moe_d[(c * NT + 8 * k) * P:(c * NT + 8 * k + 8) * P, :]
                                 .rearrange("(t p) d -> p t d", p=P)).then_inc(ld_sum[k % 2], 16)
                if k >= 1:
                    store_sum(sp, k - 1)
            store_sum(sp, 7)
            for u in range(2):
                sp.wait_ge(st_sum[u], 16 * 4)

        @block.gpsimd
        def _(pool):
            n = [0]

            def chain(ins):
                n[0] += 1
                ins.then_inc(pool_chain, 1)
                pool.wait_ge(pool_chain, n[0])

            chain(pool.memset(rows[:, :, :, :], 0.0))
            chain(pool.iota(tokid[:, 0:1], pattern=[[0, 1]], base=K * NT * P, channel_multiplier=1))
            pool.tensor_copy(rows[:, 0, 0, D:D + 1], tokid[:, 0:1]).then_inc(consts, 1)
            for t, v in ((ident, 0.0), (upper, 1.0), (strict_b, 1.0), (mask_b, 0.0)):
                chain(pool.memset(t[:, :], v))
            pool.memset(ones[:, :], 1.0)
            chain(pool.memset(ones_b[:, :], 1.0))
            chain(pool.affine_select(out=ident[:, :], in_=ident[:, :], compare_op=ALU.not_equal, fill=1.0, base=0,
                                     pattern=[[-1, P]], channel_multiplier=1))
            chain(pool.affine_select(out=upper[:, :], in_=upper[:, :], compare_op=ALU.is_ge, fill=0.0, base=0,
                                     pattern=[[1, P]], channel_multiplier=-1))
            chain(pool.affine_select(out=strict_b[:, :], in_=strict_b[:, :], compare_op=ALU.is_ge, fill=0.0, base=-1,
                                     pattern=[[1, P]], channel_multiplier=-1))
            chain(pool.affine_select(out=mask_b[:, :], in_=mask_b[:, :], compare_op=ALU.is_ge, fill=MASKED, base=0,
                                     pattern=[[1, P]], channel_multiplier=-1))
            ind = ddr0[0:8, :].rearrange("p (h l) -> p h l", h=NH)
            chain(pool.memset(ddr0[0:8, :], 0.0))
            for part in range(2):
                chain(pool.affine_select(out=ind, in_=ind, compare_op=ALU.not_equal, fill=1.0, base=NH * part,
                                         pattern=[[1, NH], [0, P]], channel_multiplier=-1))
            chain(pool.iota(rev_i, pattern=[[-1, E]], base=E, channel_multiplier=0))
            chain(pool.iota(iota_r, pattern=[[1, MP]], base=0, channel_multiplier=0))
            pool.wait_ge(consts, 1)
            chain(pool.iota(tokid, pattern=[[P, NT]], base=0, channel_multiplier=1))
            pool.tensor_copy(ident_b[:, :], ident[:, :]).then_inc(consts, 1)

            pool.wait_ge(norm_done, 2)
            pool.wait_ge(st_zero, 16 * 8)
            pool.wait_ge(slots_done, 1)

            def inputs_to_end(nn, u):
                pool.wait_ge(xdt_done, nn + 1)
                nc.gpsimd.tensor_tensor(by_head(xde[:, u, :]), by_head(xdt[:, u, :]), heads_b2(e_end, nn),
                                        ALU.mult).then_inc(xde_done, 1)

            def prepare_rows(b, j):
                nn, r = b * SC + j, j % R
                if not (is_first(b) and j < R):
                    pool.wait_ge(slots_done, 1)
                    pool.wait_ge(scat[r], 16 * K * (b * 2 + j // R))
                nc.gpsimd.tensor_copy(rows[:, r, :, D:D + 2],
                                      meta[:, tile_ix(nn), :, :].rearrange("p a k v -> p (a k) v")).then_inc(row_done, 1)
                nc.gpsimd.tensor_copy(slot_st[:, r, :],
                                      slot_i[:, tile_ix(nn), :].rearrange("p a k -> p (a k)")).then_inc(row_done, 1)
                pool.wait_ge(xn_done, nn + 1)
                pool.sem_inc(scatters, 1)
                nc.gpsimd.tensor_copy(rows[:, r, 1, 0:D], rows[:, r, 0, 0:D]).then_inc(row_done, 1)
                pool.wait_ge(row_done, 3 * (nn + 1))
                pool.sem_inc(scatters, 1)

            def scatter(r, c):
                nc.gpsimd.indirect_dma_start(
                    out=slots_d, out_offset=bass.IndirectOffsetOnAxis(ap=slot_st[:, r, c:c + 1], axis=0),
                    in_=rows[:, r, c, :], in_offset=None).then_inc(scat[r], 16)

            def sequence(b):
                for j in range(SC):
                    nn = b * SC + j
                    if j:
                        pool.wait_ge(state_done, nn)
                        nc.gpsimd.tensor_tensor(by_head(state_k[:, :]), by_head(state[:, :]),
                                                heads_b2(e_tot, nn), ALU.mult).then_inc(keep_done, 1)
                    prepare_rows(b, j)
                    scatter(j % R, 0)
                    if not (is_last(b) and j == SC - 1):
                        inputs_to_end(nn + 1, (j + 1) % 2)
                    scatter(j % R, 1)

            inputs_to_end(0, 0)
            over_sequences(pool, sequence)

            def moe_scatter(m, r):
                pool.wait_ge(id_done, m * R + r + 1)
                pool.wait_ge(ym_done, m * R + r + 1)
                pool.sem_inc(scatters, 1)
                for c in range(2):
                    nc.gpsimd.indirect_dma_start(
                        out=moe_d, out_offset=bass.IndirectOffsetOnAxis(ap=slot_st[:, r, c:c + 1], axis=0),
                        in_=ym[r][:, c * D:(c + 1) * D], in_offset=None,
                        bounds_check=K * NT * P - 1, oob_is_err=False).then_inc(st_moe[r], 16)

            over_pairs(pool, [(moe_scatter, 0)])

            for k in range(8):
                o = (k % 2) * 3072
                pool.wait_ge(ld_sum[k % 2], 48 * (k // 2 + 1))
                nc.gpsimd.tensor_tensor(act[:, o + 1024:o + 2048], act[:, o + 1024:o + 2048],
                                        act[:, o + 2048:o + 3072], ALU.add).then_inc(moe_sum, 1)

        @block.scalar
        def _(act_e):
            A = nc.scalar.activation
            n = [0]

            def chain(ins):
                n[0] += 1
                ins.then_inc(act_chain, 1)
                act_e.wait_ge(act_chain, n[0])

            act_e.wait_ge(var_done, 1)
            A(t_b, t_a, ACT.Sqrt).then_inc(sq_r1, 1)
            act_e.wait_ge(q_done, 1)
            A(sq2, q_in, ACT.Sqrt).then_inc(sq_q, 1)
            act_e.wait_ge(ld_w, 16 * 12)
            A(a_pos, alog_in, ACT.Exp).then_inc(a_exp, 1)
            A(w_hi[:, :], w_raw, ACT.Copy).then_inc(w_hi_done, 1)
            for i in range(2):
                A(wo_sb[:, i, :], wo_raw[:, i, :], ACT.Copy, scale=rms_c[:, i:i + 1]).then_inc(w_hi_done, 1)

            def group(it):
                for u in range(2):
                    g = it * 2 + u
                    act_e.wait_ge(a_tp, g + 1)
                    if not is_first(it):
                        act_e.wait_ge(a_rt, g - 1)
                        act_e.wait_ge(a_lo, g - 1)
                    A(xt_g[u], bank[u][:, :], ACT.Copy).then_inc(a_xt, 1)
                    A(xwf[u], bank[u][:, :], ACT.Identity, bias=lnb_c, scale=lnw_c).then_inc(a_xw, 1)
                    act_e.wait_ge(sq_q, 1)
                    act_e.wait_ge(a_xw, g + 1)
                    A(xw_hi[:, bass.ds(it * SW + PADW + u * GT, GT)], xwf[u], ACT.Copy).then_inc(a_hi, 1)

            group(0)
            with act_e.Fori(1, NB) as it:
                group(it)

            act_e.wait_ge(dabs, 1)
            A(th[2], th[1], ACT.Exp, scale=-1.0).then_inc(dexp, 1)
            act_e.wait_ge(cs_copied, 2)
            A(e_cs[:, :, :], cs_sb[:, :, :], ACT.Exp).then_inc(e_done, 1)
            A(e_tot[:, :, :], th[5], ACT.Exp).then_inc(e_done, 1)
            act_e.wait_ge(dsub_done, 1)
            A(e_end[:, :, :], th[3], ACT.Exp).then_inc(e_done, 1)
            act_e.wait_ge(gap_done, 1)
            A(te[3], te[1], ACT.Exp).then_inc(gap_exp, 1)
            act_e.wait_ge(top2_done, 1)
            A(tv[4], tv[3], ACT.Exp).then_inc(top2_exp, 1)
            act_e.wait_ge(dp_done, 1)
            A(tv[7], tv[6], ACT.Exp).then_inc(dp_exp, 1)
            act_e.wait_ge(norm_done, 2)
            act_e.wait_ge(st_zero, 16 * 8)
            act_e.wait_ge(slots_done, 1)
            act_e.wait_ge(eid_done, 1)

            def keep_proj(g6, i, par):
                act_e.wait_ge(proj_ps, g6 + i + 1)
                t = ORDER[i]
                A(proj[:, t, HALO:] if t < NCT else group_act(par)[:, t, :], bank[0][:, :], ACT.Copy)\
                    .then_inc(proj_done, 1)

            def tap0(g6, i, par):
                act_e.wait_ge(proj_done, g6 + i + 1)
                t = ORDER[i]
                A(group_act(par)[:, t, :], proj[:, t, HALO:], ACT.Identity, bias=cb_c[:, t:t + 1],
                  scale=taps[:, t, HALO:]).then_inc(tap0_done, 1)

            def halo(g, par):
                src = proj[:, :, GT:] if par else xw_hi[:, 0:HALO].bitcast(F32).unsqueeze(1).broadcast_to([P, NCT, HALO])
                A(proj[:, :, 0:HALO], src, ACT.Copy).then_inc(halo_done, 1)
                act_e.wait_ge(halo_done, g + 1)

            def silu(g, par):
                act_e.wait_ge(taps_done, (g + 1) * NCT * HALO)
                act_e.wait_ge(proj_done, (g + 1) * NAT)
                conv, gate = (act[:, (par * NAT + t) * GT:(par * NAT + t + n) * GT]
                              for t, n in ((0, NCT), (NCT, NAT - NCT)))
                A(conv, conv, ACT.Silu).then_inc(silu_done, 1)
                A(gate, gate, ACT.Silu).then_inc(gate_silu, 1)

            def decays(nn, u):
                act_e.wait_ge(dd_done, nn + 1)
                A(l_sb[:, u, :], bank[2][:, :], ACT.Exp).then_inc(l_done, 1)

            halo(0, 0)
            for i in range(NAT):
                keep_proj(0, i, 0)
                if i < NCT:
                    tap0(0, i, 0)
            silu(0, 0)
            decays(0, 0)

            def row(nn, r, uses):
                act_e.wait_ge(norm_done, 2)
                if uses is not None:
                    act_e.wait_ge(scat[r], 16 * K * uses)
                t = tile_ix(nn)
                A(rows[:, r, 0, 0:D], x_sb[:, t, :].rearrange("p a d -> p (a d)"), ACT.Identity,
                  bias=nmr1[:, t], scale=r1[:, t]).then_inc(xn_done, 1)

            def keep_out(nn):
                act_e.wait_ge(norm_done, 2)
                act_e.wait_ge(o_done, nn + 1)
                act_e.wait_ge(xn_done, nn + 1)
                A(x_sb[:, tile_ix(nn), :].rearrange("p a d -> p (a d)"), bank[7][:, 0:D], ACT.Copy)
                A(ssq[:, tile_ix(nn)], bank[7][:, D:D + 1], ACT.Copy).then_inc(o_kept, 1)

            def square(nn, u):
                act_e.wait_ge(gate_done, nn + 1)
                A(sq[:, u, :], yg[:, u, :], ACT.Square).then_inc(sq_done, 1)

            def sequence(b):
                first, last = is_first(b), is_last(b)
                for j in range(SC):
                    nn, q, g = b * SC + j, j % GC, j // GC
                    more = not (last and g == 1)
                    nxt, g6 = b * 2 + g + 1, (b * 2 + g + 1) * NAT
                    if not (first and j < 4):
                        keep_out(nn - 4)
                    if not (last and j == SC - 1):
                        decays(nn + 1, (j + 1) % 2)
                    if more and q == 0:
                        halo(nxt, 1 - g)
                    if more and q < 3:
                        keep_proj(g6, 2 * q, 1 - g)
                    if more and q == 0:
                        tap0(g6, 0, 1 - g)
                    if more and q == 3:
                        silu(nxt, 1 - g)
                    if not (first and j < 2):
                        square(nn - 2, j % 2)
                    if more and q == 1:
                        tap0(g6, 2, 1 - g)
                    row(nn, j % R, None if first and j < R else b * 2 + j // R)
                    if more and q < 3:
                        keep_proj(g6, 2 * q + 1, 1 - g)
                    if more and q < 2:
                        tap0(g6, 2 * q + 1, 1 - g)

            over_sequences(act_e, sequence)
            keep_out(NT - 4)
            keep_out(NT - 3)
            for n_ in (NT - 2, NT - 1):
                square(n_, n_ % 2)
            for n_ in (NT - 2, NT - 1):
                keep_out(n_)
            act_e.wait_ge(ms_done, 1)
            A(t_b, t_a, ACT.Sqrt).then_inc(rms_sq, 1)

            def silu_pair(m, r):
                act_e.wait_ge(gu_done, m * R + r + 1)
                for c in range(2):
                    a = A(l_sb[:, r % 2, c * F:(c + 1) * F], bank[2 + 2 * (r % 2) + c][:, 0:F], ACT.Silu)
                a.then_inc(silu_m, 1)

            def hidden_keep(m, r):
                act_e.wait_ge(ht_done, m * R + r + 1)
                A(ht[r % 2], bank[6 + r % 2][:, :], ACT.Copy).then_inc(hts_done, 1)

            over_pairs(act_e, [(silu_pair, 1), (hidden_keep, 2)])

            act_e.wait_ge(rms_done, 1)
            for k in range(8):
                act_e.wait_ge(ld_sum[k % 2], 48 * (k // 2 + 1))
                for i in range(8):
                    t, o = 8 * k + i, (k % 2) * 3072 + i * D
                    A(act[:, o:o + D], act[:, o:o + D], ACT.Identity, bias=nmr1[:, t:t + 1],
                      scale=r12[:, t:t + 1]).then_inc(resid_done, 1)

        @block.tensor
        def _(pe):
            mm = nc.tensor.matmul
            pe.wait_ge(lnb_done, 1)
            mm(bank[7][:, 0:NH], lnb_b[:, :], wdt_sb[:, :], start=True, stop=True).then_inc(dtb_ps, 1)
            pe.wait_ge(wdt_done, 1)
            pe.wait_ge(consts, 2)

            def group(it):
                for u in range(2):
                    g = it * 2 + u
                    for i in range(4):
                        pe.wait_ge(a_xn, g * 4 + i + 1)
                        if i == 0 and not is_first(it):
                            pe.wait_ge(a_xt, g - 1)
                            pe.wait_ge(a_xw, g - 1)
                        tp = nc.tensor.transpose(bank[u][:, i * P:(i + 1) * P], xn2[u][:, i * P:(i + 1) * P], ident[:, :])
                    tp.then_inc(a_tp, 1)
                    pe.wait_ge(a_xt, g + 1)
                    if not is_first(it):
                        pe.wait_ge(a_rs, g - 1)
                    for i in range(4):
                        rt = mm(bank[4 + u][:, i * ROUTE:(i + 1) * ROUTE], xt_g[u][:, i * P:(i + 1) * P], rdt_w[:, :],
                                start=True, stop=True)
                    rt.then_inc(a_rt, 1)

            group(0)
            with pe.Fori(1, NB) as it:
                group(it)

            pe.wait_ge(adt_done, 1)
            adt = th[4].rearrange("p t h -> p (t h)")
            mm(bank[7][:, 0:256], upper[:, :], adt, start=True, stop=True)
            mm(bank[7][:, 256:512], ones[:, :], adt, start=True, stop=True).then_inc(cs_ps, 1)
            pe.wait_ge(cs_copied, 2)
            csf = cs_sb[:, :, :].rearrange("p t h -> p (t h)")
            nc.tensor.transpose(bank[6][:, 0:P], csf[:, 0:P], ident[:, :])
            nc.tensor.transpose(bank[6][:, P:2 * P], csf[:, P:2 * P], ident[:, :]).then_inc(csT_ps, 1)
            pe.wait_ge(oh_done, 1)
            ohf = oh_b.rearrange("p t e -> p (t e)")
            mm(bank[4][:, :], strict_b[:, :], ohf, start=True, stop=True)
            mm(bank[5][:, :], ones_b[:, :], ohf, start=True, stop=True).then_inc(rank_ps, 1)

            pe.wait_ge(wdve_done, 1)
            pe.wait_ge(w_hi_done, 3)
            for done in (a_hi, a_xt, a_xw, a_rs):
                pe.wait_ge(done, NG)
            pe.wait_ge(a_lo, NG)

            def project(b, half, g6, i):
                if not (isinstance(g6, int) and g6 + i < 1):
                    pe.wait_ge(proj_done, g6 + i)
                t = ORDER[i]
                c = slice(DI + t * P, DI + (t + 1) * P) if t < NCT else slice((t - NCT) * P, (t - NCT + 1) * P)
                for a, (w, v) in enumerate(((w_hi, xw_hi), (w_hi, xw_lo), (w_lo, xw_hi))):
                    m = mm(bank[0][:, :], w[:, c], v[:, bass.ds(b * SW + PADW + half * GT, GT)], start=(a == 0),
                           stop=(a == 2))
                m.then_inc(proj_ps, 1)

            def exponents(b, j):
                nn, pr, o = b * SC + j, (j // 2) % 2, j % 2
                pe.wait_ge(ld_dd[pr], 32 * (b * 2 + j // 4 + 1))
                if not (is_first(b) and j < 1):
                    pe.wait_ge(l_done, nn)
                mm(bank[2][:, :], dd_l[:, pr, o, :], dd_r[:, pr, o * NH * P:(o + 1) * NH * P], start=True, stop=False)
                mm(bank[2][:, :], ident_b[:, :], mask_b[:, :].unsqueeze(1).broadcast_to([P, NH, P]),
                   start=False, stop=True).then_inc(dd_done, 1)

            def front(b, j):
                if j % GC == 0:
                    pe.wait_ge(silu_done, b * 2 + j // GC + 1)
                ab, cs, fb = group_act(j // GC), in_group(j), bank[3 + j % 2]
                mm(fb[:, 0:P], ab[:, BT, cs], ab[:, CT, cs], start=True, stop=True)
                for i, t in enumerate((XT0, XT0 + 1, BT)):
                    tp = nc.tensor.transpose(fb[:, (i + 1) * P:(i + 2) * P], ab[:, t, cs], ident[:, :])
                tp.then_inc(front_done, 1)

            def middle(b, j):
                nn, u = b * SC + j, j % 2
                if is_first(b) and j < 1:
                    pe.wait_ge(m_done, 1)
                else:
                    pe.wait_ge(y_done, nn)
                pe.wait_ge(xde_done, nn + 1)
                for h in range(NH):
                    mm(bank[5][:, h * HD:(h + 1) * HD], m_sb[:, u, h * P:(h + 1) * P],
                       xdt[:, u, h * HD:(h + 1) * HD], start=True, stop=True)
                if j:
                    mm(bank[5][:, DI:2 * DI], group_act(j // GC)[:, CT, in_group(j)], state[:, :], start=True, stop=True)
                mm(bank[6][:, 0:DI], b_sb[:, u, :], xde[:, u, :], start=True, stop=True).then_inc(mid_done, 1)

            def turn_y(nn, u, early):
                pe.wait_ge(y_done, nn + 1)
                if not early:
                    pe.wait_ge(skip_done, nn)
                for c in range(2):
                    tp = nc.tensor.transpose(bank[1][:, c * P:(c + 1) * P], y_sb[:, u, c * P:(c + 1) * P], ident[:, :])
                tp.then_inc(yt_done, 1)

            def project_out(nn, u, early):
                pe.wait_ge(sq_done, nn + 1)
                if not early:
                    pe.wait_ge(o_kept, nn)
                for c in range(2):
                    mm(bank[7][:, 0:D], yg[:, u, c * P:(c + 1) * P], wo_sb[:, c, :], start=(c == 0), stop=(c == 1))
                for c in range(2):
                    m = mm(bank[7][:, D:D + 1], sq[:, u, c * P:(c + 1) * P], ones[:, 0:1], start=(c == 0),
                           stop=(c == 1))
                m.then_inc(o_done, 1)

            pe.wait_ge(e_done, 2)
            pe.wait_ge(csp_done, 4)
            for i in range(NAT):
                project(0, 0, 0, i)
            exponents(0, 0)
            front(0, 0)

            def sequence(b):
                first, last = is_first(b), is_last(b)
                for j in range(SC):
                    nn, q, g = b * SC + j, j % GC, j // GC
                    ahead = not (last and j == SC - 1)
                    more = not (last and g == 1) and q < 3
                    nxt = (b if g == 0 else b + 1), 1 - g, (b * 2 + g + 1) * NAT
                    if ahead:
                        exponents(b, j + 1)
                    if ahead and q < 3:
                        front(b, j + 1)
                    if more:
                        project(*nxt, 2 * q)
                    if not (first and j < 3):
                        project_out(nn - 3, (j - 3) % 2, first and j < 4)
                    middle(b, j)
                    if not (first and j < 1):
                        turn_y(nn - 1, (j - 1) % 2, first and j < 2)
                    if more:
                        project(*nxt, 2 * q + 1)
                    if ahead and q == 3:
                        front(b, j + 1)

            over_sequences(pe, sequence)
            project_out(NT - 3, (NT - 3) % 2, False)
            turn_y(NT - 1, (NT - 1) % 2, False)
            project_out(NT - 2, (NT - 2) % 2, False)
            project_out(NT - 1, (NT - 1) % 2, False)
            pe.wait_ge(o_kept, NT)
            pe.wait_ge(ld_moe_w, 48)

            def expert(m, r):
                return pe.value_load(eid[0:1, bass.ds(m * R + r, 1)], min_val=0, max_val=E - 1)

            def gate_up(m, r):
                ex = expert(m, r)
                pe.wait_ge(xts_done, m * R + r + 1)
                for c in range(2):
                    gu = mm(bank[2 + 2 * (r % 2) + c][:, :], xdt[:, r % 2, c * P:(c + 1) * P],
                            gu_sb[:, bass.ds(ex * (2 * F), 2 * F)], start=True, stop=True)
                gu.then_inc(gu_done, 1)

            def turn_x(m, r):
                pe.wait_ge(ld_slot[r], 16 * (m + 1))
                for c in range(2):
                    tp = nc.tensor.transpose(bank[0][:, c * P:(c + 1) * P], rows[:, r, c, 0:D], ident[:, :])
                tp.then_inc(xt_done, 1)

            def turn_h(m, r):
                pe.wait_ge(h_done, m * R + r + 1)
                for i in range(4):
                    tp = nc.tensor.transpose(bank[6 + r % 2][:, i * P:(i + 1) * P], m_sb[:, r % 2, i * P:(i + 1) * P],
                                             ident[:, :])
                tp.then_inc(ht_done, 1)

            def down(m, r):
                ex = expert(m, r)
                pe.wait_ge(hts_done, m * R + r + 1)
                if not (is_first(m) and r < 1):
                    pe.wait_ge(ym_done, m * R + r)
                for c in range(2):
                    for f in range(2):
                        o = mm(bank[1][:, c * D:(c + 1) * D], ht[r % 2][:, (2 * c + f) * P:(2 * c + f + 1) * P],
                               dn_sb[:, bass.ds(ex * (2 * D) + f * D, D)], start=(f == 0), stop=(f == 1))
                o.then_inc(out_done, 1)

            over_pairs(pe, [(gate_up, 1), (turn_x, 0), (turn_h, 2), (down, 3)])

        @block.vector
        def _(dve):
            V = nc.vector
            n = [0]

            def chain(ins):
                n[0] += 1
                ins.then_inc(dve_chain, 1)
                dve.wait_ge(dve_chain, n[0])

            for t in (xw_hi, xw_lo):
                V.memset(t[:, :].rearrange("p (b s) -> p b s", b=NB)[:, :, 0:PADW].bitcast(F32), 0.0)
            V.memset(dd_l[:, :, :, :].bitcast(F32), 1.0)
            for t in range(NT):
                if t % 8 == 0:
                    dve.wait_ge(ld_x[t // 8], 16)
                st = V.bn_stats(stats[:, t, :], x_sb[:, t, :])
            chain(st)
            me, mo, ve, vo = (stats[:, :, i] for i in (1, 4, 2, 5))
            chain(V.tensor_tensor(mean, me, mo, ALU.add))
            chain(V.tensor_scalar(nm, mean, -0.5, None, ALU.mult))
            chain(V.tensor_tensor(t_a, me, mo, ALU.subtract))
            chain(V.tensor_tensor(t_a, t_a, t_a, ALU.mult))
            chain(V.tensor_tensor(var, ve, vo, ALU.add))
            chain(V.scalar_tensor_tensor(out=var, in0=t_a, scalar=float(D // 4), in1=var, op0=ALU.mult, op1=ALU.add))
            chain(V.tensor_scalar(var, var, 1.0 / D, None, ALU.mult))
            V.tensor_scalar(t_a, var, EPS, None, ALU.add).then_inc(var_done, 1)
            dve.wait_ge(sq_r1, 1)
            chain(V.reciprocal(r1, t_b))
            chain(V.tensor_tensor(t_b, r1, r1, ALU.mult))
            chain(V.tensor_tensor(t_b, t_b, var, ALU.mult))
            V.tensor_scalar(q_in, t_b, EPS, None, ALU.add).then_inc(q_done, 1)
            dve.wait_ge(sq_q, 1)
            chain(V.reciprocal(r12, sq2))
            V.tensor_tensor(nmr1, nm, r1, ALU.mult).then_inc(norm_done, 1)
            V.tensor_tensor(r12, r12, r1, ALU.mult).then_inc(norm_done, 1)
            dve.wait_ge(norm_done, 2)

            dve.wait_ge(ld_w, 16 * 12)
            chain(V.memset(lnb_b[:, :], 1.0))
            V.tensor_scalar(lnb_b[:, :], lnb_b[:, :], lnb_c, None, ALU.mult).then_inc(lnb_done, 1)
            V.tensor_scalar(rdt_w[:, E:ROUTE], wdt_sb[:, :], lnw_c, None, ALU.mult).then_inc(wdt_done, 1)
            dve.wait_ge(a_exp, 1)
            chain(V.tensor_scalar(a_neg, a_pos, -1.0, None, ALU.mult))
            dve.wait_ge(dtb_ps, 1)
            chain(V.tensor_tensor(dtb, dtb_in, bank[7][:, 0:NH], ALU.add))
            dve.wait_ge(w_hi_done, 3)
            chain(V.tensor_tensor(w_lo[:, :], w_raw, w_hi[:, :].bitcast(F32), ALU.subtract))
            dve.wait_ge(consts, 2)
            for i in range(2):
                for a in range(2):
                    last = V.tensor_copy(dd_r[0:8, i, a * NH * P:(a + 1) * NH * P], ddr0[0:8, :])
            last.then_inc(wdve_done, 1)
            V.tensor_copy(rev, rev_i)
            V.tensor_copy(iota_f, iota_r)
            V.tensor_copy(meta[:, :, 0, 0], tokid)
            chain(V.tensor_copy(meta[:, :, 1, 0], tokid))
            chain(V.tensor_scalar(meta[:, :, 1, 0], meta[:, :, 1, 0], float(NT * P), None, ALU.add))

            def norm_group(it, u):
                g = it * 2 + u
                if not is_first(it):
                    dve.wait_ge(a_tp, g - 1)
                for i in range(4):
                    t = bass.ds(it * 8 + u * 4 + i, 1)
                    V.tensor_scalar(xn2[u][:, i * P:(i + 1) * P], x_sb[:, t, :].rearrange("p a d -> p (a d)"),
                                    nm[:, t], r12[:, t], ALU.add, ALU.mult).then_inc(a_xn, 1)

            def low_part(it, u):
                g = it * 2 + u
                dve.wait_ge(a_hi, g + 1)
                c = bass.ds(it * SW + PADW + u * GT, GT)
                V.tensor_tensor(xw_lo[:, c], xwf[u], xw_hi[:, c].bitcast(F32), ALU.subtract).then_inc(a_lo, 1)
                dve.wait_ge(a_rt, g + 1)
                V.tensor_copy(route_sb[:, bass.ds(g * 4, 4), :],
                              bank[4 + u][:, 0:4 * ROUTE].rearrange("p (t c) -> p t c", c=ROUTE)).then_inc(a_rs, 1)

            norm_group(0, 0)
            norm_group(0, 1)
            with dve.Fori(1, NB) as it:
                for u in range(2):
                    low_part(it - 1, u)
                    norm_group(it, u)
            low_part(NB - 1, 0)
            low_part(NB - 1, 1)
            dve.wait_ge(a_rs, NG)

            def over_tok(c):
                return c.unsqueeze(1).broadcast_to([P, NT, NH])

            chain(V.tensor_tensor(th[0], route_sb[:, :, E:ROUTE], over_tok(dtb), ALU.add))
            V.scalar_tensor_tensor(out=th[1], in0=th[0], scalar=-1.0, in1=th[0], op0=ALU.mult, op1=ALU.max)\
                .then_inc(dabs, 1)
            dve.wait_ge(dexp, 1)
            chain(V.tensor_scalar(th[3], th[2], 2.0, None, ALU.add))
            chain(V.reciprocal(th[3], th[3]))
            chain(V.tensor_tensor(th[2], th[2], th[3], ALU.mult))
            chain(V.tensor_tensor(th[3], th[2], th[2], ALU.mult))
            chain(V.tensor_scalar(th[5], th[3], 1.0 / 17, None, ALU.mult))
            for c in (15, 13, 11, 9, 7, 5, 3):
                chain(V.scalar_tensor_tensor(out=th[5], in0=th[5], scalar=1.0 / c, in1=th[3], op0=ALU.add,
                                             op1=ALU.mult))
            chain(V.scalar_tensor_tensor(out=th[5], in0=th[5], scalar=1.0, in1=th[2], op0=ALU.add, op1=ALU.mult))
            chain(V.tensor_scalar(th[0], th[0], 0.0, None, ALU.max))
            chain(V.scalar_tensor_tensor(out=dts[:, :, :], in0=th[5], scalar=2.0, in1=th[0], op0=ALU.mult,
                                         op1=ALU.add))
            V.tensor_tensor(th[4], dts[:, :, :], over_tok(a_neg), ALU.mult).then_inc(adt_done, 1)
            dve.wait_ge(cs_ps, 1)
            V.tensor_copy(cs_sb[:, :, :], bank[7][:, 0:256].rearrange("p (t h) -> p t h", h=NH))\
                .then_inc(cs_copied, 1)
            V.tensor_copy(th[5], bank[7][:, 256:512].rearrange("p (t h) -> p t h", h=NH)).then_inc(cs_copied, 1)
            dve.wait_ge(cs_copied, 2)
            chain(V.tensor_tensor(th[3], th[5], cs_sb[:, :, :], ALU.subtract))
            V.tensor_scalar(th[3], th[3], 0.0, None, ALU.min).then_inc(dsub_done, 1)
            dve.wait_ge(csT_ps, 1)
            tp = bank[6][:, 0:2 * P].rearrange("p (k l) -> p k l", k=2)
            hi, lo, nhi, nlo = (csp[:, i, :, :] for i in range(4))
            V.tensor_copy(hi, tp).then_inc(csp_done, 1)
            dve.wait_ge(csp_done, 1)
            V.tensor_tensor(lo, tp, hi.bitcast(F32), ALU.subtract).then_inc(csp_done, 1)
            dve.wait_ge(csp_done, 2)
            V.tensor_scalar(nhi, hi.bitcast(F32), -1.0, None, ALU.mult).then_inc(csp_done, 1)
            V.tensor_scalar(nlo, lo.bitcast(F32), -1.0, None, ALU.mult).then_inc(csp_done, 1)

            def over_e(c):
                return c.unsqueeze(2).broadcast_to([P, NT, E])

            def over_t(c):
                return c.unsqueeze(1).broadcast_to([P, NT, E])

            lg, gap, pick, ex, oh0, gap2, oh1, pos, cnt = te
            chain(V.tensor_tensor(lg, route_sb[:, :, 0:E], over_e(sq2), ALU.mult))
            chain(V.tensor_reduce(tv[0], lg, AX, ALU.max))
            chain(V.tensor_tensor(gap, lg, over_e(tv[0]), ALU.subtract))
            V.tensor_scalar(gap, gap, EXP_FLOOR, None, ALU.max).then_inc(gap_done, 1)
            dve.wait_ge(gap_done, 1)
            chain(V.scalar_tensor_tensor(out=pick, in0=gap, scalar=0.0, in1=over_t(rev), op0=ALU.is_ge,
                                         op1=ALU.mult))
            chain(V.tensor_reduce(tv[1], pick, AX, ALU.max))
            chain(V.tensor_tensor(oh0, pick, over_e(tv[1]), ALU.is_equal))
            chain(V.scalar_tensor_tensor(out=gap2, in0=oh0, scalar=-1.0e4, in1=gap, op0=ALU.mult, op1=ALU.add))
            V.tensor_reduce(tv[3], gap2, AX, ALU.max).then_inc(top2_done, 1)
            dve.wait_ge(top2_done, 1)
            chain(V.tensor_tensor(pick, gap2, over_e(tv[3]), ALU.is_equal))
            chain(V.tensor_tensor(pick, pick, over_t(rev), ALU.mult))
            chain(V.tensor_reduce(tv[1], pick, AX, ALU.max))
            chain(V.tensor_tensor(oh1, pick, over_e(tv[1]), ALU.is_equal))
            V.tensor_tensor(oh_b, oh0, oh1, ALU.add).then_inc(oh_done, 1)
            dve.wait_ge(gap_exp, 1)
            chain(V.tensor_reduce(tv[0], ex, AX, ALU.add))
            chain(V.reciprocal(tv[5], tv[0]))
            dve.wait_ge(top2_exp, 1)
            chain(V.tensor_tensor(tv[6], tv[4], tv[5], ALU.mult))
            V.tensor_tensor(tv[6], tv[6], tv[5], ALU.subtract).then_inc(dp_done, 1)
            dve.wait_ge(rank_ps, 1)
            chain(V.tensor_copy(cnt, bank[5][:, :].rearrange("p (t e) -> p t e", e=E)))
            src, spare = cnt, [lg, gap2]
            step, turn = 1, 0
            while step < NT:
                dst = spare[turn % 2]
                V.tensor_copy(dst[:, 0:step, :], src[:, 0:step, :])
                chain(V.tensor_tensor(dst[:, step:, :], src[:, step:, :], src[:, 0:NT - step, :], ALU.add))
                src, step, turn = dst, 2 * step, turn + 1
            incl = src
            chain(V.tensor_tensor(pos, incl, bank[4][:, :].rearrange("p (t e) -> p t e", e=E), ALU.add))
            chain(V.tensor_tensor(pos, pos, cnt, ALU.subtract))
            chain(V.tensor_scalar(cnt_i, incl[:, NT - 1, :], float(PS - 1), None, ALU.add))
            chain(V.tensor_scalar(cnt_i, cnt_i, PS.bit_length() - 1, None, ALU.arith_shift_right))
            chain(V.tensor_copy(ntl, cnt_i))
            chain(V.memset(base, 0.0))
            for e in range(1, E):
                chain(V.tensor_tensor(base[:, e:e + 1], base[:, e - 1:e], ntl[:, e - 1:e], ALU.add))
            chain(V.tensor_scalar(base_s, base, float(PS), None, ALU.mult))
            chain(V.tensor_tensor(pos, pos, over_t(base_s), ALU.add))
            for c, oh in enumerate((oh0, oh1)):
                chain(V.tensor_tensor(pick, oh, pos, ALU.mult))
                chain(V.tensor_reduce(tv[8], pick, AX, ALU.add))
                chain(V.tensor_copy(slot_i[:, :, c], tv[8]))
            dve.wait_ge(dp_exp, 1)
            chain(V.tensor_scalar(tv[8], tv[7], 1.0, None, ALU.add))
            chain(V.reciprocal(tv[9], tv[8]))
            chain(V.tensor_tensor(meta[:, :, 1, 1], tv[7], tv[9], ALU.mult))
            V.tensor_copy(meta[:, :, 0, 1], tv[9]).then_inc(slots_done, 1)
            chain(V.memset(eid_f[0:1, :], 0.0))
            for e in range(1, E):
                chain(V.scalar_tensor_tensor(out=eid_f[0:1, :], in0=iota_f[0:1, :], scalar=base[0:1, e:e + 1],
                                             in1=eid_f[0:1, :], op0=ALU.is_ge, op1=ALU.add))
            V.tensor_copy(eid[:, :], eid_f[0:1, :]).then_inc(eid_done, 1)

            dve.wait_ge(e_done, 3)

            def other_taps(g, par, lo, hi):
                for n_ in range(lo, hi):
                    i, k = divmod(n_, HALO)
                    t = ORDER[i]
                    if k:
                        dve.wait_ge(taps_done, g * NCT * HALO + n_)
                    else:
                        dve.wait_ge(tap0_done, g * NCT + i + 1)
                    V.scalar_tensor_tensor(out=group_act(par)[:, t, :], in0=proj[:, t, k:k + GT],
                                           scalar=taps[:, t, k:k + 1], in1=group_act(par)[:, t, :],
                                           op0=ALU.mult, op1=ALU.add).then_inc(taps_done, 1)

            def by_token(b, j, fill):
                nn, u = b * SC + j, j % 2
                fb = bank[3 + u]
                dve.wait_ge(front_done, nn + 1)
                V.tensor_tensor(by_head(xdt[:, u, :]), by_head(fb[:, P:P + DI]), heads_b2(dts, nn),
                                ALU.mult).then_inc(xdt_done, 1)
                V.tensor_copy(b_sb[:, u, :], fb[:, 3 * P:4 * P]).then_inc(b_done, 1)
                fill()
                dve.wait_ge(l_done, nn + 1)
                V.tensor_tensor(m_sb[:, u, :].rearrange("p (h l) -> p h l", h=NH),
                                l_sb[:, u, :].rearrange("p (h l) -> p h l", h=NH),
                                fb[:, 0:P].unsqueeze(1).broadcast_to([P, NH, P]), ALU.mult).then_inc(m_done, 1)

            def outputs(b, j):
                nn, u, later = b * SC + j, j % 2, b * (SC - 1) + j
                dve.wait_ge(mid_done, nn + 1)
                if j:
                    if not (is_first(b) and j == 1):
                        dve.wait_ge(y_done, nn)
                    V.tensor_tensor(by_head(yo_sb[:, :]), by_head(bank[5][:, DI:2 * DI]), heads_b2(e_cs, nn),
                                    ALU.mult).then_inc(yo_done, 1)
                    dve.wait_ge(keep_done, later)
                    V.tensor_tensor(state[:, :], state_k[:, :], bank[6][:, 0:DI], ALU.add).then_inc(state_done, 1)
                    dve.wait_ge(yo_done, later)
                    V.tensor_tensor(y_sb[:, u, :], yo_sb[:, :], bank[5][:, 0:DI], ALU.add).then_inc(y_done, 1)
                else:
                    V.tensor_copy(state[:, :], bank[6][:, 0:DI]).then_inc(state_done, 1)
                    V.tensor_copy(y_sb[:, u, :], bank[5][:, 0:DI]).then_inc(y_done, 1)

            def skip(nn, j):
                ab, cs = group_act(j // GC), in_group(j)
                dve.wait_ge(yt_done, nn + 1)
                if not (isinstance(nn, int) and nn < 1):
                    dve.wait_ge(gate_done, nn)
                for c in range(2):
                    sk = V.scalar_tensor_tensor(out=yd_sb[:, c * P:(c + 1) * P], in0=ab[:, XT0 + c, cs],
                                                scalar=ds_c[:, c:c + 1], in1=bank[1][:, c * P:(c + 1) * P],
                                                op0=ALU.mult, op1=ALU.add)
                sk.then_inc(skip_done, 1)

            def gate(nn, j, group):
                ab, cs, u = group_act(j // GC), in_group(j), j % 2
                dve.wait_ge(skip_done, nn + 1)
                if j % GC == 0:
                    dve.wait_ge(gate_silu, group + 1)
                V.tensor_tensor(yg[:, u, :].rearrange("p (c l) -> p c l", c=2),
                                yd_sb[:, :].rearrange("p (c l) -> p c l", c=2), ab[:, ZT0:ZT0 + 2, cs],
                                ALU.mult).then_inc(gate_done, 1)

            FILL = (((0, 0), (0, 0), (0, 1), (1, 3)),
                    ((3, 4), (4, 5), (5, 6), (6, 7)),
                    ((7, 8), (8, 9), (9, 10), (10, 12)),
                    ((0, 0),) * 4)

            other_taps(0, 0, 0, NCT * HALO)
            by_token(0, 0, lambda: None)

            def sequence(b):
                first, last = is_first(b), is_last(b)
                for j in range(SC):
                    nn, q, g = b * SC + j, j % GC, j // GC

                    def fill(place):
                        if not (last and g == 1):
                            other_taps(b * 2 + g + 1, 1 - g, *FILL[q][place])

                    if j:
                        outputs(b, j - 1)
                    elif not first:
                        outputs(b - 1, SC - 1)
                    if not (first and j < 2):
                        skip(nn - 2, (j - 2) % SC)
                    fill(0)
                    if not (first and j < 2):
                        gate(nn - 2, (j - 2) % SC, b * 2 + (j - 2) // GC)
                    fill(1)
                    if not (last and j == SC - 1):
                        by_token(b, j + 1, lambda: fill(2))
                    fill(3)

            over_sequences(dve, sequence)
            outputs(NB - 1, SC - 1)
            for n_ in (NT - 2, NT - 1):
                skip(n_, n_ % SC)
                gate(n_, n_ % SC, NG - 1)
            dve.wait_ge(o_kept, NT)
            V.tensor_scalar(t_a, ssq, 1.0 / DI, EPS, ALU.mult, ALU.add).then_inc(ms_done, 1)
            dve.wait_ge(rms_sq, 1)
            chain(V.reciprocal(var, t_b))
            V.tensor_scalar(r12, r1, 1.0, None, ALU.add).then_inc(rms_done, 1)
            for r in range(R):
                dve.wait_ge(scat[r], 16 * K * NT // R)

            def x_keep(m, r):
                dve.wait_ge(xt_done, m * R + r + 1)
                V.tensor_copy(xdt[:, r % 2, :], bank[0][:, 0:PS]).then_inc(xts_done, 1)

            def destination(m, r):
                if not is_first(m):
                    dve.wait_ge(st_moe[r], 16 * 2 * m)
                V.tensor_copy(slot_st[:, r, :], rows[:, r, :, D]).then_inc(id_done, 1)

            def hidden(m, r):
                dve.wait_ge(silu_m, m * R + r + 1)
                for c in range(2):
                    h = V.scalar_tensor_tensor(out=m_sb[:, r % 2, c * F:(c + 1) * F],
                                               in0=l_sb[:, r % 2, c * F:(c + 1) * F],
                                               scalar=rows[:, r, c, D + 1:D + 2],
                                               in1=bank[2 + 2 * (r % 2) + c][:, F:2 * F], op0=ALU.mult, op1=ALU.mult)
                h.then_inc(h_done, 1)

            def y_keep(m, r):
                dve.wait_ge(out_done, m * R + r + 1)
                V.tensor_copy(ym[r], bank[1][:, 0:2 * D]).then_inc(ym_done, 1)

            over_pairs(dve, [(y_keep, 4), (x_keep, 0), (hidden, 1), (destination, 1)])

            for k in range(8):
                o = (k % 2) * 3072
                for i in range(8):
                    t = 8 * k + i
                    dve.wait_ge(resid_done, t + 1)
                    V.scalar_tensor_tensor(out=act[:, o + i * D:o + (i + 1) * D], in0=x_sb[:, t, :],
                                           scalar=var[:, t:t + 1], in1=act[:, o + i * D:o + (i + 1) * D],
                                           op0=ALU.mult, op1=ALU.add).then_inc(part_done, 1)
                dve.wait_ge(part_done, 8 * (k + 1))
                dve.wait_ge(moe_sum, k + 1)
                V.tensor_tensor(act[:, o:o + 1024], act[:, o:o + 1024], act[:, o + 1024:o + 2048], ALU.add)\
                    .then_inc(total_done, 1)


def kernel(**inputs):
    import numpy as np
    import concourse.bacc as bacc
    from concourse.bass_utils import run_bass_kernel_spmd

    a = {k.removeprefix("L0_"): np.asarray(v) for k, v in inputs.items()}
    xi = a["attn_x"]
    w_in = a["attn_W_in"]
    arrays = {
        "x": xi.reshape(NT, P, D).transpose(1, 0, 2),
        "ln_w": a["attn_ln_w"].reshape(D, 1),
        "ln_b": a["attn_ln_b"].reshape(D, 1),
        "w_in_t": w_in[:DI + CONV].T,
        "w_dt": w_in[DI + CONV:].T,
        "conv_w": a["attn_conv_w"].reshape(NCT, P, TAPS).transpose(1, 0, 2),
        "conv_b": a["attn_conv_b"].reshape(NCT, P).T,
        "dt_bias": a["attn_dt_bias"].reshape(1, NH),
        "a_log": a["attn_A_log"].reshape(1, NH),
        "d_skip": np.repeat(a["attn_D"], HD).reshape(2, P).T,
        "rms_w": a["attn_rms_w"].reshape(2, P).T,
        "w_out_t": a["attn_W_out"].T.reshape(2, P, D).transpose(1, 0, 2),
        "router": a["ffn_kernel_router_DE"],
        "gate_w": a["ffn_kernel_gating_EDF"],
        "up_w": a["ffn_kernel_up_EDF"],
        "down_w": a["ffn_kernel_down_EFD"],
    }
    nc = bacc.Bacc("TRN2", target_bir_lowering=False, num_devices=1)
    feeds, args = {}, []
    for name, v in arrays.items():
        v = np.ascontiguousarray(v)
        feeds[f"in_{name}"] = v
        args.append(nc.dram_tensor(f"in_{name}", v.shape, mybir.dt.from_np(v.dtype), kind="ExternalInput").ap())
    args.append(nc.dram_tensor("out_0", (P, NT, D), F32, kind="ExternalOutput").ap())
    program(nc, *args)
    r = run_bass_kernel_spmd(nc, [feeds], core_ids=[0])
    got = r.results[0]["out_0"]
    return np.ascontiguousarray(got.transpose(1, 0, 2)).reshape(NB, SEQ, D)
```

```python
from contextlib import ExitStack

import concourse.bass as bass
from concourse import mybir

F32 = mybir.dt.float32
F32R = mybir.dt.float32r
BF16 = mybir.dt.bfloat16
I32 = mybir.dt.int32
ALU = mybir.AluOpType
ACT = mybir.ActivationFunctionType
AX = mybir.AxisListType.X

P = 128
NB, SEQ, D = 8, 1024, 128
NT = NB * SEQ // P
NH, HD = 4, 64
DI = NH * HD
NS = 128
CONV = DI + 2 * NS
TAPS = 4
PADW = 4
SW = SEQ + PADW
GT = 512
GC = GT // P
NG = NB * SEQ // GT
SC = SEQ // P
NCT = CONV // P
NAT = NCT + DI // P
XT0, BT, CT, ZT0 = 0, 2, 3, 4
ORDER = (BT, CT, XT0, XT0 + 1, ZT0, ZT0 + 1)
HALO = TAPS - 1
E, F = 8, 256
K = 2
ROUTE = E + NH
PS = 2 * P
MP = K * NT * P // PS + E
ROW = D + 4
R = 4
TURN0, TURN1 = 2, MP // R
EPS = 1e-5
EXP_FLOOR = -104.0
MASKED = -1.0e30


def program(nc, x, ln_w, ln_b, w_in_t, w_dt, conv_w, conv_b, dt_bias, a_log, d_skip, rms_w, w_out_t,
            router, gate_w, up_w, down_w, out):
    ctx = ExitStack()
    with ctx:
        def sb(name, shape, dt=F32):
            return ctx.enter_context(nc.sbuf_tensor(name, shape, dt))

        def sem(name):
            return ctx.enter_context(nc.semaphore(name))

        bank = [ctx.enter_context(nc.psum_tensor(f"bank{i}", [P, 512], F32)) for i in range(8)]

        slots_d = nc.dram_tensor("slots_d", (MP * PS, ROW), F32, kind="Internal").ap()
        moe_d = nc.dram_tensor("moe_d", (K * NT * P, D), F32, kind="Internal").ap()
        cs_d = nc.dram_tensor("cs_d", (2, NT * NH * P), F32, kind="Internal").ap()
        ncs_d = nc.dram_tensor("ncs_d", (2 * NH, NT, P), F32, kind="Internal").ap()

        x_sb = sb("x_sb", [P, NT, D])
        xw_hi = sb("xw_hi", [P, NB * SW], F32R)
        xw_lo = sb("xw_lo", [P, NB * SW], F32R)
        act = sb("act", [P, 2 * NAT * GT])
        raw = sb("raw", [P, NAT * GT])
        w_hi = sb("w_hi", [P, DI + CONV], F32R)
        w_lo = sb("w_lo", [P, DI + CONV], F32R)
        taps = sb("taps", [P, NCT, TAPS])
        wo_sb = sb("wo_sb", [P, 2, D])
        rdt_w = sb("rdt_w", [P, ROUTE])
        ident = sb("ident", [P, P])
        upper = sb("upper", [P, P])
        ones = sb("ones", [P, P])
        ident_b = sb("ident_b", [P, P], BF16)
        mask_b = sb("mask_b", [P, P], BF16)
        strict_b = sb("strict_b", [P, P], BF16)
        ones_b = sb("ones_b", [P, P], BF16)
        dd_l = sb("dd_l", [10, 2, 2, P], F32R)
        dd_r = sb("dd_r", [10, 2, 2 * NH * P], F32R)
        csp = sb("csp", [P, 4, 2, P], F32R)
        cols = sb("cols", [P, 10])
        lnw_c, lnb_c, cb_c, ds_c, rms_c = (cols[:, 0:1], cols[:, 1:2], cols[:, 2:6], cols[:, 6:8], cols[:, 8:10])
        heads = sb("heads", [P, 5, NH])
        dtb_in, alog_in, dtb, a_pos, a_neg = (heads[:, i, :] for i in range(5))
        lnb_b = sb("lnb_b", [P, P])
        wdt_sb = sb("wdt_sb", [P, NH])
        proj_b = sb("proj_b", [P, NAT])
        stats = sb("stats", [P, NT, 6])
        tok = sb("tok", [P, 11, NT])
        mean, var, r1, q_in, sq2, r12, nm, t_a, t_b, ssq, nmr1 = (tok[:, i, :] for i in range(11))
        dts = sb("dts", [P, NT, NH])
        cs_sb = sb("cs_sb", [P, NT, NH])
        e_cs = sb("e_cs", [P, NT, NH])
        e_end = sb("e_end", [P, NT, NH])
        e_tot = sb("e_tot", [P, NT, NH])
        meta = sb("meta", [P, NT, K, 2])
        slot_i = sb("slot_i", [P, NT, K], I32)
        eid = sb("eid", [1, MP], I32)
        l_sb = sb("l_sb", [P, 2, NH * P])
        m_sb = sb("m_sb", [P, 2, NH * P])
        xdt = sb("xdt", [P, 2, DI])
        xde = sb("xde", [P, 2, DI])
        b_sb = sb("b_sb", [P, 2, NS])
        yo_sb = sb("yo_sb", [P, DI])
        y_sb = sb("y_sb", [P, 2, DI])
        yd_sb = sb("yd_sb", [P, DI])
        yg = sb("yg", [P, 2, DI])
        sq = sb("sq", [P, 2, DI])
        state = sb("state", [P, DI])
        state_k = sb("state_k", [P, DI])
        small = sb("small", [P, 1432])
        x_hi = sb("x_hi", [P, 2, PS], F32R)
        x_lo = sb("x_lo", [P, 2, PS], F32R)
        rows = sb("rows", [P, R, K, ROW])
        slot_st = sb("slot_st", [P, R, K], I32)

        w_ln = act[:, 0:DI + CONV]
        w_raw, wo_raw = act[:, 2048:2816], act[:, 2816:3072].rearrange("p (j d) -> p j d", j=2)
        proj = raw[:, 0:NCT * (HALO + GT)].rearrange("p (i n) -> p i n", i=NCT)
        route_sb = raw[:, 2064:2064 + NT * ROUTE].rearrange("p (t c) -> p t c", c=ROUTE)
        xn2 = [m_sb[:, u, :] for u in range(2)]
        xt_g = [l_sb[:, u, :] for u in range(2)]
        te = [v.rearrange("p (t e) -> p t e", e=E) for v in
              [act[:, 3072 + i * 512:3072 + (i + 1) * 512] for i in range(6)]
              + [m_sb[:, 0, :], m_sb[:, 1, :], xde[:, :, :].rearrange("p a n -> p (a n)")]]
        th = [act[:, i * 256:(i + 1) * 256].rearrange("p (t h) -> p t h", h=NH) for i in range(6)]
        tv = [small[:, i * NT:(i + 1) * NT] for i in range(10)]
        oh_b = small[:, 640:896].bitcast(BF16).rearrange("p (t e) -> p t e", e=E)
        rev = small[:, 896:904]
        cnt_i = small[:, 904:912].bitcast(I32)
        ntl = small[:, 912:920]
        base = small[:, 920:928]
        base_s = small[:, 928:936]
        iota_r = small[:, 936:936 + MP].bitcast(I32)
        iota_f = small[:, 1080:1080 + MP]
        eid_f = small[:, 1220:1220 + MP]
        tokid = small[:, 1360:1360 + NT].bitcast(I32)
        rev_i = small[:, 1424:1432].bitcast(I32)
        ddr0 = raw[:, 1440:1440 + 2 * NH * P // 2]
        ym = [raw[:, r * 2 * D:(r + 1) * 2 * D] for r in range(R)]
        ht = [raw[:, (2 * R + u * 4) * P:(2 * R + u * 4 + 4) * P] for u in range(2)]
        gu_raw = [raw[:, i * 1024:(i + 1) * 1024] for i in range(3)] + [act[:, 0:1024]]
        gu_hi, gu_lo = xw_hi[:, 0:E * 2 * F], xw_lo[:, 0:E * 2 * F]
        dn_sb = act[:, 1024:1024 + 2 * E * D]
        x_again = [act[:, 3072 + r * D:3072 + (r + 1) * D] for r in range(R)]
        y_ch = [[t[:, o + c * 1024:o + (c + 1) * 1024].rearrange("p (t d) -> p t d", d=D) for c in range(K)]
                for t, o in ((act, 0), (act, 2048), (act, 4096), (raw, 0))]

        ld_w, ld_moe_w, ld_moe_w2, st_zero, st_cs, st_out = (sem(n) for n in (
            "ld_w", "ld_moe_w", "ld_moe_w2", "st_zero", "st_cs", "st_out"))
        scatters = sem("scatters")
        ld_x = [sem(f"ld_x{i}") for i in range(8)]
        ld_dd = [sem(f"ld_dd{i}") for i in range(2)]
        scat = [sem(f"scat{i}") for i in range(R)]
        ld_slot = [sem(f"ld_slot{i}") for i in range(R)]
        st_moe = [sem(f"st_moe{i}") for i in range(R)]
        ld_again = [sem(f"ld_again{i}") for i in range(R)]
        ld_sum = [sem(f"ld_sum{i}") for i in range(8)]
        pool_chain, consts, w_ln_done, w_hi_done, wdt_done, lnb_done, dtb_ps, wdve_done = (sem(n) for n in (
            "pool_chain", "consts", "w_ln_done", "w_hi_done", "wdt_done", "lnb_done", "dtb_ps", "wdve_done"))
        dve_chain, act_chain = sem("dve_chain"), sem("act_chain")
        var_done, sq_r1, q_done, sq_q, norm_done = (sem(n) for n in ("var_done", "sq_r1", "q_done", "sq_q", "norm_done"))
        a_xn, a_tp, a_xt, a_hi, a_lo, a_rt, a_rs = (sem(n) for n in (
            "a_xn", "a_tp", "a_xt", "a_hi", "a_lo", "a_rt", "a_rs"))
        a_exp, dabs, dexp, adt_done, cs_ps, cs_copied, e_done, dsub_done, csT_ps, csp_done = (sem(n) for n in (
            "a_exp", "dabs", "dexp", "adt_done", "cs_ps", "cs_copied", "e_done", "dsub_done", "csT_ps", "csp_done"))
        gap_done, gap_exp, oh_done, rank_ps, top2_done, top2_exp, dp_done, dp_exp, slots_done, eid_done = (
            sem(n) for n in ("gap_done", "gap_exp", "oh_done", "rank_ps", "top2_done", "top2_exp", "dp_done",
                             "dp_exp", "slots_done", "eid_done"))
        proj_ps, proj_done, halo_done, tap0_done, taps_done, silu_done, gate_silu = (sem(n) for n in (
            "proj_ps", "proj_done", "halo_done", "tap0_done", "taps_done", "silu_done", "gate_silu"))
        (dd_done, l_done, front_done, b_done, m_done, xdt_done, xde_done, mid_done, yo_done, y_done, keep_done,
         state_done, yt_done, skip_done, gate_done, sq_done, o_done, o_kept, row_done, xn_done) = (sem(n) for n in (
            "dd_done", "l_done", "front_done", "b_done", "m_done", "xdt_done", "xde_done", "mid_done", "yo_done",
            "y_done", "keep_done", "state_done", "yt_done", "skip_done", "gate_done", "sq_done", "o_done", "o_kept",
            "row_done", "xn_done"))
        (xt_done, xts_done, gu_done, silu_m, h_done, ht_done, hts_done, id_done, out_done, ym_done) = (
            sem(n) for n in ("xt_done", "xts_done", "gu_done", "silu_m", "h_done", "ht_done", "hts_done", "id_done",
                             "out_done", "ym_done"))
        gu_hi_done, gu_lo_done, xhi_done = sem("gu_hi_done"), sem("gu_lo_done"), sem("xhi_done")
        ms_done, rms_sq, rms_done, resid_done, place_free, moe_sum, total_done = (sem(n) for n in (
            "ms_done", "rms_sq", "rms_done", "resid_done", "place_free", "moe_sum", "total_done"))

        def by_head(t):
            return t.rearrange("p (h c) -> p h c", h=NH)

        def tile_ix(nn):
            return bass.ds(nn, 1)

        def per_head(t, nn):
            return t[:, tile_ix(nn), :].rearrange("p a h -> p (a h)").unsqueeze(2).broadcast_to([P, NH, HD])

        block = ctx.enter_context(nc.Block())

        def over_sequences(eng, body):
            body(0)
            with eng.Fori(1, NB - 1) as b:
                body(b)
            body(NB - 1)

        def over_pairs(eng, stages, beside=()):
            def turn(m, checked):
                for r in range(R):
                    for fn, lag in stages:
                        if not checked or 0 <= m * R + r - lag < MP:
                            fn(m + (r - lag) // R, (r - lag) % R)
                    if not checked:
                        for fn in beside:
                            fn(m - TURN0, r)

            lags = [lag for _, lag in stages]
            assert (TURN1 - TURN0) * R == NT and 0 <= min(lags) and max(lags) <= R
            for m in range(TURN0):
                turn(m, True)
            with eng.Fori(TURN0, TURN1) as m:
                turn(m, False)
            for m in range(TURN1, -(-(MP + max(lags)) // R)):
                turn(m, True)

        def is_first(m):
            return isinstance(m, int) and m <= 0

        def is_last(b):
            return isinstance(b, int) and b == NB - 1

        def group_act(g):
            return act[:, (g % 2) * NAT * GT:(g % 2 + 1) * NAT * GT].rearrange("p (t n) -> p t n", n=GT)

        def in_group(j):
            return slice((j % GC) * P, (j % GC + 1) * P)

        @block.sync
        def _(sp):
            for i in range(8):
                sp.dma_start(x_sb[:, 8 * i:8 * i + 8, :], x[:, 8 * i:8 * i + 8, :]).then_inc(ld_x[i], 16)
            for dst, src in ((cols[:, 0:1], ln_w), (cols[:, 1:2], ln_b), (cols[:, 2:6], conv_b), (cols[:, 6:8], d_skip),
                             (cols[:, 8:10], rms_w), (w_raw, w_in_t), (wdt_sb[:, :], w_dt), (rdt_w[:, 0:E], router),
                             (wo_raw, w_out_t), (dtb_in, dt_bias.broadcast_to([P, NH])),
                             (alog_in, a_log.broadcast_to([P, NH])), (taps[:, :, :], conv_w)):
                sp.dma_start(dst, src).then_inc(ld_w, 16)
            sp.wait_ge(consts, 1)
            for i in range(8):
                n = MP * PS // P // 8
                sp.dma_start(slots_d[i * n * P:(i + 1) * n * P, :].rearrange("(t p) c -> p t c", p=P),
                             rows[:, 0, 0, :].unsqueeze(1).broadcast_to([P, n, ROW])).then_inc(st_zero, 16)
            sp.wait_ge(csp_done, 4)
            for hl in range(2):
                sp.dma_start(cs_d[hl].rearrange("(k p l) -> p k l", p=P, l=P),
                             csp[:, hl, :, :].bitcast(F32)).then_inc(st_cs, 16)
                for k in range(2):
                    nt = NT // 2
                    for h in range(NH):
                        sp.dma_start(ncs_d[hl * NH + h, k * nt:(k + 1) * nt, :],
                                     csp[h:P:NH, 2 + hl, k, :].bitcast(F32)).then_inc(st_cs, 16)
            sp.wait_ge(st_cs, 16 * 2 * (1 + 2 * NH))
            sp.wait_ge(wdve_done, 1)

            def dd_loads(b):
                for i in range(SC // 2):
                    if not (is_first(b) and i < 2):
                        sp.wait_ge(dd_done, b * SC + 2 * i - 2)
                    n = b * SC + 2 * i
                    sp.dma_start(dd_l[0:8, i % 2, :, :].bitcast(F32), ncs_d[:, bass.ds(n, 2), :])\
                        .then_inc(ld_dd[i % 2], 16)
                    sp.dma_start(dd_r[8:10, i % 2, :].bitcast(F32), cs_d[:, bass.ds(n * NH * P, 2 * NH * P)])\
                        .then_inc(ld_dd[i % 2], 16)

            over_sequences(sp, dd_loads)

            def gate_up_load(dst, e, n, signal):
                for g, w in enumerate((gate_w, up_w)):
                    sp.dma_start(dst.rearrange("p (e g f) -> p e g f", e=n, g=2)[:, :, g, :],
                                 w[e:e + n].rearrange("e d f -> d e f")).then_inc(signal, 16)

            sp.wait_ge(taps_done, NG * NCT * HALO)
            gate_up_load(raw[:, 0:3072], 0, 6, ld_moe_w)
            sp.wait_ge(gate_done, NT - GC)
            gate_up_load(act[:, 0:1024], 6, 2, ld_moe_w2)
            sp.dma_start(dn_sb.rearrange("p (j d) -> p j d", d=D),
                         down_w.rearrange("e (j p) d -> p (e j) d", p=P)).then_inc(ld_moe_w2, 16)
            sp.wait_ge(gate_done, NT)
            for r in range(R):
                sp.wait_ge(scat[r], 16 * K * NT // R)

            def slot_load(m, r):
                if not is_first(m):
                    sp.wait_ge(id_done, (m - 1) * R + r + 1)
                sp.dma_start(rows[:, r, :, :], slots_d[bass.ds((m * R + r) * PS, PS), :]
                             .rearrange("(p c) v -> p c v", c=2)).then_inc(ld_slot[r], 16)

            def load_again(m, r):
                sp.wait_ge(place_free, m * R + r + 1)
                sp.dma_start(x_again[r], x[:, tile_ix(m * R + r), :].rearrange("p a d -> p (a d)"))\
                    .then_inc(ld_again[r], 16)

            sp.sem_inc(place_free, R)
            over_pairs(sp, [(slot_load, 0)], [load_again])

            for r in range(R):
                sp.wait_ge(st_moe[r], 16 * 2 * MP // R)
            for k in range(8):
                if k >= 4:
                    sp.wait_ge(total_done, k - 3)
                for c in range(K):
                    sp.dma_start(y_ch[k % 4][c],
                                 moe_d[(c * NT + 8 * k) * P:(c * NT + 8 * k + 8) * P, :]
                                 .rearrange("(t p) d -> p t d", p=P)).then_inc(ld_sum[k], 16)
            for k in range(8):
                sp.wait_ge(total_done, k + 1)
                sp.dma_start(out[:, 8 * k:8 * k + 8, :], x_sb[:, 8 * k:8 * k + 8, :]).then_inc(st_out, 16)
            sp.wait_ge(st_out, 16 * 8)

        @block.gpsimd
        def _(pool):
            n = [0]

            def chain(ins):
                n[0] += 1
                ins.then_inc(pool_chain, 1)
                pool.wait_ge(pool_chain, n[0])

            chain(pool.memset(rows[:, :, :, :], 0.0))
            chain(pool.iota(tokid[:, 0:1], pattern=[[0, 1]], base=K * NT * P, channel_multiplier=1))
            pool.tensor_copy(rows[:, 0, 0, D:D + 1], tokid[:, 0:1]).then_inc(consts, 1)
            for t, v in ((ident, 0.0), (upper, 1.0), (strict_b, 1.0), (mask_b, 0.0)):
                chain(pool.memset(t[:, :], v))
            pool.memset(ones[:, :], 1.0)
            chain(pool.memset(ones_b[:, :], 1.0))
            chain(pool.affine_select(out=ident[:, :], in_=ident[:, :], compare_op=ALU.not_equal, fill=1.0, base=0,
                                     pattern=[[-1, P]], channel_multiplier=1))
            chain(pool.affine_select(out=upper[:, :], in_=upper[:, :], compare_op=ALU.is_ge, fill=0.0, base=0,
                                     pattern=[[1, P]], channel_multiplier=-1))
            chain(pool.affine_select(out=strict_b[:, :], in_=strict_b[:, :], compare_op=ALU.is_ge, fill=0.0, base=-1,
                                     pattern=[[1, P]], channel_multiplier=-1))
            chain(pool.affine_select(out=mask_b[:, :], in_=mask_b[:, :], compare_op=ALU.is_ge, fill=MASKED, base=0,
                                     pattern=[[1, P]], channel_multiplier=-1))
            ind = ddr0[0:8, :].rearrange("p (h l) -> p h l", h=NH)
            chain(pool.memset(ddr0[0:8, :], 0.0))
            for part in range(2):
                chain(pool.affine_select(out=ind, in_=ind, compare_op=ALU.not_equal, fill=1.0, base=NH * part,
                                         pattern=[[1, NH], [0, P]], channel_multiplier=-1))
            chain(pool.iota(rev_i, pattern=[[-1, E]], base=E, channel_multiplier=0))
            chain(pool.iota(iota_r, pattern=[[1, MP]], base=0, channel_multiplier=0))
            pool.wait_ge(consts, 1)
            chain(pool.iota(tokid, pattern=[[P, NT]], base=0, channel_multiplier=1))
            pool.tensor_copy(ident_b[:, :], ident[:, :]).then_inc(consts, 1)

            pool.wait_ge(norm_done, 2)
            pool.wait_ge(st_zero, 16 * 8)
            pool.wait_ge(slots_done, 1)

            def inputs_to_end(nn, u):
                pool.wait_ge(xdt_done, nn + 1)
                nc.gpsimd.tensor_tensor(by_head(xde[:, u, :]), by_head(xdt[:, u, :]), per_head(e_end, nn),
                                        ALU.mult).then_inc(xde_done, 1)

            def prepare_rows(b, j):
                nn, r = b * SC + j, j % R
                if not (is_first(b) and j < R):
                    pool.wait_ge(slots_done, 1)
                    pool.wait_ge(scat[r], 16 * K * (b * 2 + j // R))
                nc.gpsimd.tensor_copy(rows[:, r, :, D:D + 2],
                                      meta[:, tile_ix(nn), :, :].rearrange("p a k v -> p (a k) v")).then_inc(row_done, 1)
                nc.gpsimd.tensor_copy(slot_st[:, r, :],
                                      slot_i[:, tile_ix(nn), :].rearrange("p a k -> p (a k)")).then_inc(row_done, 1)
                pool.wait_ge(xn_done, nn + 1)
                pool.sem_inc(scatters, 1)
                nc.gpsimd.tensor_copy(rows[:, r, 1, 0:D], rows[:, r, 0, 0:D]).then_inc(row_done, 1)
                pool.wait_ge(row_done, 3 * (nn + 1))
                pool.sem_inc(scatters, 1)

            def scatter(r, c):
                nc.gpsimd.indirect_dma_start(
                    out=slots_d, out_offset=bass.IndirectOffsetOnAxis(ap=slot_st[:, r, c:c + 1], axis=0),
                    in_=rows[:, r, c, :], in_offset=None).then_inc(scat[r], 16)

            def sequence(b):
                for j in range(SC):
                    nn = b * SC + j
                    if j:
                        pool.wait_ge(state_done, nn)
                        nc.gpsimd.tensor_tensor(by_head(state_k[:, :]), by_head(state[:, :]),
                                                per_head(e_tot, nn), ALU.mult).then_inc(keep_done, 1)
                    prepare_rows(b, j)
                    scatter(j % R, 0)
                    if not (is_last(b) and j == SC - 1):
                        inputs_to_end(nn + 1, (j + 1) % 2)
                    scatter(j % R, 1)

            inputs_to_end(0, 0)
            over_sequences(pool, sequence)

            def moe_scatter(m, r):
                pool.wait_ge(id_done, m * R + r + 1)
                pool.wait_ge(ym_done, m * R + r + 1)
                pool.sem_inc(scatters, 1)
                for c in range(2):
                    nc.gpsimd.indirect_dma_start(
                        out=moe_d, out_offset=bass.IndirectOffsetOnAxis(ap=slot_st[:, r, c:c + 1], axis=0),
                        in_=ym[r][:, c * D:(c + 1) * D], in_offset=None,
                        bounds_check=K * NT * P - 1, oob_is_err=False).then_inc(st_moe[r], 16)

            over_pairs(pool, [(moe_scatter, 0)])

            for k in range(7):
                pool.wait_ge(ld_sum[k], 32)
                nc.gpsimd.tensor_tensor(y_ch[k % 4][0], y_ch[k % 4][0], y_ch[k % 4][1], ALU.add).then_inc(moe_sum, 1)

        @block.scalar
        def _(act_e):
            A = nc.scalar.activation
            n = [0]

            def chain(ins):
                n[0] += 1
                ins.then_inc(act_chain, 1)
                act_e.wait_ge(act_chain, n[0])

            act_e.wait_ge(var_done, 1)
            A(t_b, t_a, ACT.Sqrt).then_inc(sq_r1, 1)
            act_e.wait_ge(q_done, 1)
            A(sq2, q_in, ACT.Sqrt).then_inc(sq_q, 1)
            act_e.wait_ge(ld_w, 16 * 12)
            A(a_pos, alog_in, ACT.Exp).then_inc(a_exp, 1)
            act_e.wait_ge(w_ln_done, 1)
            A(w_hi[:, :], w_ln, ACT.Copy).then_inc(w_hi_done, 1)
            for i in range(2):
                A(wo_sb[:, i, :], wo_raw[:, i, :], ACT.Copy, scale=rms_c[:, i:i + 1]).then_inc(w_hi_done, 1)

            def group(it):
                for u in range(2):
                    g = it * 2 + u
                    act_e.wait_ge(a_tp, g + 1)
                    if not is_first(it):
                        act_e.wait_ge(a_rt, g - 1)
                        act_e.wait_ge(a_lo, g - 1)
                    A(xt_g[u], bank[u][:, :], ACT.Copy).then_inc(a_xt, 1)
                    act_e.wait_ge(sq_q, 1)
                    act_e.wait_ge(a_xt, g + 1)
                    A(xw_hi[:, bass.ds(it * SW + PADW + u * GT, GT)], xt_g[u], ACT.Copy).then_inc(a_hi, 1)

            group(0)
            with act_e.Fori(1, NB) as it:
                group(it)

            act_e.wait_ge(dabs, 1)
            A(th[2], th[1], ACT.Exp, scale=-1.0).then_inc(dexp, 1)
            act_e.wait_ge(cs_copied, 2)
            A(e_cs[:, :, :], cs_sb[:, :, :], ACT.Exp).then_inc(e_done, 1)
            A(e_tot[:, :, :], th[5], ACT.Exp).then_inc(e_done, 1)
            act_e.wait_ge(dsub_done, 1)
            A(e_end[:, :, :], th[3], ACT.Exp).then_inc(e_done, 1)
            def keep_proj(g6, i, par):
                act_e.wait_ge(proj_ps, g6 + i + 1)
                t = ORDER[i]
                A(proj[:, t, HALO:] if t < NCT else group_act(par)[:, t, :], bank[0][:, :], ACT.Identity,
                  bias=proj_b[:, t:t + 1]).then_inc(proj_done, 1)

            def tap0(g6, i, par):
                act_e.wait_ge(proj_done, g6 + i + 1)
                t = ORDER[i]
                A(group_act(par)[:, t, :], proj[:, t, HALO:], ACT.Identity, bias=cb_c[:, t:t + 1],
                  scale=taps[:, t, HALO:]).then_inc(tap0_done, 1)

            def halo(g, par):
                src = proj[:, :, GT:] if par else xw_hi[:, 0:HALO].bitcast(F32).unsqueeze(1).broadcast_to([P, NCT, HALO])
                A(proj[:, :, 0:HALO], src, ACT.Copy).then_inc(halo_done, 1)
                act_e.wait_ge(halo_done, g + 1)

            def silu(g, par):
                act_e.wait_ge(taps_done, (g + 1) * NCT * HALO)
                act_e.wait_ge(proj_done, (g + 1) * NAT)
                conv, gate = (act[:, (par * NAT + t) * GT:(par * NAT + t + n) * GT]
                              for t, n in ((0, NCT), (NCT, NAT - NCT)))
                A(conv, conv, ACT.Silu).then_inc(silu_done, 1)
                A(gate, gate, ACT.Silu).then_inc(gate_silu, 1)

            def decays(nn, u):
                act_e.wait_ge(dd_done, nn + 1)
                A(l_sb[:, u, :], bank[2][:, :], ACT.Exp).then_inc(l_done, 1)

            act_e.wait_ge(e_done, 3)
            halo(0, 0)
            for i in range(NAT):
                keep_proj(0, i, 0)
                if i < NCT:
                    tap0(0, i, 0)
            act_e.wait_ge(gap_done, 1)
            A(te[3], te[1], ACT.Exp).then_inc(gap_exp, 1)
            act_e.wait_ge(top2_done, 1)
            A(tv[4], tv[3], ACT.Exp).then_inc(top2_exp, 1)
            silu(0, 0)
            decays(0, 0)
            act_e.wait_ge(dp_done, 1)
            A(tv[7], tv[6], ACT.Exp).then_inc(dp_exp, 1)
            act_e.wait_ge(norm_done, 2)
            act_e.wait_ge(st_zero, 16 * 8)
            act_e.wait_ge(slots_done, 1)

            def row(nn, r, uses):
                act_e.wait_ge(norm_done, 2)
                if uses is not None:
                    act_e.wait_ge(scat[r], 16 * K * uses)
                t = tile_ix(nn)
                A(rows[:, r, 0, 0:D], x_sb[:, t, :].rearrange("p a d -> p (a d)"), ACT.Identity,
                  bias=nmr1[:, t], scale=r1[:, t]).then_inc(xn_done, 1)

            def keep_out(nn):
                act_e.wait_ge(norm_done, 2)
                act_e.wait_ge(o_done, nn + 1)
                act_e.wait_ge(xn_done, nn + 1)
                A(x_sb[:, tile_ix(nn), :].rearrange("p a d -> p (a d)"), bank[7][:, 0:D], ACT.Copy)
                A(ssq[:, tile_ix(nn)], bank[7][:, D:D + 1], ACT.Copy).then_inc(o_kept, 1)

            def square(nn, u):
                act_e.wait_ge(gate_done, nn + 1)
                A(sq[:, u, :], yg[:, u, :], ACT.Square).then_inc(sq_done, 1)

            def sequence(b):
                first, last = is_first(b), is_last(b)
                for j in range(SC):
                    nn, q, g = b * SC + j, j % GC, j // GC
                    more = not (last and g == 1)
                    nxt, g6 = b * 2 + g + 1, (b * 2 + g + 1) * NAT
                    if not (first and j < 4):
                        keep_out(nn - 4)
                    if not (last and j == SC - 1):
                        decays(nn + 1, (j + 1) % 2)
                    row(nn, j % R, None if first and j < R else b * 2 + j // R)
                    if more and q == 0:
                        halo(nxt, 1 - g)
                    if more and q < 3:
                        keep_proj(g6, 2 * q, 1 - g)
                    if more and q == 0:
                        tap0(g6, 0, 1 - g)
                    if more and q == 3:
                        silu(nxt, 1 - g)
                    if not (first and j < 2):
                        square(nn - 2, j % 2)
                    if more and q == 1:
                        tap0(g6, 2, 1 - g)
                    if more and q < 3:
                        keep_proj(g6, 2 * q + 1, 1 - g)
                    if more and q < 2:
                        tap0(g6, 2 * q + 1, 1 - g)
                    if last and g == 1 and q:
                        weights_high(q - 1)

            def weights_high(i):
                if i < 3:
                    act_e.wait_ge(ld_moe_w, 32)
                else:
                    act_e.wait_ge(ld_moe_w2, 48)
                A(gu_hi[:, i * 1024:(i + 1) * 1024], gu_raw[i], ACT.Copy).then_inc(gu_hi_done, 1)

            over_sequences(act_e, sequence)
            weights_high(3)
            keep_out(NT - 4)
            keep_out(NT - 3)
            for n_ in (NT - 2, NT - 1):
                square(n_, n_ % 2)
            for n_ in (NT - 2, NT - 1):
                keep_out(n_)
            act_e.wait_ge(ms_done, 1)
            A(t_b, t_a, ACT.Sqrt).then_inc(rms_sq, 1)

            def silu_pair(m, r):
                act_e.wait_ge(gu_done, m * R + r + 1)
                for c in range(2):
                    a = A(l_sb[:, r % 2, c * F:(c + 1) * F], bank[2 + 2 * (r % 2) + c][:, 0:F], ACT.Silu)
                a.then_inc(silu_m, 1)

            def hidden_keep(m, r):
                act_e.wait_ge(ht_done, m * R + r + 1)
                A(ht[r % 2], bank[6 + r % 2][:, :], ACT.Copy).then_inc(hts_done, 1)

            def y_keep(m, r):
                if isinstance(m, int) and m * R + r == MP - 1:
                    act_e.wait_ge(id_done, MP)
                act_e.wait_ge(out_done, m * R + r + 1)
                A(ym[r], bank[1][:, 0:2 * D], ACT.Copy).then_inc(ym_done, 1)

            def residual(m, r):
                act_e.wait_ge(rms_done, 1)
                act_e.wait_ge(ld_again[r], 16 * (m + 1))
                t = tile_ix(m * R + r)
                A(x_again[r], x_again[r], ACT.Identity, bias=nmr1[:, t], scale=r12[:, t]).then_inc(resid_done, 1)

            over_pairs(act_e, [(y_keep, 4), (silu_pair, 1), (hidden_keep, 2)], [residual])

        @block.tensor
        def _(pe):
            mm = nc.tensor.matmul

            def turn_x(it, u):
                g = it * 2 + u
                if not is_first(it):
                    pe.wait_ge(a_xt, g - 1)
                pe.wait_ge(a_xn, g * 4 + 4)
                for i in range(4):
                    tp = nc.tensor.transpose(bank[u][:, i * P:(i + 1) * P], xn2[u][:, i * P:(i + 1) * P], ident[:, :])
                tp.then_inc(a_tp, 1)

            def route(it, u):
                g = it * 2 + u
                pe.wait_ge(a_xt, g + 1)
                if not is_first(it):
                    pe.wait_ge(a_rs, g - 1)
                for i in range(4):
                    rt = mm(bank[4 + u][:, i * ROUTE:(i + 1) * ROUTE], xt_g[u][:, i * P:(i + 1) * P], rdt_w[:, :],
                            start=True, stop=True)
                rt.then_inc(a_rt, 1)

            pe.wait_ge(consts, 2)
            turn_x(0, 0)
            turn_x(0, 1)
            pe.wait_ge(lnb_done, 1)
            mm(bank[7][:, 0:NH], lnb_b[:, :], wdt_sb[:, :], start=True, stop=True)
            for t in range(NAT):
                c = slice(DI + t * P, DI + (t + 1) * P) if t < NCT else slice((t - NCT) * P, (t - NCT + 1) * P)
                m = mm(bank[7][:, NH + t:NH + t + 1], w_raw[:, c], lnb_c, start=True, stop=True)
            m.then_inc(dtb_ps, 1)
            pe.wait_ge(wdt_done, 1)
            route(0, 0)
            with pe.Fori(1, NB) as it:
                turn_x(it, 0)
                route(it - 1, 1)
                turn_x(it, 1)
                route(it, 0)
            route(NB - 1, 1)

            pe.wait_ge(adt_done, 1)
            adt = th[4].rearrange("p t h -> p (t h)")
            mm(bank[7][:, 0:256], upper[:, :], adt, start=True, stop=True)
            mm(bank[7][:, 256:512], ones[:, :], adt, start=True, stop=True).then_inc(cs_ps, 1)
            pe.wait_ge(cs_copied, 2)
            csf = cs_sb[:, :, :].rearrange("p t h -> p (t h)")
            nc.tensor.transpose(bank[6][:, 0:P], csf[:, 0:P], ident[:, :])
            nc.tensor.transpose(bank[6][:, P:2 * P], csf[:, P:2 * P], ident[:, :]).then_inc(csT_ps, 1)
            pe.wait_ge(wdve_done, 1)
            pe.wait_ge(w_hi_done, 3)
            for done in (a_hi, a_xt, a_rs):
                pe.wait_ge(done, NG)
            pe.wait_ge(a_lo, NG)

            def project(b, half, g6, i):
                if not (isinstance(g6, int) and g6 + i < 1):
                    pe.wait_ge(proj_done, g6 + i)
                t = ORDER[i]
                c = slice(DI + t * P, DI + (t + 1) * P) if t < NCT else slice((t - NCT) * P, (t - NCT + 1) * P)
                for a, (w, v) in enumerate(((w_hi, xw_hi), (w_hi, xw_lo), (w_lo, xw_hi))):
                    m = mm(bank[0][:, :], w[:, c], v[:, bass.ds(b * SW + PADW + half * GT, GT)], start=(a == 0),
                           stop=(a == 2))
                m.then_inc(proj_ps, 1)

            def exponents(b, j):
                nn, pr, o = b * SC + j, (j // 2) % 2, j % 2
                pe.wait_ge(ld_dd[pr], 32 * (b * 2 + j // 4 + 1))
                if not (is_first(b) and j < 1):
                    pe.wait_ge(l_done, nn)
                mm(bank[2][:, :], dd_l[:, pr, o, :], dd_r[:, pr, o * NH * P:(o + 1) * NH * P], start=True, stop=False)
                mm(bank[2][:, :], ident_b[:, :], mask_b[:, :].unsqueeze(1).broadcast_to([P, NH, P]),
                   start=False, stop=True).then_inc(dd_done, 1)

            def front(b, j):
                if j % GC == 0:
                    pe.wait_ge(silu_done, b * 2 + j // GC + 1)
                ab, cs, fb = group_act(j // GC), in_group(j), bank[3 + j % 2]
                mm(fb[:, 0:P], ab[:, BT, cs], ab[:, CT, cs], start=True, stop=True)
                for i, t in enumerate((XT0, XT0 + 1, BT)):
                    tp = nc.tensor.transpose(fb[:, (i + 1) * P:(i + 2) * P], ab[:, t, cs], ident[:, :])
                tp.then_inc(front_done, 1)

            def middle(b, j):
                nn, u = b * SC + j, j % 2
                if is_first(b) and j < 1:
                    pe.wait_ge(m_done, 1)
                else:
                    pe.wait_ge(y_done, nn)
                pe.wait_ge(xde_done, nn + 1)
                for h in range(NH):
                    mm(bank[5][:, h * HD:(h + 1) * HD], m_sb[:, u, h * P:(h + 1) * P],
                       xdt[:, u, h * HD:(h + 1) * HD], start=True, stop=True)
                if j:
                    mm(bank[5][:, DI:2 * DI], group_act(j // GC)[:, CT, in_group(j)], state[:, :], start=True, stop=True)
                mm(bank[6][:, 0:DI], b_sb[:, u, :], xde[:, u, :], start=True, stop=True).then_inc(mid_done, 1)

            def turn_y(nn, u, early):
                pe.wait_ge(y_done, nn + 1)
                if not early:
                    pe.wait_ge(skip_done, nn)
                for c in range(2):
                    tp = nc.tensor.transpose(bank[1][:, c * P:(c + 1) * P], y_sb[:, u, c * P:(c + 1) * P], ident[:, :])
                tp.then_inc(yt_done, 1)

            def project_out(nn, u, early):
                pe.wait_ge(sq_done, nn + 1)
                if not early:
                    pe.wait_ge(o_kept, nn)
                for c in range(2):
                    mm(bank[7][:, 0:D], yg[:, u, c * P:(c + 1) * P], wo_sb[:, c, :], start=(c == 0), stop=(c == 1))
                for c in range(2):
                    m = mm(bank[7][:, D:D + 1], sq[:, u, c * P:(c + 1) * P], ones[:, 0:1], start=(c == 0),
                           stop=(c == 1))
                m.then_inc(o_done, 1)

            pe.wait_ge(e_done, 2)
            pe.wait_ge(csp_done, 4)
            for i in range(NAT):
                project(0, 0, 0, i)
            pe.wait_ge(oh_done, 1)
            ohf = oh_b.rearrange("p t e -> p (t e)")
            mm(bank[4][:, :], strict_b[:, :], ohf, start=True, stop=True)
            mm(bank[5][:, :], ones_b[:, :], ohf, start=True, stop=True).then_inc(rank_ps, 1)
            exponents(0, 0)
            front(0, 0)
            pe.wait_ge(slots_done, 1)

            def sequence(b):
                first, last = is_first(b), is_last(b)
                for j in range(SC):
                    nn, q, g = b * SC + j, j % GC, j // GC
                    ahead = not (last and j == SC - 1)
                    more = not (last and g == 1) and q < 3
                    nxt = (b if g == 0 else b + 1), 1 - g, (b * 2 + g + 1) * NAT
                    if ahead:
                        exponents(b, j + 1)
                    if ahead and q < 3:
                        front(b, j + 1)
                    if more:
                        project(*nxt, 2 * q)
                    if not (first and j < 3):
                        project_out(nn - 3, (j - 3) % 2, first and j < 4)
                    middle(b, j)
                    if not (first and j < 1):
                        turn_y(nn - 1, (j - 1) % 2, first and j < 2)
                    if more:
                        project(*nxt, 2 * q + 1)
                    if ahead and q == 3:
                        front(b, j + 1)

            over_sequences(pe, sequence)
            project_out(NT - 3, (NT - 3) % 2, False)
            turn_y(NT - 1, (NT - 1) % 2, False)
            project_out(NT - 2, (NT - 2) % 2, False)
            project_out(NT - 1, (NT - 1) % 2, False)
            pe.wait_ge(o_kept, NT)
            pe.wait_ge(gu_lo_done, 1)
            pe.wait_ge(eid_done, 1)

            def expert(m, r):
                return pe.value_load(eid[0:1, bass.ds(m * R + r, 1)], min_val=0, max_val=E - 1)

            def gate_up(m, r):
                ex = expert(m, r)
                pe.wait_ge(xts_done, m * R + r + 1)
                for c in range(2):
                    for a, (xs, w) in enumerate(((x_hi, gu_hi), (x_hi, gu_lo), (x_lo, gu_hi))):
                        gu = mm(bank[2 + 2 * (r % 2) + c][:, :], xs[:, r % 2, c * P:(c + 1) * P],
                                w[:, bass.ds(ex * (2 * F), 2 * F)], start=(a == 0), stop=(a == 2))
                gu.then_inc(gu_done, 1)

            def turn_x(m, r):
                pe.wait_ge(ld_slot[r], 16 * (m + 1))
                for c in range(2):
                    tp = nc.tensor.transpose(bank[0][:, c * P:(c + 1) * P], rows[:, r, c, 0:D], ident[:, :])
                tp.then_inc(xt_done, 1)

            def turn_h(m, r):
                pe.wait_ge(h_done, m * R + r + 1)
                for i in range(4):
                    tp = nc.tensor.transpose(bank[6 + r % 2][:, i * P:(i + 1) * P], m_sb[:, r % 2, i * P:(i + 1) * P],
                                             ident[:, :])
                tp.then_inc(ht_done, 1)

            def down(m, r):
                ex = expert(m, r)
                pe.wait_ge(hts_done, m * R + r + 1)
                if not (is_first(m) and r < 1):
                    pe.wait_ge(ym_done, m * R + r)
                for c in range(2):
                    for f in range(2):
                        o = mm(bank[1][:, c * D:(c + 1) * D], ht[r % 2][:, (2 * c + f) * P:(2 * c + f + 1) * P],
                               dn_sb[:, bass.ds(ex * (2 * D) + f * D, D)], start=(f == 0), stop=(f == 1))
                o.then_inc(out_done, 1)

            over_pairs(pe, [(gate_up, 1), (turn_x, 0), (turn_h, 2), (down, 3)])

        @block.vector
        def _(dve):
            V = nc.vector
            n = [0]

            def chain(ins):
                n[0] += 1
                ins.then_inc(dve_chain, 1)
                dve.wait_ge(dve_chain, n[0])

            for t in (xw_hi, xw_lo):
                V.memset(t[:, :].rearrange("p (b s) -> p b s", b=NB)[:, :, 0:PADW].bitcast(F32), 0.0)
            V.memset(dd_l[:, :, :, :].bitcast(F32), 1.0)
            for t in range(NT):
                if t % 8 == 0:
                    dve.wait_ge(ld_x[t // 8], 16)
                st = V.bn_stats(stats[:, t, :], x_sb[:, t, :])
            chain(st)
            me, mo, ve, vo = (stats[:, :, i] for i in (1, 4, 2, 5))
            chain(V.tensor_tensor(mean, me, mo, ALU.add))
            chain(V.tensor_scalar(nm, mean, -0.5, None, ALU.mult))
            chain(V.tensor_tensor(t_a, me, mo, ALU.subtract))
            chain(V.tensor_tensor(t_a, t_a, t_a, ALU.mult))
            chain(V.tensor_tensor(var, ve, vo, ALU.add))
            chain(V.scalar_tensor_tensor(out=var, in0=t_a, scalar=float(D // 4), in1=var, op0=ALU.mult, op1=ALU.add))
            chain(V.tensor_scalar(var, var, 1.0 / D, None, ALU.mult))
            V.tensor_scalar(t_a, var, EPS, None, ALU.add).then_inc(var_done, 1)
            dve.wait_ge(sq_r1, 1)
            chain(V.reciprocal(r1, t_b))
            chain(V.tensor_tensor(t_b, r1, r1, ALU.mult))
            chain(V.tensor_tensor(t_b, t_b, var, ALU.mult))
            V.tensor_scalar(q_in, t_b, EPS, None, ALU.add).then_inc(q_done, 1)
            dve.wait_ge(sq_q, 1)
            chain(V.reciprocal(r12, sq2))
            V.tensor_tensor(nmr1, nm, r1, ALU.mult).then_inc(norm_done, 1)
            V.tensor_tensor(r12, r12, r1, ALU.mult).then_inc(norm_done, 1)
            dve.wait_ge(norm_done, 2)

            def norm_group(it, u):
                g = it * 2 + u
                if not is_first(it):
                    dve.wait_ge(a_tp, g - 1)
                for i in range(4):
                    t = bass.ds(it * 8 + u * 4 + i, 1)
                    V.tensor_scalar(xn2[u][:, i * P:(i + 1) * P], x_sb[:, t, :].rearrange("p a d -> p (a d)"),
                                    nm[:, t], r12[:, t], ALU.add, ALU.mult).then_inc(a_xn, 1)

            norm_group(0, 0)
            norm_group(0, 1)

            dve.wait_ge(ld_w, 16 * 12)
            chain(V.memset(lnb_b[:, :], 1.0))
            V.tensor_scalar(lnb_b[:, :], lnb_b[:, :], lnb_c, None, ALU.mult).then_inc(lnb_done, 1)
            V.tensor_scalar(rdt_w[:, E:ROUTE], wdt_sb[:, :], lnw_c, None, ALU.mult).then_inc(wdt_done, 1)
            V.tensor_scalar(w_ln, w_raw, lnw_c, None, ALU.mult).then_inc(w_ln_done, 1)
            dve.wait_ge(a_exp, 1)
            chain(V.tensor_scalar(a_neg, a_pos, -1.0, None, ALU.mult))
            dve.wait_ge(dtb_ps, 1)
            V.tensor_copy(proj_b[:, :], bank[7][:, NH:NH + NAT])
            chain(V.tensor_tensor(dtb, dtb_in, bank[7][:, 0:NH], ALU.add))
            dve.wait_ge(w_hi_done, 3)
            chain(V.tensor_tensor(w_lo[:, :], w_ln, w_hi[:, :].bitcast(F32), ALU.subtract))
            dve.wait_ge(consts, 2)
            for i in range(2):
                for a in range(2):
                    last = V.tensor_copy(dd_r[0:8, i, a * NH * P:(a + 1) * NH * P], ddr0[0:8, :])
            last.then_inc(wdve_done, 1)
            V.tensor_copy(rev, rev_i)
            V.tensor_copy(iota_f, iota_r)
            V.tensor_copy(meta[:, :, 0, 0], tokid)
            chain(V.tensor_copy(meta[:, :, 1, 0], tokid))
            chain(V.tensor_scalar(meta[:, :, 1, 0], meta[:, :, 1, 0], float(NT * P), None, ALU.add))

            def low_part(it, u):
                g = it * 2 + u
                dve.wait_ge(a_hi, g + 1)
                c = bass.ds(it * SW + PADW + u * GT, GT)
                V.tensor_tensor(xw_lo[:, c], xt_g[u], xw_hi[:, c].bitcast(F32), ALU.subtract).then_inc(a_lo, 1)
                dve.wait_ge(a_rt, g + 1)
                V.tensor_copy(route_sb[:, bass.ds(g * 4, 4), :],
                              bank[4 + u][:, 0:4 * ROUTE].rearrange("p (t c) -> p t c", c=ROUTE)).then_inc(a_rs, 1)

            with dve.Fori(1, NB) as it:
                for u in range(2):
                    norm_group(it, u)
                    low_part(it - 1, u)
            low_part(NB - 1, 0)
            low_part(NB - 1, 1)
            dve.wait_ge(a_rs, NG)

            def over_tok(c):
                return c.unsqueeze(1).broadcast_to([P, NT, NH])

            chain(V.tensor_tensor(th[0], route_sb[:, :, E:ROUTE], over_tok(dtb), ALU.add))
            V.scalar_tensor_tensor(out=th[1], in0=th[0], scalar=-1.0, in1=th[0], op0=ALU.mult, op1=ALU.max)\
                .then_inc(dabs, 1)
            dve.wait_ge(dexp, 1)
            chain(V.tensor_scalar(th[3], th[2], 2.0, None, ALU.add))
            chain(V.reciprocal(th[3], th[3]))
            chain(V.tensor_tensor(th[2], th[2], th[3], ALU.mult))
            chain(V.tensor_tensor(th[3], th[2], th[2], ALU.mult))
            chain(V.tensor_scalar(th[5], th[3], 1.0 / 17, None, ALU.mult))
            for c in (15, 13, 11, 9, 7, 5, 3):
                chain(V.scalar_tensor_tensor(out=th[5], in0=th[5], scalar=1.0 / c, in1=th[3], op0=ALU.add,
                                             op1=ALU.mult))
            chain(V.scalar_tensor_tensor(out=th[5], in0=th[5], scalar=1.0, in1=th[2], op0=ALU.add, op1=ALU.mult))
            chain(V.tensor_scalar(th[0], th[0], 0.0, None, ALU.max))
            chain(V.scalar_tensor_tensor(out=dts[:, :, :], in0=th[5], scalar=2.0, in1=th[0], op0=ALU.mult,
                                         op1=ALU.add))
            V.tensor_tensor(th[4], dts[:, :, :], over_tok(a_neg), ALU.mult).then_inc(adt_done, 1)
            dve.wait_ge(cs_ps, 1)
            V.tensor_copy(cs_sb[:, :, :], bank[7][:, 0:256].rearrange("p (t h) -> p t h", h=NH))\
                .then_inc(cs_copied, 1)
            V.tensor_copy(th[5], bank[7][:, 256:512].rearrange("p (t h) -> p t h", h=NH)).then_inc(cs_copied, 1)
            dve.wait_ge(cs_copied, 2)
            chain(V.tensor_tensor(th[3], th[5], cs_sb[:, :, :], ALU.subtract))
            V.tensor_scalar(th[3], th[3], 0.0, None, ALU.min).then_inc(dsub_done, 1)
            dve.wait_ge(csT_ps, 1)
            tp = bank[6][:, 0:2 * P].rearrange("p (k l) -> p k l", k=2)
            hi, lo, nhi, nlo = (csp[:, i, :, :] for i in range(4))
            V.tensor_copy(hi, tp).then_inc(csp_done, 1)
            dve.wait_ge(csp_done, 1)
            V.tensor_tensor(lo, tp, hi.bitcast(F32), ALU.subtract).then_inc(csp_done, 1)
            dve.wait_ge(csp_done, 2)
            V.tensor_scalar(nhi, hi.bitcast(F32), -1.0, None, ALU.mult).then_inc(csp_done, 1)
            V.tensor_scalar(nlo, lo.bitcast(F32), -1.0, None, ALU.mult).then_inc(csp_done, 1)

            def other_taps(g, par, lo, hi):
                for n_ in range(lo, hi):
                    i, k = divmod(n_, HALO)
                    t = ORDER[i]
                    if k:
                        dve.wait_ge(taps_done, g * NCT * HALO + n_)
                    else:
                        dve.wait_ge(tap0_done, g * NCT + i + 1)
                    V.scalar_tensor_tensor(out=group_act(par)[:, t, :], in0=proj[:, t, k:k + GT],
                                           scalar=taps[:, t, k:k + 1], in1=group_act(par)[:, t, :],
                                           op0=ALU.mult, op1=ALU.add).then_inc(taps_done, 1)

            def over_e(c):
                return c.unsqueeze(2).broadcast_to([P, NT, E])

            def over_t(c):
                return c.unsqueeze(1).broadcast_to([P, NT, E])

            lg, gap, pick, ex, oh0, gap2, oh1, pos, cnt = te
            chain(V.tensor_tensor(lg, route_sb[:, :, 0:E], over_e(sq2), ALU.mult))
            chain(V.tensor_reduce(tv[0], lg, AX, ALU.max))
            chain(V.tensor_tensor(gap, lg, over_e(tv[0]), ALU.subtract))
            V.tensor_scalar(gap, gap, EXP_FLOOR, None, ALU.max).then_inc(gap_done, 1)
            dve.wait_ge(gap_done, 1)
            chain(V.scalar_tensor_tensor(out=pick, in0=gap, scalar=0.0, in1=over_t(rev), op0=ALU.is_ge,
                                         op1=ALU.mult))
            chain(V.tensor_reduce(tv[1], pick, AX, ALU.max))
            chain(V.tensor_tensor(oh0, pick, over_e(tv[1]), ALU.is_equal))
            chain(V.scalar_tensor_tensor(out=gap2, in0=oh0, scalar=-1.0e4, in1=gap, op0=ALU.mult, op1=ALU.add))
            V.tensor_reduce(tv[3], gap2, AX, ALU.max).then_inc(top2_done, 1)
            dve.wait_ge(top2_done, 1)
            chain(V.tensor_tensor(pick, gap2, over_e(tv[3]), ALU.is_equal))
            chain(V.tensor_tensor(pick, pick, over_t(rev), ALU.mult))
            chain(V.tensor_reduce(tv[1], pick, AX, ALU.max))
            chain(V.tensor_tensor(oh1, pick, over_e(tv[1]), ALU.is_equal))
            V.tensor_tensor(oh_b, oh0, oh1, ALU.add).then_inc(oh_done, 1)
            other_taps(0, 0, 0, NCT * HALO)
            dve.wait_ge(gap_exp, 1)
            chain(V.tensor_reduce(tv[0], ex, AX, ALU.add))
            chain(V.reciprocal(tv[5], tv[0]))
            dve.wait_ge(top2_exp, 1)
            chain(V.tensor_tensor(tv[6], tv[4], tv[5], ALU.mult))
            V.tensor_tensor(tv[6], tv[6], tv[5], ALU.subtract).then_inc(dp_done, 1)
            dve.wait_ge(rank_ps, 1)
            chain(V.tensor_copy(cnt, bank[5][:, :].rearrange("p (t e) -> p t e", e=E)))
            src, spare = cnt, [lg, gap2]
            step, turn = 1, 0
            while step < NT:
                dst = spare[turn % 2]
                V.tensor_copy(dst[:, 0:step, :], src[:, 0:step, :])
                chain(V.tensor_tensor(dst[:, step:, :], src[:, step:, :], src[:, 0:NT - step, :], ALU.add))
                src, step, turn = dst, 2 * step, turn + 1
            incl = src
            chain(V.tensor_tensor(pos, incl, bank[4][:, :].rearrange("p (t e) -> p t e", e=E), ALU.add))
            chain(V.tensor_tensor(pos, pos, cnt, ALU.subtract))
            chain(V.tensor_scalar(cnt_i, incl[:, NT - 1, :], float(PS - 1), None, ALU.add))
            chain(V.tensor_scalar(cnt_i, cnt_i, PS.bit_length() - 1, None, ALU.arith_shift_right))
            chain(V.tensor_copy(ntl, cnt_i))
            chain(V.memset(base, 0.0))
            for e in range(1, E):
                chain(V.tensor_tensor(base[:, e:e + 1], base[:, e - 1:e], ntl[:, e - 1:e], ALU.add))
            chain(V.tensor_scalar(base_s, base, float(PS), None, ALU.mult))
            chain(V.tensor_tensor(pos, pos, over_t(base_s), ALU.add))
            for c, oh in enumerate((oh0, oh1)):
                chain(V.tensor_tensor(pick, oh, pos, ALU.mult))
                chain(V.tensor_reduce(tv[8], pick, AX, ALU.add))
                chain(V.tensor_copy(slot_i[:, :, c], tv[8]))
            dve.wait_ge(dp_exp, 1)
            chain(V.tensor_scalar(tv[8], tv[7], 1.0, None, ALU.add))
            chain(V.reciprocal(tv[9], tv[8]))
            chain(V.tensor_tensor(meta[:, :, 1, 1], tv[7], tv[9], ALU.mult))
            V.tensor_copy(meta[:, :, 0, 1], tv[9]).then_inc(slots_done, 1)
            dve.wait_ge(e_done, 3)

            def by_token(b, j, fill):
                nn, u = b * SC + j, j % 2
                fb = bank[3 + u]
                dve.wait_ge(front_done, nn + 1)
                V.tensor_tensor(by_head(xdt[:, u, :]), by_head(fb[:, P:P + DI]), per_head(dts, nn),
                                ALU.mult).then_inc(xdt_done, 1)
                V.tensor_copy(b_sb[:, u, :], fb[:, 3 * P:4 * P]).then_inc(b_done, 1)
                fill()
                dve.wait_ge(l_done, nn + 1)
                V.tensor_tensor(m_sb[:, u, :].rearrange("p (h l) -> p h l", h=NH),
                                l_sb[:, u, :].rearrange("p (h l) -> p h l", h=NH),
                                fb[:, 0:P].unsqueeze(1).broadcast_to([P, NH, P]), ALU.mult).then_inc(m_done, 1)

            def outputs(b, j):
                nn, u, later = b * SC + j, j % 2, b * (SC - 1) + j
                dve.wait_ge(mid_done, nn + 1)
                if j:
                    if not (is_first(b) and j == 1):
                        dve.wait_ge(y_done, nn)
                    V.tensor_tensor(by_head(yo_sb[:, :]), by_head(bank[5][:, DI:2 * DI]), per_head(e_cs, nn),
                                    ALU.mult).then_inc(yo_done, 1)
                    dve.wait_ge(keep_done, later)
                    V.tensor_tensor(state[:, :], state_k[:, :], bank[6][:, 0:DI], ALU.add).then_inc(state_done, 1)
                    dve.wait_ge(yo_done, later)
                    V.tensor_tensor(y_sb[:, u, :], yo_sb[:, :], bank[5][:, 0:DI], ALU.add).then_inc(y_done, 1)
                else:
                    V.tensor_copy(state[:, :], bank[6][:, 0:DI]).then_inc(state_done, 1)
                    V.tensor_copy(y_sb[:, u, :], bank[5][:, 0:DI]).then_inc(y_done, 1)

            def pair_experts():
                chain(V.memset(eid_f[0:1, :], 0.0))
                for e in range(1, E):
                    chain(V.scalar_tensor_tensor(out=eid_f[0:1, :], in0=iota_f[0:1, :], scalar=base[0:1, e:e + 1],
                                                 in1=eid_f[0:1, :], op0=ALU.is_ge, op1=ALU.add))
                V.tensor_copy(eid[:, :], eid_f[0:1, :]).then_inc(eid_done, 1)

            def skip(nn, j):
                ab, cs = group_act(j // GC), in_group(j)
                dve.wait_ge(yt_done, nn + 1)
                if not (isinstance(nn, int) and nn < 1):
                    dve.wait_ge(gate_done, nn)
                for c in range(2):
                    sk = V.scalar_tensor_tensor(out=yd_sb[:, c * P:(c + 1) * P], in0=ab[:, XT0 + c, cs],
                                                scalar=ds_c[:, c:c + 1], in1=bank[1][:, c * P:(c + 1) * P],
                                                op0=ALU.mult, op1=ALU.add)
                sk.then_inc(skip_done, 1)

            def gate(nn, j, group):
                ab, cs, u = group_act(j // GC), in_group(j), j % 2
                dve.wait_ge(skip_done, nn + 1)
                if j % GC == 0:
                    dve.wait_ge(gate_silu, group + 1)
                V.tensor_tensor(yg[:, u, :].rearrange("p (c l) -> p c l", c=2),
                                yd_sb[:, :].rearrange("p (c l) -> p c l", c=2), ab[:, ZT0:ZT0 + 2, cs],
                                ALU.mult).then_inc(gate_done, 1)

            FILL = (((0, 0), (0, 0), (0, 1), (1, 4)),
                    ((4, 5), (5, 6), (0, 0), (6, 8)),
                    ((8, 9), (9, 10), (10, 11), (11, 12)),
                    ((0, 0),) * 4)

            by_token(0, 0, lambda: None)

            def sequence(b):
                first, last = is_first(b), is_last(b)
                for j in range(SC):
                    nn, q, g = b * SC + j, j % GC, j // GC

                    def fill(place):
                        if not (last and g == 1):
                            other_taps(b * 2 + g + 1, 1 - g, *FILL[q][place])

                    if j:
                        outputs(b, j - 1)
                    elif not first:
                        outputs(b - 1, SC - 1)
                    if not (first and j < 2):
                        skip(nn - 2, (j - 2) % SC)
                    fill(0)
                    if not (first and j < 2):
                        gate(nn - 2, (j - 2) % SC, b * 2 + (j - 2) // GC)
                    fill(1)
                    if not (last and j == SC - 1):
                        by_token(b, j + 1, lambda: fill(2))
                    fill(3)
                    if first and j == 3:
                        pair_experts()
                    if last and g == 1 and q:
                        weights_low(q - 1)

            def weights_low(i):
                dve.wait_ge(gu_hi_done, i + 1)
                c = slice(i * 1024, (i + 1) * 1024)
                w = V.tensor_tensor(gu_lo[:, c], gu_raw[i], gu_hi[:, c].bitcast(F32), ALU.subtract)
                if i == 3:
                    w.then_inc(gu_lo_done, 1)

            over_sequences(dve, sequence)
            outputs(NB - 1, SC - 1)
            for n_ in (NT - 2, NT - 1):
                skip(n_, n_ % SC)
                gate(n_, n_ % SC, NG - 1)
            weights_low(3)
            dve.wait_ge(o_kept, NT)
            V.tensor_scalar(t_a, ssq, 1.0 / DI, EPS, ALU.mult, ALU.add).then_inc(ms_done, 1)
            dve.wait_ge(rms_sq, 1)
            chain(V.reciprocal(var, t_b))
            V.tensor_scalar(r12, r1, 1.0, None, ALU.add).then_inc(rms_done, 1)
            for r in range(R):
                dve.wait_ge(scat[r], 16 * K * NT // R)

            def x_keep(m, r):
                dve.wait_ge(xt_done, m * R + r + 1)
                V.tensor_copy(x_hi[:, r % 2, :], bank[0][:, 0:PS]).then_inc(xhi_done, 1)
                dve.wait_ge(xhi_done, m * R + r + 1)
                V.tensor_tensor(x_lo[:, r % 2, :], bank[0][:, 0:PS], x_hi[:, r % 2, :].bitcast(F32), ALU.subtract)\
                    .then_inc(xts_done, 1)

            def destination(m, r):
                if not is_first(m):
                    dve.wait_ge(st_moe[r], 16 * 2 * m)
                V.tensor_copy(slot_st[:, r, :], rows[:, r, :, D]).then_inc(id_done, 1)

            def hidden(m, r):
                dve.wait_ge(silu_m, m * R + r + 1)
                for c in range(2):
                    h = V.scalar_tensor_tensor(out=m_sb[:, r % 2, c * F:(c + 1) * F],
                                               in0=l_sb[:, r % 2, c * F:(c + 1) * F],
                                               scalar=rows[:, r, c, D + 1:D + 2],
                                               in1=bank[2 + 2 * (r % 2) + c][:, F:2 * F], op0=ALU.mult, op1=ALU.mult)
                h.then_inc(h_done, 1)

            def residual(m, r):
                dve.wait_ge(resid_done, m * R + r + 1)
                t = tile_ix(m * R + r)
                xt = x_sb[:, t, :].rearrange("p a d -> p (a d)")
                V.scalar_tensor_tensor(out=xt, in0=xt, scalar=var[:, t], in1=x_again[r], op0=ALU.mult, op1=ALU.add)\
                    .then_inc(place_free, 1)

            over_pairs(dve, [(x_keep, 0), (destination, 2), (hidden, 1)], [residual])

            dve.wait_ge(place_free, NT + R)
            for k in range(8):
                xk = x_sb[:, 8 * k:8 * k + 8, :]
                if k == 7:
                    dve.wait_ge(ld_sum[k], 32)
                    chain(V.tensor_tensor(xk, xk, y_ch[k % 4][1], ALU.add))
                else:
                    dve.wait_ge(moe_sum, k + 1)
                V.tensor_tensor(xk, xk, y_ch[k % 4][0], ALU.add).then_inc(total_done, 1)


def kernel(**inputs):
    import numpy as np
    import concourse.bacc as bacc
    from concourse.bass_utils import run_bass_kernel_spmd

    a = {k.removeprefix("L0_"): np.asarray(v) for k, v in inputs.items()}
    xi = a["attn_x"]
    w_in = a["attn_W_in"]
    arrays = {
        "x": xi.reshape(NT, P, D).transpose(1, 0, 2),
        "ln_w": a["attn_ln_w"].reshape(D, 1),
        "ln_b": a["attn_ln_b"].reshape(D, 1),
        "w_in_t": w_in[:DI + CONV].T,
        "w_dt": w_in[DI + CONV:].T,
        "conv_w": a["attn_conv_w"].reshape(NCT, P, TAPS).transpose(1, 0, 2),
        "conv_b": a["attn_conv_b"].reshape(NCT, P).T,
        "dt_bias": a["attn_dt_bias"].reshape(1, NH),
        "a_log": a["attn_A_log"].reshape(1, NH),
        "d_skip": np.repeat(a["attn_D"], HD).reshape(2, P).T,
        "rms_w": a["attn_rms_w"].reshape(2, P).T,
        "w_out_t": a["attn_W_out"].T.reshape(2, P, D).transpose(1, 0, 2),
        "router": a["ffn_kernel_router_DE"],
        "gate_w": a["ffn_kernel_gating_EDF"],
        "up_w": a["ffn_kernel_up_EDF"],
        "down_w": a["ffn_kernel_down_EFD"],
    }
    nc = bacc.Bacc("TRN2", target_bir_lowering=False, num_devices=1)
    feeds, args = {}, []
    for name, v in arrays.items():
        v = np.ascontiguousarray(v)
        feeds[f"in_{name}"] = v
        args.append(nc.dram_tensor(f"in_{name}", v.shape, mybir.dt.from_np(v.dtype), kind="ExternalInput").ap())
    args.append(nc.dram_tensor("out_0", (P, NT, D), F32, kind="ExternalOutput").ap())
    program(nc, *args)
    r = run_bass_kernel_spmd(nc, [feeds], core_ids=[0])
    got = r.results[0]["out_0"]
    return np.ascontiguousarray(got.transpose(1, 0, 2)).reshape(NB, SEQ, D)
```
